# Optimizing a Trainium2 kernel written in Bass

```python
import numpy as np
import jax
import jax.numpy as jnp

def _softmax(x, axis=-1):
    return jax.nn.softmax(x, axis=axis)

def _gelu(x):
    return jax.nn.gelu(x, approximate=True)

def _silu(x):
    return jax.nn.silu(x)

def _sigmoid(x):
    return jax.nn.sigmoid(x)

def _layernorm(x, axis=-1, eps=1e-05):
    m = jnp.mean(x, axis=axis, keepdims=True)
    v = jnp.var(x, axis=axis, keepdims=True)
    return (x - m) / jnp.sqrt(v + eps)

def _scatter_add(tgt, idx, src, axis=0):
    return tgt.at[idx].add(src)

def _segment_sum(src, seg, n):
    return jax.ops.segment_sum(src, seg, n)
kernel_name = 'mk_decoder_preln_d2_seqx_r8_95ce6c'

def setup_inputs(seed: int=0):
    np.random.seed(seed)
    _w = jnp.asarray

    def _rec_inputs():
        import jax
        import jax.numpy as jnp
        _rk = jax.random.key(seed)
        x = -0.0002928 + 1 * jax.random.normal(jax.random.fold_in(_rk, 1), (64, 128, 128), jnp.float32)
        _lenS = 128 - jax.random.randint(jax.random.fold_in(_rk, 7), (64,), 0, max(1, 128 // 4) + 1, jnp.int32)
        _lenS2 = 77 - jax.random.randint(jax.random.fold_in(_rk, 8), (64,), 0, max(1, 77 // 4) + 1, jnp.int32)
        _ctx_512P = jax.random.normal(jax.random.fold_in(_rk, 11), (64, 16, 64), jnp.float32)
        _ctx_512c = jax.random.dirichlet(jax.random.fold_in(_rk, 511), 0.3 * jnp.ones((16,), jnp.float32), (64, 77))
        _ctx_512t = jnp.einsum('bsk,bkd->bsd', _ctx_512c, _ctx_512P)
        _ctx_512t = _ctx_512t * jax.lax.rsqrt(jnp.mean(jnp.square(_ctx_512t)) + 1e-12) * 0.953939
        ctx_512 = -1.52775e-05 + 0.999936 * (_ctx_512t + 0.3 * jax.random.normal(jax.random.fold_in(_rk, 611), (64, 77, 64), jnp.float32))
        return (x, ctx_512)
    x, ctx_512 = _rec_inputs()

    def _L0_attn_setup():
        import jax, jax.numpy as jnp
        import numpy as np
        EMBED = 128
        HEADS = 16
        HD = EMBED // HEADS
        M = 32
        R = 2
        EPS = 1e-06
        C_CONST = 2.0 + EPS
        CHUNK = 64

        def _features(x, omega, quad_nodes, quad_weights):
            B, H, T, D = x.shape
            xn = x / jnp.maximum(jnp.linalg.norm(x, axis=-1, keepdims=True), 1e-12)
            proj = jnp.einsum('bhtd,rhdm->rbhtm', xn, omega)
            s = quad_nodes[:, None, None, None, None]
            sqrt_2s = jnp.sqrt(2.0 * jnp.maximum(s, 0.0))
            arg = jnp.clip(proj * sqrt_2s - s, -20.0, 20.0)
            feat = jnp.exp(arg) / np.sqrt(M).astype(np.float32)
            feat = feat * jnp.sqrt(jnp.maximum(quad_weights, 0.0))[:, None, None, None, None]
            return jnp.transpose(feat, (1, 2, 3, 0, 4)).reshape(B, H, T, R * M)
        key = jax.random.key(seed)
        ks = jax.random.split(key, 4)
        B, T = (2, 256)
        x = jax.random.normal(ks[0], (B, T, EMBED), jnp.float32)
        Wqkv = jax.random.normal(ks[1], (EMBED, 3 * EMBED), jnp.float32) * 0.02
        bqkv = jnp.zeros((3 * EMBED,), jnp.float32)
        Wout = jax.random.normal(ks[2], (EMBED, EMBED), jnp.float32) * 0.02
        bout = jnp.zeros((EMBED,), jnp.float32)
        omega = jax.random.normal(ks[3], (R, HEADS, HD, M), jnp.float32)
        nodes, weights = np.polynomial.laguerre.laggauss(R)
        quad_nodes = jnp.asarray(nodes / C_CONST, jnp.float32)
        quad_weights = jnp.asarray(weights * (C_CONST / 4.0), jnp.float32)
        return {'x': x, 'Wqkv': Wqkv, 'bqkv': bqkv, 'Wout': Wout, 'bout': bout, 'omega': omega, 'quad_nodes': quad_nodes, 'quad_weights': quad_weights}
    _L0_attn_all = _L0_attn_setup()
    _L0_attn_in = {k: v for k, v in _L0_attn_all.items() if k in ('Wqkv', 'bqkv', 'Wout', 'bout', 'omega', 'quad_nodes', 'quad_weights')}
    del _L0_attn_all

    def _L0_xattn_setup():
        import jax, jax.numpy as jnp
        import numpy as np
        NUM_HEADS = 16
        HEAD_DIM = 64
        Q_DIM = 128
        KV_DIM = 64
        INNER = NUM_HEADS * HEAD_DIM
        key = jax.random.key(seed)
        ks = jax.random.split(key, 7)
        B, N, M = (32, 128, 256)
        q = jax.random.normal(ks[0], (B, N, Q_DIM), dtype=jnp.float32)
        kv = jax.random.normal(ks[1], (B, M, KV_DIM), dtype=jnp.float32)
        Wq = jax.random.normal(ks[2], (Q_DIM, INNER), dtype=jnp.float32) / np.sqrt(Q_DIM)
        Wk = jax.random.normal(ks[3], (KV_DIM, INNER), dtype=jnp.float32) / np.sqrt(KV_DIM)
        Wv = jax.random.normal(ks[4], (KV_DIM, INNER), dtype=jnp.float32) / np.sqrt(KV_DIM)
        Wo = jax.random.normal(ks[5], (INNER, Q_DIM), dtype=jnp.float32) / np.sqrt(INNER)
        bo = jax.random.normal(ks[6], (Q_DIM,), dtype=jnp.float32) * 0.01
        return {'q': q, 'kv': kv, 'Wq': Wq, 'Wk': Wk, 'Wv': Wv, 'Wo': Wo, 'bo': bo}
    _L0_xattn_all = _L0_xattn_setup()
    _L0_xattn_in = {k: v for k, v in _L0_xattn_all.items() if k in ('Wq', 'Wk', 'Wv', 'Wo', 'bo')}
    del _L0_xattn_all

    def _L0_ffn_setup():
        import jax, jax.numpy as jnp
        import numpy as np
        DIM = 128
        DEPTH = 2
        HEADS = 8
        DIM_HEAD = 64
        WINDOW = 64
        INNER = HEADS * DIM_HEAD
        HID = int(DIM * 4 * 2 / 3)
        B, N = (2, 1024)
        QK_SCALE = 8.0

        def shift_token(t):
            t1, t2 = jnp.split(t, 2, axis=-1)
            t2 = jnp.pad(t2, ((0, 0), (1, 0), (0, 0)))[:, :-1]
            return jnp.concatenate([t1, t2], axis=-1)

        def l2norm(t):
            return t / jnp.clip(jnp.linalg.norm(t, axis=-1, keepdims=True), 1e-12)

        def rotate_half(x):
            x1, x2 = jnp.split(x, 2, axis=-1)
            return jnp.concatenate([-x2, x1], axis=-1)

        def rotary_xpos(q, k):
            n = q.shape[-2]
            half_idx = jnp.arange(0, DIM_HEAD, 2, dtype=jnp.float32)
            inv_freq = 1.0 / 10000.0 ** (half_idx / DIM_HEAD)
            t = jnp.arange(n, dtype=jnp.float32)
            freqs = t[:, None] * inv_freq[None, :]
            freqs = jnp.concatenate([freqs, freqs], axis=-1)
            base = (half_idx + 0.4 * DIM_HEAD) / (1.4 * DIM_HEAD)
            power = (t - n // 2) / float(WINDOW // 2)
            scale = base[None, :] ** power[:, None]
            scale = jnp.concatenate([scale, scale], axis=-1)
            cos, sin = (jnp.cos(freqs), jnp.sin(freqs))
            q = q * cos * scale + rotate_half(q) * sin * scale
            k = k * cos / scale + rotate_half(k) * sin / scale
            return (q, k)

        def local_attention(q, k, v):
            b, h, n, d = q.shape
            w = n // WINDOW
            bq = q.reshape(b, h, w, WINDOW, d) * QK_SCALE
            bk = k.reshape(b, h, w, WINDOW, d)
            bv = v.reshape(b, h, w, WINDOW, d)

            def look_around(t):
                p = jnp.pad(t, ((0, 0), (0, 0), (1, 0), (0, 0), (0, 0)))
                return jnp.concatenate([p[:, :, :w], p[:, :, 1:]], axis=3)
            bk, bv = (look_around(bk), look_around(bv))
            bt = jnp.arange(n).reshape(w, WINDOW)
            btp = jnp.pad(bt, ((1, 0), (0, 0)), constant_values=-1)
            btk = jnp.concatenate([btp[:w], btp[1:]], axis=1)
            sim = jnp.einsum('bhwid,bhwjd->bhwij', bq, bk)
            i = bt[:, :, None]
            j = btk[:, None, :]
            mask = (i < j) | (i > j + WINDOW) | (j == -1)
            sim = jnp.where(mask, -jnp.finfo(sim.dtype).max, sim)
            attn = jax.nn.softmax(sim, axis=-1)
            out = jnp.einsum('bhwij,bhwjd->bhwid', attn, bv)
            return out.reshape(b, h, n, d)

        def _layer(x, wqkv, qs, ksc, wo, lg, lb, w1, b1, w2, b2):
            b, n, _ = x.shape
            h = shift_token(x)
            qkv = h @ wqkv
            q, k, v = jnp.split(qkv, 3, axis=-1)
            to_heads = lambda t: t.reshape(b, n, HEADS, DIM_HEAD).transpose(0, 2, 1, 3)
            q, k, v = (to_heads(q), to_heads(k), to_heads(v))
            q = l2norm(q) * qs
            k = l2norm(k) * ksc
            q, k = rotary_xpos(q, k)
            o = local_attention(q, k, v)
            o = o.transpose(0, 2, 1, 3).reshape(b, n, INNER)
            x = x + o @ wo
            h = shift_token(x)
            mu = h.mean(-1, keepdims=True)
            var = h.var(-1, keepdims=True)
            h = (h - mu) / jnp.sqrt(var + 1e-05) * lg + lb
            h = h @ w1 + b1
            a, g = jnp.split(h, 2, axis=-1)
            h = a * jax.nn.gelu(g, approximate=False)
            x = x + h @ w2 + b2
            return x
        key = jax.random.key(seed)
        ks = jax.random.split(key, 6)
        return {'x': jax.random.normal(ks[0], (B, N, DIM), jnp.float32), 'wqkv': jax.random.normal(ks[1], (DEPTH, DIM, 3 * INNER), jnp.float32) * 0.02, 'q_scale': jnp.ones((DEPTH, DIM_HEAD), jnp.float32), 'k_scale': jnp.ones((DEPTH, DIM_HEAD), jnp.float32), 'wo': jax.random.normal(ks[2], (DEPTH, INNER, DIM), jnp.float32) * 0.02, 'ln_g': jnp.ones((DEPTH, DIM), jnp.float32), 'ln_b': jnp.zeros((DEPTH, DIM), jnp.float32), 'w1': jax.random.normal(ks[3], (DEPTH, DIM, 2 * HID), jnp.float32) * 0.02, 'b1': jnp.zeros((DEPTH, 2 * HID), jnp.float32), 'w2': jax.random.normal(ks[4], (DEPTH, HID, DIM), jnp.float32) * 0.02, 'b2': jnp.zeros((DEPTH, DIM), jnp.float32)}
    _L0_ffn_all = _L0_ffn_setup()
    _L0_ffn_in = {k: v for k, v in _L0_ffn_all.items() if k in ('wqkv', 'q_scale', 'k_scale', 'wo', 'ln_g', 'ln_b', 'w1', 'b1', 'w2', 'b2')}
    del _L0_ffn_all

    def _L1_attn_setup():
        import jax, jax.numpy as jnp
        import numpy as np
        D_MODEL = 128
        D_STATE = 128
        D_CONV = 4
        EXPAND = 2
        HEADDIM = 64
        D_INNER = EXPAND * D_MODEL
        NHEADS = D_INNER // HEADDIM
        CONV_DIM = D_INNER + 2 * D_STATE
        D_IN_PROJ = 2 * D_INNER + 2 * D_STATE + NHEADS
        B = 2
        L = 256
        EPS = 1e-05

        def _rmsnorm(x, w):
            return x * jax.lax.rsqrt(jnp.mean(x * x, axis=-1, keepdims=True) + EPS) * w

        def _mamba2(x, W_in, conv_w, conv_b, dt_bias, A_log, Dskip, norm_w, W_out):
            Bb, Ll, _ = x.shape
            zxbcdt = x @ W_in.T
            z = zxbcdt[..., :D_INNER]
            xBC = zxbcdt[..., D_INNER:D_INNER + CONV_DIM]
            dt = jax.nn.softplus(zxbcdt[..., D_INNER + CONV_DIM:] + dt_bias)
            xBC = jnp.transpose(xBC, (0, 2, 1))
            xBC = jax.lax.conv_general_dilated(xBC, conv_w[:, None, :], (1,), [(D_CONV - 1, 0)], feature_group_count=CONV_DIM)
            xBC = jax.nn.silu(jnp.transpose(xBC + conv_b[None, :, None], (0, 2, 1)))
            xs = xBC[..., :D_INNER].reshape(Bb, Ll, NHEADS, HEADDIM)
            Bm = xBC[..., D_INNER:D_INNER + D_STATE]
            Cm = xBC[..., D_INNER + D_STATE:]
            A = -jnp.exp(A_log)
            dA = jnp.exp(dt * A)

            def step(state, inp):
                dA_t, dt_t, B_t, C_t, x_t = inp
                dBx = jnp.einsum('bh,bn,bhp->bhpn', dt_t, B_t, x_t)
                state = state * dA_t[:, :, None, None] + dBx
                return (state, jnp.einsum('bhpn,bn->bhp', state, C_t))
            state0 = jnp.zeros((Bb, NHEADS, HEADDIM, D_STATE), x.dtype)
            _, y = jax.lax.scan(step, state0, (jnp.moveaxis(dA, 1, 0), jnp.moveaxis(dt, 1, 0), jnp.moveaxis(Bm, 1, 0), jnp.moveaxis(Cm, 1, 0), jnp.moveaxis(xs, 1, 0)))
            y = jnp.moveaxis(y, 0, 1) + Dskip[None, None, :, None] * xs
            y = y.reshape(Bb, Ll, D_INNER)
            y = _rmsnorm(y * jax.nn.silu(z), norm_w)
            return y @ W_out.T
        key = jax.random.key(seed)
        ks = jax.random.split(key, 4)

        def nrm(k, shape, s=0.02):
            return jax.random.normal(k, shape, jnp.float32) * s

        def mamba_params(kk):
            k = jax.random.split(kk, 5)
            return dict(W_in=nrm(k[0], (D_IN_PROJ, D_MODEL)), conv_w=nrm(k[1], (CONV_DIM, D_CONV), 0.2), conv_b=jnp.zeros((CONV_DIM,), jnp.float32), dt_bias=jax.random.uniform(k[2], (NHEADS,), jnp.float32, -4.0, -2.0), A_log=jnp.log(jax.random.uniform(k[3], (NHEADS,), jnp.float32, 1.0, 16.0)), D=jnp.ones((NHEADS,), jnp.float32), norm_w=jnp.ones((D_INNER,), jnp.float32), W_out=nrm(k[4], (D_MODEL, D_INNER)))
        pf = mamba_params(ks[1])
        pb = mamba_params(ks[2])
        out = {'x': jax.random.normal(ks[0], (B, L, D_MODEL), jnp.float32), 'norm_weight': jnp.ones((D_MODEL,), jnp.float32)}
        out.update({f'fwd_{k}': v for k, v in pf.items()})
        out.update({f'bwd_{k}': v for k, v in pb.items()})
        out['proj_W'] = nrm(ks[3], (D_MODEL, 2 * D_MODEL))
        out['proj_b'] = jnp.zeros((D_MODEL,), jnp.float32)
        return out
    _L1_attn_all = _L1_attn_setup()
    _L1_attn_in = {k: v for k, v in _L1_attn_all.items() if k in ('norm_weight', 'fwd_W_in', 'fwd_conv_w', 'fwd_conv_b', 'fwd_dt_bias', 'fwd_A_log', 'fwd_D', 'fwd_norm_w', 'fwd_W_out', 'bwd_W_in', 'bwd_conv_w', 'bwd_conv_b', 'bwd_dt_bias', 'bwd_A_log', 'bwd_D', 'bwd_norm_w', 'bwd_W_out', 'proj_W', 'proj_b')}
    del _L1_attn_all

    def _L1_xattn_setup():
        import jax, jax.numpy as jnp
        import numpy as np
        HEADS = 16
        D_MODEL = 128
        IMG_MODEL = 64
        D_K = D_MODEL // HEADS
        key = jax.random.key(seed)
        ks = jax.random.split(key, 12)
        B, LQ, LKV = (8, 256, 128)
        s_dm = 1.0 / np.sqrt(D_MODEL)
        s_im = 1.0 / np.sqrt(IMG_MODEL)
        return {'q': jax.random.normal(ks[0], (B, LQ, D_MODEL), jnp.float32), 'k': jax.random.normal(ks[1], (B, LKV, IMG_MODEL), jnp.float32), 'v': jax.random.normal(ks[2], (B, LKV, IMG_MODEL), jnp.float32), 'Wq': jax.random.normal(ks[3], (D_MODEL, D_MODEL), jnp.float32) * s_dm, 'bq': jnp.zeros((D_MODEL,), jnp.float32), 'Wk': jax.random.normal(ks[4], (IMG_MODEL, D_MODEL), jnp.float32) * s_im, 'bk': jnp.zeros((D_MODEL,), jnp.float32), 'Wv': jax.random.normal(ks[5], (IMG_MODEL, D_MODEL), jnp.float32) * s_im, 'bv': jnp.zeros((D_MODEL,), jnp.float32), 'Wo': jax.random.normal(ks[6], (D_MODEL, D_MODEL), jnp.float32) * s_dm, 'bo': jnp.zeros((D_MODEL,), jnp.float32)}
    _L1_xattn_all = _L1_xattn_setup()
    _L1_xattn_in = {k: v for k, v in _L1_xattn_all.items() if k in ('Wq', 'bq', 'Wk', 'bk', 'Wv', 'bv', 'Wo', 'bo')}
    del _L1_xattn_all

    def _L1_ffn_setup():
        import jax, jax.numpy as jnp
        import numpy as np
        K = 2
        key = jax.random.key(seed)
        ks = jax.random.split(key, 5)
        B, S, D, E, H = (8, 512, 128, 16, 64)
        x = jax.random.normal(ks[0], (B, S, D), dtype=jnp.float32)
        W1 = jax.random.normal(ks[1], (E, D, H), dtype=jnp.float32) * (1.0 / np.sqrt(D))
        b1 = jnp.zeros((E, H), dtype=jnp.float32)
        W2 = jax.random.normal(ks[2], (E, H, D), dtype=jnp.float32) * (1.0 / np.sqrt(H))
        b2 = jnp.zeros((E, D), dtype=jnp.float32)
        Wr = jax.random.normal(ks[3], (D, E), dtype=jnp.float32) * (1.0 / np.sqrt(D))
        br = jnp.zeros((E,), dtype=jnp.float32)
        return {'x': x, 'W1': W1, 'b1': b1, 'W2': W2, 'b2': b2, 'Wr': Wr, 'br': br}
    _L1_ffn_all = _L1_ffn_setup()
    _L1_ffn_in = {k: v for k, v in _L1_ffn_all.items() if k in ('W1', 'b1', 'W2', 'b2', 'Wr', 'br')}
    del _L1_ffn_all
    return {'x': x, 'ctx_512': ctx_512, 'L0_attn_Wqkv': _L0_attn_in['Wqkv'], 'L0_attn_bqkv': _L0_attn_in['bqkv'], 'L0_attn_Wout': _L0_attn_in['Wout'], 'L0_attn_bout': _L0_attn_in['bout'], 'L0_attn_omega': _L0_attn_in['omega'], 'L0_attn_quad_nodes': _L0_attn_in['quad_nodes'], 'L0_attn_quad_weights': _L0_attn_in['quad_weights'], 'L0_xattn_Wq': _L0_xattn_in['Wq'], 'L0_xattn_Wk': _L0_xattn_in['Wk'], 'L0_xattn_Wv': _L0_xattn_in['Wv'], 'L0_xattn_Wo': _L0_xattn_in['Wo'], 'L0_xattn_bo': _L0_xattn_in['bo'], 'L0_ffn_wqkv': _L0_ffn_in['wqkv'], 'L0_ffn_q_scale': _L0_ffn_in['q_scale'], 'L0_ffn_k_scale': _L0_ffn_in['k_scale'], 'L0_ffn_wo': _L0_ffn_in['wo'], 'L0_ffn_ln_g': _L0_ffn_in['ln_g'], 'L0_ffn_ln_b': _L0_ffn_in['ln_b'], 'L0_ffn_w1': _L0_ffn_in['w1'], 'L0_ffn_b1': _L0_ffn_in['b1'], 'L0_ffn_w2': _L0_ffn_in['w2'], 'L0_ffn_b2': _L0_ffn_in['b2'], 'L1_attn_norm_weight': _L1_attn_in['norm_weight'], 'L1_attn_fwd_W_in': _L1_attn_in['fwd_W_in'], 'L1_attn_fwd_conv_w': _L1_attn_in['fwd_conv_w'], 'L1_attn_fwd_conv_b': _L1_attn_in['fwd_conv_b'], 'L1_attn_fwd_dt_bias': _L1_attn_in['fwd_dt_bias'], 'L1_attn_fwd_A_log': _L1_attn_in['fwd_A_log'], 'L1_attn_fwd_D': _L1_attn_in['fwd_D'], 'L1_attn_fwd_norm_w': _L1_attn_in['fwd_norm_w'], 'L1_attn_fwd_W_out': _L1_attn_in['fwd_W_out'], 'L1_attn_bwd_W_in': _L1_attn_in['bwd_W_in'], 'L1_attn_bwd_conv_w': _L1_attn_in['bwd_conv_w'], 'L1_attn_bwd_conv_b': _L1_attn_in['bwd_conv_b'], 'L1_attn_bwd_dt_bias': _L1_attn_in['bwd_dt_bias'], 'L1_attn_bwd_A_log': _L1_attn_in['bwd_A_log'], 'L1_attn_bwd_D': _L1_attn_in['bwd_D'], 'L1_attn_bwd_norm_w': _L1_attn_in['bwd_norm_w'], 'L1_attn_bwd_W_out': _L1_attn_in['bwd_W_out'], 'L1_attn_proj_W': _L1_attn_in['proj_W'], 'L1_attn_proj_b': _L1_attn_in['proj_b'], 'L1_xattn_Wq': _L1_xattn_in['Wq'], 'L1_xattn_bq': _L1_xattn_in['bq'], 'L1_xattn_Wk': _L1_xattn_in['Wk'], 'L1_xattn_bk': _L1_xattn_in['bk'], 'L1_xattn_Wv': _L1_xattn_in['Wv'], 'L1_xattn_bv': _L1_xattn_in['bv'], 'L1_xattn_Wo': _L1_xattn_in['Wo'], 'L1_xattn_bo': _L1_xattn_in['bo'], 'L1_ffn_W1': _L1_ffn_in['W1'], 'L1_ffn_b1': _L1_ffn_in['b1'], 'L1_ffn_W2': _L1_ffn_in['W2'], 'L1_ffn_b2': _L1_ffn_in['b2'], 'L1_ffn_Wr': _L1_ffn_in['Wr'], 'L1_ffn_br': _L1_ffn_in['br']}

def reference(x, ctx_512, L0_attn_Wqkv, L0_attn_bqkv, L0_attn_Wout, L0_attn_bout, L0_attn_omega, L0_attn_quad_nodes, L0_attn_quad_weights, L0_xattn_Wq, L0_xattn_Wk, L0_xattn_Wv, L0_xattn_Wo, L0_xattn_bo, L0_ffn_wqkv, L0_ffn_q_scale, L0_ffn_k_scale, L0_ffn_wo, L0_ffn_ln_g, L0_ffn_ln_b, L0_ffn_w1, L0_ffn_b1, L0_ffn_w2, L0_ffn_b2, L1_attn_norm_weight, L1_attn_fwd_W_in, L1_attn_fwd_conv_w, L1_attn_fwd_conv_b, L1_attn_fwd_dt_bias, L1_attn_fwd_A_log, L1_attn_fwd_D, L1_attn_fwd_norm_w, L1_attn_fwd_W_out, L1_attn_bwd_W_in, L1_attn_bwd_conv_w, L1_attn_bwd_conv_b, L1_attn_bwd_dt_bias, L1_attn_bwd_A_log, L1_attn_bwd_D, L1_attn_bwd_norm_w, L1_attn_bwd_W_out, L1_attn_proj_W, L1_attn_proj_b, L1_xattn_Wq, L1_xattn_bq, L1_xattn_Wk, L1_xattn_bk, L1_xattn_Wv, L1_xattn_bv, L1_xattn_Wo, L1_xattn_bo, L1_ffn_W1, L1_ffn_b1, L1_ffn_W2, L1_ffn_b2, L1_ffn_Wr, L1_ffn_br):
    import jax
    import jax.numpy as jnp

    def _L0_attn_ref(x, Wqkv, bqkv, Wout, bout, omega, quad_nodes, quad_weights):
        import jax, jax.numpy as jnp
        import numpy as np
        EMBED = 128
        HEADS = 16
        HD = EMBED // HEADS
        M = 32
        R = 2
        EPS = 1e-06
        C_CONST = 2.0 + EPS
        CHUNK = 64

        def _features(x, omega, quad_nodes, quad_weights):
            B, H, T, D = x.shape
            xn = x / jnp.maximum(jnp.linalg.norm(x, axis=-1, keepdims=True), 1e-12)
            proj = jnp.einsum('bhtd,rhdm->rbhtm', xn, omega)
            s = quad_nodes[:, None, None, None, None]
            sqrt_2s = jnp.sqrt(2.0 * jnp.maximum(s, 0.0))
            arg = jnp.clip(proj * sqrt_2s - s, -20.0, 20.0)
            feat = jnp.exp(arg) / np.sqrt(M).astype(np.float32)
            feat = feat * jnp.sqrt(jnp.maximum(quad_weights, 0.0))[:, None, None, None, None]
            return jnp.transpose(feat, (1, 2, 3, 0, 4)).reshape(B, H, T, R * M)
        B, T, C = x.shape
        qkv = x @ Wqkv + bqkv
        q, k, v = jnp.split(qkv, 3, axis=-1)
        resh = lambda t: t.reshape(B, T, HEADS, HD).transpose(0, 2, 1, 3)
        q, k, v = (resh(q), resh(k), resh(v))
        qf = _features(q, omega, quad_nodes, quad_weights)
        kf = _features(k, omega, quad_nodes, quad_weights)
        Fd = R * M
        nc = T // CHUNK
        to_chunks = lambda t, last: t.reshape(B, HEADS, nc, CHUNK, last).transpose(2, 0, 1, 3, 4)
        qc = to_chunks(qf, Fd)
        kc = to_chunks(kf, Fd)
        vc = to_chunks(v, HD)

        def step(carry, inp):
            kv_state, k_state = carry
            q_ch, k_ch, v_ch = inp
            kv_prod = jnp.einsum('bhtf,bhtd->bhtfd', k_ch, v_ch)
            kv_cur = jnp.cumsum(kv_prod, axis=2) + kv_state[:, :, None]
            k_cur = jnp.cumsum(k_ch, axis=2) + k_state[:, :, None]
            ctx = jnp.einsum('bhtf,bhtfd->bhtd', q_ch, kv_cur)
            den = jnp.maximum(jnp.einsum('bhtf,bhtf->bht', q_ch, k_cur), 1e-06)
            out_ch = ctx / den[..., None]
            return ((kv_cur[:, :, -1], k_cur[:, :, -1]), out_ch)
        init = (jnp.zeros((B, HEADS, Fd, HD), jnp.float32), jnp.zeros((B, HEADS, Fd), jnp.float32))
        _, outs = jax.lax.scan(step, init, (qc, kc, vc))
        out = outs.transpose(1, 2, 0, 3, 4).reshape(B, HEADS, T, HD)
        out = out.transpose(0, 2, 1, 3).reshape(B, T, C)
        return out @ Wout + bout

    def _L0_xattn_ref(q, kv, Wq, Wk, Wv, Wo, bo):
        import jax, jax.numpy as jnp
        import numpy as np
        NUM_HEADS = 16
        HEAD_DIM = 64
        Q_DIM = 128
        KV_DIM = 64
        INNER = NUM_HEADS * HEAD_DIM
        B, N, _ = q.shape
        M = kv.shape[1]
        scale = HEAD_DIM ** (-0.5)
        qh = (q @ Wq).reshape(B, N, NUM_HEADS, HEAD_DIM).transpose(0, 2, 1, 3)
        kh = (kv @ Wk).reshape(B, M, NUM_HEADS, HEAD_DIM).transpose(0, 2, 1, 3)
        vh = (kv @ Wv).reshape(B, M, NUM_HEADS, HEAD_DIM).transpose(0, 2, 1, 3)
        scores = jnp.einsum('bhnd,bhmd->bhnm', qh, kh) * scale
        attn = jax.nn.softmax(scores, axis=-1)
        out = jnp.einsum('bhnm,bhmd->bhnd', attn, vh)
        out = out.transpose(0, 2, 1, 3).reshape(B, N, INNER)
        return out @ Wo + bo

    def _L0_ffn_ref(x, wqkv, q_scale, k_scale, wo, ln_g, ln_b, w1, b1, w2, b2):
        import jax, jax.numpy as jnp
        import numpy as np
        DIM = 128
        DEPTH = 2
        HEADS = 8
        DIM_HEAD = 64
        WINDOW = 64
        INNER = HEADS * DIM_HEAD
        HID = int(DIM * 4 * 2 / 3)
        B, N = (2, 1024)
        QK_SCALE = 8.0

        def shift_token(t):
            t1, t2 = jnp.split(t, 2, axis=-1)
            t2 = jnp.pad(t2, ((0, 0), (1, 0), (0, 0)))[:, :-1]
            return jnp.concatenate([t1, t2], axis=-1)

        def l2norm(t):
            return t / jnp.clip(jnp.linalg.norm(t, axis=-1, keepdims=True), 1e-12)

        def rotate_half(x):
            x1, x2 = jnp.split(x, 2, axis=-1)
            return jnp.concatenate([-x2, x1], axis=-1)

        def rotary_xpos(q, k):
            n = q.shape[-2]
            half_idx = jnp.arange(0, DIM_HEAD, 2, dtype=jnp.float32)
            inv_freq = 1.0 / 10000.0 ** (half_idx / DIM_HEAD)
            t = jnp.arange(n, dtype=jnp.float32)
            freqs = t[:, None] * inv_freq[None, :]
            freqs = jnp.concatenate([freqs, freqs], axis=-1)
            base = (half_idx + 0.4 * DIM_HEAD) / (1.4 * DIM_HEAD)
            power = (t - n // 2) / float(WINDOW // 2)
            scale = base[None, :] ** power[:, None]
            scale = jnp.concatenate([scale, scale], axis=-1)
            cos, sin = (jnp.cos(freqs), jnp.sin(freqs))
            q = q * cos * scale + rotate_half(q) * sin * scale
            k = k * cos / scale + rotate_half(k) * sin / scale
            return (q, k)

        def local_attention(q, k, v):
            b, h, n, d = q.shape
            w = n // WINDOW
            bq = q.reshape(b, h, w, WINDOW, d) * QK_SCALE
            bk = k.reshape(b, h, w, WINDOW, d)
            bv = v.reshape(b, h, w, WINDOW, d)

            def look_around(t):
                p = jnp.pad(t, ((0, 0), (0, 0), (1, 0), (0, 0), (0, 0)))
                return jnp.concatenate([p[:, :, :w], p[:, :, 1:]], axis=3)
            bk, bv = (look_around(bk), look_around(bv))
            bt = jnp.arange(n).reshape(w, WINDOW)
            btp = jnp.pad(bt, ((1, 0), (0, 0)), constant_values=-1)
            btk = jnp.concatenate([btp[:w], btp[1:]], axis=1)
            sim = jnp.einsum('bhwid,bhwjd->bhwij', bq, bk)
            i = bt[:, :, None]
            j = btk[:, None, :]
            mask = (i < j) | (i > j + WINDOW) | (j == -1)
            sim = jnp.where(mask, -jnp.finfo(sim.dtype).max, sim)
            attn = jax.nn.softmax(sim, axis=-1)
            out = jnp.einsum('bhwij,bhwjd->bhwid', attn, bv)
            return out.reshape(b, h, n, d)

        def _layer(x, wqkv, qs, ksc, wo, lg, lb, w1, b1, w2, b2):
            b, n, _ = x.shape
            h = shift_token(x)
            qkv = h @ wqkv
            q, k, v = jnp.split(qkv, 3, axis=-1)
            to_heads = lambda t: t.reshape(b, n, HEADS, DIM_HEAD).transpose(0, 2, 1, 3)
            q, k, v = (to_heads(q), to_heads(k), to_heads(v))
            q = l2norm(q) * qs
            k = l2norm(k) * ksc
            q, k = rotary_xpos(q, k)
            o = local_attention(q, k, v)
            o = o.transpose(0, 2, 1, 3).reshape(b, n, INNER)
            x = x + o @ wo
            h = shift_token(x)
            mu = h.mean(-1, keepdims=True)
            var = h.var(-1, keepdims=True)
            h = (h - mu) / jnp.sqrt(var + 1e-05) * lg + lb
            h = h @ w1 + b1
            a, g = jnp.split(h, 2, axis=-1)
            h = a * jax.nn.gelu(g, approximate=False)
            x = x + h @ w2 + b2
            return x
        for l in range(DEPTH):
            x = _layer(x, wqkv[l], q_scale[l], k_scale[l], wo[l], ln_g[l], ln_b[l], w1[l], b1[l], w2[l], b2[l])
        return x

    def _L1_attn_ref(x, norm_weight, fwd_W_in, fwd_conv_w, fwd_conv_b, fwd_dt_bias, fwd_A_log, fwd_D, fwd_norm_w, fwd_W_out, bwd_W_in, bwd_conv_w, bwd_conv_b, bwd_dt_bias, bwd_A_log, bwd_D, bwd_norm_w, bwd_W_out, proj_W, proj_b):
        import jax, jax.numpy as jnp
        import numpy as np
        D_MODEL = 128
        D_STATE = 128
        D_CONV = 4
        EXPAND = 2
        HEADDIM = 64
        D_INNER = EXPAND * D_MODEL
        NHEADS = D_INNER // HEADDIM
        CONV_DIM = D_INNER + 2 * D_STATE
        D_IN_PROJ = 2 * D_INNER + 2 * D_STATE + NHEADS
        B = 2
        L = 256
        EPS = 1e-05

        def _rmsnorm(x, w):
            return x * jax.lax.rsqrt(jnp.mean(x * x, axis=-1, keepdims=True) + EPS) * w

        def _mamba2(x, W_in, conv_w, conv_b, dt_bias, A_log, Dskip, norm_w, W_out):
            Bb, Ll, _ = x.shape
            zxbcdt = x @ W_in.T
            z = zxbcdt[..., :D_INNER]
            xBC = zxbcdt[..., D_INNER:D_INNER + CONV_DIM]
            dt = jax.nn.softplus(zxbcdt[..., D_INNER + CONV_DIM:] + dt_bias)
            xBC = jnp.transpose(xBC, (0, 2, 1))
            xBC = jax.lax.conv_general_dilated(xBC, conv_w[:, None, :], (1,), [(D_CONV - 1, 0)], feature_group_count=CONV_DIM)
            xBC = jax.nn.silu(jnp.transpose(xBC + conv_b[None, :, None], (0, 2, 1)))
            xs = xBC[..., :D_INNER].reshape(Bb, Ll, NHEADS, HEADDIM)
            Bm = xBC[..., D_INNER:D_INNER + D_STATE]
            Cm = xBC[..., D_INNER + D_STATE:]
            A = -jnp.exp(A_log)
            dA = jnp.exp(dt * A)

            def step(state, inp):
                dA_t, dt_t, B_t, C_t, x_t = inp
                dBx = jnp.einsum('bh,bn,bhp->bhpn', dt_t, B_t, x_t)
                state = state * dA_t[:, :, None, None] + dBx
                return (state, jnp.einsum('bhpn,bn->bhp', state, C_t))
            state0 = jnp.zeros((Bb, NHEADS, HEADDIM, D_STATE), x.dtype)
            _, y = jax.lax.scan(step, state0, (jnp.moveaxis(dA, 1, 0), jnp.moveaxis(dt, 1, 0), jnp.moveaxis(Bm, 1, 0), jnp.moveaxis(Cm, 1, 0), jnp.moveaxis(xs, 1, 0)))
            y = jnp.moveaxis(y, 0, 1) + Dskip[None, None, :, None] * xs
            y = y.reshape(Bb, Ll, D_INNER)
            y = _rmsnorm(y * jax.nn.silu(z), norm_w)
            return y @ W_out.T
        residual = x
        xn = _rmsnorm(x, norm_weight)
        y_fwd = _mamba2(xn, fwd_W_in, fwd_conv_w, fwd_conv_b, fwd_dt_bias, fwd_A_log, fwd_D, fwd_norm_w, fwd_W_out)
        y_bwd = jnp.flip(_mamba2(jnp.flip(xn, 1), bwd_W_in, bwd_conv_w, bwd_conv_b, bwd_dt_bias, bwd_A_log, bwd_D, bwd_norm_w, bwd_W_out), 1)
        out = jnp.concatenate([y_fwd, y_bwd], axis=-1) @ proj_W.T + proj_b
        return residual + out

    def _L1_xattn_ref(q, k, v, Wq, bq, Wk, bk, Wv, bv, Wo, bo):
        import jax, jax.numpy as jnp
        import numpy as np
        HEADS = 16
        D_MODEL = 128
        IMG_MODEL = 64
        D_K = D_MODEL // HEADS
        B, LQ, _ = q.shape
        LKV = k.shape[1]
        qh = (q @ Wq + bq).reshape(B, LQ, HEADS, D_K).transpose(0, 2, 1, 3)
        kh = (k @ Wk + bk).reshape(B, LKV, HEADS, D_K).transpose(0, 2, 1, 3)
        vh = (v @ Wv + bv).reshape(B, LKV, HEADS, D_K).transpose(0, 2, 1, 3)
        scale = 1.0 / np.sqrt(D_K)
        scores = jnp.einsum('bhqd,bhkd->bhqk', qh, kh) * scale
        attn = jax.nn.softmax(scores, axis=-1)
        out = jnp.einsum('bhqk,bhkd->bhqd', attn, vh)
        concat = out.transpose(0, 2, 1, 3).reshape(B, LQ, D_MODEL)
        return concat @ Wo + bo

    def _L1_ffn_ref(x, W1, b1, W2, b2, Wr, br):
        import jax, jax.numpy as jnp
        import numpy as np
        K = 2
        B, S, D = x.shape
        xf = x.reshape(-1, D)
        T = xf.shape[0]
        logits = xf @ Wr + br
        _, topk_idx = jax.lax.top_k(logits, K)
        mask = jnp.zeros_like(logits).at[jnp.arange(T)[:, None], topk_idx].set(1.0)
        gates = mask + logits - jax.lax.stop_gradient(logits)
        h = jax.nn.relu(jnp.einsum('td,edh->eth', xf, W1) + b1[:, None, :])
        combined = jnp.einsum('te,eth,ehd->td', gates, h, W2) + gates @ b2
        return x + combined.reshape(B, S, D)
    x = x + _L0_attn_ref(_layernorm(x, axis=-1), L0_attn_Wqkv, L0_attn_bqkv, L0_attn_Wout, L0_attn_bout, L0_attn_omega, L0_attn_quad_nodes, L0_attn_quad_weights)
    x = x + _L0_xattn_ref(_layernorm(x, axis=-1), ctx_512, L0_xattn_Wq, L0_xattn_Wk, L0_xattn_Wv, L0_xattn_Wo, L0_xattn_bo)
    x = x + _L0_ffn_ref(_layernorm(x, axis=-1), L0_ffn_wqkv, L0_ffn_q_scale, L0_ffn_k_scale, L0_ffn_wo, L0_ffn_ln_g, L0_ffn_ln_b, L0_ffn_w1, L0_ffn_b1, L0_ffn_w2, L0_ffn_b2)
    x = x + _L1_attn_ref(_layernorm(x, axis=-1), L1_attn_norm_weight, L1_attn_fwd_W_in, L1_attn_fwd_conv_w, L1_attn_fwd_conv_b, L1_attn_fwd_dt_bias, L1_attn_fwd_A_log, L1_attn_fwd_D, L1_attn_fwd_norm_w, L1_attn_fwd_W_out, L1_attn_bwd_W_in, L1_attn_bwd_conv_w, L1_attn_bwd_conv_b, L1_attn_bwd_dt_bias, L1_attn_bwd_A_log, L1_attn_bwd_D, L1_attn_bwd_norm_w, L1_attn_bwd_W_out, L1_attn_proj_W, L1_attn_proj_b)
    x = x + _L1_xattn_ref(_layernorm(x, axis=-1), ctx_512, ctx_512, L1_xattn_Wq, L1_xattn_bq, L1_xattn_Wk, L1_xattn_bk, L1_xattn_Wv, L1_xattn_bv, L1_xattn_Wo, L1_xattn_bo)
    x = x + _L1_ffn_ref(_layernorm(x, axis=-1), L1_ffn_W1, L1_ffn_b1, L1_ffn_W2, L1_ffn_b2, L1_ffn_Wr, L1_ffn_br)
    return x

_drawn_inputs = setup_inputs


def setup_inputs(seed=0):
    import zlib

    import numpy as np

    out = dict(_drawn_inputs(seed))
    spreads = {'L0_attn_bqkv': (0.0, 0.1),
     'L0_attn_bout': (0.0, 0.1),
     'L0_ffn_q_scale': (1.0, 0.6),
     'L0_ffn_k_scale': (1.0, 0.6),
     'L0_ffn_ln_g': (1.0, 0.6),
     'L0_ffn_ln_b': (0.0, 0.768),
     'L0_ffn_b1': (0.0, 0.39),
     'L0_ffn_b2': (0.0, 0.1),
     'L1_attn_norm_weight': (1.0, 0.2),
     'L1_attn_fwd_conv_b': (0.0, 0.1),
     'L1_attn_fwd_D': (1.0, 0.6),
     'L1_attn_fwd_norm_w': (1.0, 0.6),
     'L1_attn_bwd_conv_b': (0.0, 0.1),
     'L1_attn_bwd_D': (1.0, 0.6),
     'L1_attn_bwd_norm_w': (1.0, 0.6),
     'L1_attn_proj_b': (0.0, 0.1),
     'L1_xattn_bq': (0.0, 0.294),
     'L1_xattn_bk': (0.0, 0.8),
     'L1_xattn_bv': (0.0, 0.1),
     'L1_xattn_bo': (0.0, 0.1),
     'L1_ffn_b1': (0.0, 0.35),
     'L1_ffn_b2': (0.0, 0.1),
     'L1_ffn_br': (0.0, 0.1)}
    factors = {'L0_attn_omega': 4.346,
     'L0_attn_quad_nodes': 2.92,
     'L0_attn_quad_weights': 2.919,
     'L1_attn_fwd_dt_bias': 8.0,
     'L1_attn_fwd_A_log': 8.0,
     'L1_attn_bwd_dt_bias': 8.0,
     'L1_attn_bwd_A_log': 8.0}
    for name, (base, spread) in spreads.items():
        noise = np.random.default_rng([zlib.crc32(name.encode()), seed]).standard_normal(out[name].shape)
        drawn = base * np.exp(spread * noise) if base else spread * noise
        out[name] = jnp.asarray(drawn.astype(out[name].dtype))
    for name, factor in factors.items():
        out[name] = (out[name] * factor).astype(out[name].dtype)
    return out
```

```python
from contextlib import ExitStack

import numpy as np

import concourse.bass as bass
from concourse import mybir

F32 = mybir.dt.float32
ALU = mybir.AluOpType
ACT = mybir.ActivationFunctionType
AX = mybir.AxisListType.X

T = 128
C = 128
LN_EPS = 1e-5


class Steps:

    def __init__(self, sems, steps):
        self.sems = sems
        self.order = " ".join(steps).split()
        self.index = {name: i for i, name in enumerate(self.order)}
        assert len(self.index) == len(self.order), "a step's name stands twice"
        self.per_trip = len(self.order)
        self.next = [0, 0]

    def start(self, eng):
        for sem in self.sems:
            eng.sem_inc(sem, self.per_trip)

    def did(self, name, lane):
        assert self.order[self.next[lane]] == name, (self.order[self.next[lane]], name, lane)
        self.next[lane] = (self.next[lane] + 1) % self.per_trip
        return self.sems[lane], 1

    def at(self, name, trip, lane, ago=0):
        return self.sems[lane], trip * self.per_trip + (self.per_trip * (1 - ago) + self.index[name] + 1)


class Memory:

    def __init__(self, nc, stack, prefix):
        self.nc, self.stack, self.prefix = nc, stack, prefix

    def sb(self, name, shape):
        return self.stack.enter_context(self.nc.sbuf_tensor(f"{self.prefix}_{name}", shape, F32))

    def ps(self, name, shape):
        return self.stack.enter_context(self.nc.psum_tensor(f"{self.prefix}_{name}", shape, F32))

    def sem(self, name):
        return self.stack.enter_context(self.nc.semaphore(f"{self.prefix}_{name}"))

    def lanes(self, name):
        return [self.sem(f"{name}{lane}") for lane in (0, 1)]


def flat(ap):
    return ap.rearrange("p b c -> p (b c)")


def row_bc(dram, n=128):
    return dram.partition_broadcast(n)


def diagonal(buf, blocks, step, width, rows=128):
    whole = buf[:]
    return bass.AP(tensor=whole.tensor, offset=whole.offset,
                   ap=[[whole.ap[0][0], rows], [step, blocks], [1, width]])


def constants(nc, g, block_scope):
    m = Memory(nc, block_scope, "k")
    g.ident = m.sb("ident", [128, 128])
    g.tri = m.sb("tri", [128, 128])
    g.after = m.sb("after", [128, 128])
    g.shift = m.sb("shift", [128, 128])
    g.local = m.sb("local", [128, 128])
    g.ones = m.sb("ones", [128, 128])
    g.x = m.sb("x", [T, g.NB, C])
    made, xload = m.sem("made"), m.sem("xload")
    with nc.Block() as block:
        @block.sync
        def _(sp):
            sp.dma_start(g.x[:], g.d["x"].rearrange("b t c -> t b c")).then_inc(xload, 16)
            sp.wait_ge(xload, 16)

        @block.gpsimd
        def _(pool):
            for i, (buf, value) in enumerate([(g.ident, 0.0), (g.shift, 0.0), (g.tri, 1.0), (g.after, 1.0),
                                              (g.local, 0.0), (g.ones, 1.0)]):
                pool.memset(buf[:], value).then_inc(made, 1)
            pool.wait_ge(made, 6)
            pool.affine_select(out=g.ident[:], in_=g.ident[:], compare_op=ALU.not_equal, fill=1.0,
                               base=0, pattern=[[-1, 128]], channel_multiplier=1).then_inc(made, 1)
            pool.affine_select(out=g.shift[:], in_=g.shift[:], compare_op=ALU.not_equal, fill=1.0,
                               base=1, pattern=[[-1, 128]], channel_multiplier=1).then_inc(made, 1)
            pool.affine_select(out=g.tri[:], in_=g.tri[:], compare_op=ALU.is_ge, fill=0.0,
                               base=0, pattern=[[1, 128]], channel_multiplier=-1).then_inc(made, 1)
            pool.affine_select(out=g.after[:], in_=g.after[:], compare_op=ALU.is_gt, fill=0.0,
                               base=0, pattern=[[-1, 128]], channel_multiplier=1).then_inc(made, 1)
            pool.affine_select(out=g.local[:], in_=g.local[:], compare_op=ALU.is_ge, fill=-1e30,
                               base=0, pattern=[[-1, 128]], channel_multiplier=1).then_inc(made, 1)
            pool.wait_ge(made, 11)
            pool.affine_select(out=g.local[:], in_=g.local[:], compare_op=ALU.is_ge, fill=-1e30,
                               base=64, pattern=[[1, 128]], channel_multiplier=-1).then_inc(made, 1)
            pool.wait_ge(made, 12)


def both(m, name, shape):
    return [m.sb(f"{name}{lane}", shape) for lane in (0, 1)]


def row_statistics(v, vec, trip, l, stats, mv, carrier, src):
    v.bn_stats(stats, src).then_inc(*vec.did("stats", l))
    v.wait_ge(*vec.at("stats", trip, l))
    v.memset(carrier, 0.0)
    v.bn_aggr(mv[:], stats).then_inc(*vec.did("mv", l))


def rsqrt_of_variance(sc, act, trip, l, rstd, mv, eps, ln="lnv", exp="rstd"):
    sc.activation(rstd[:, 0:1], mv[:, 1:2], ACT.Ln, bias=eps[:]).then_inc(*act.did(ln, l))
    sc.wait_ge(*act.at(ln, trip, l))
    sc.activation(rstd[:, 1:2], rstd[:, 0:1], ACT.Exp, scale=-0.5).then_inc(*act.did(exp, l))


def linear_attention(nc, g):
    H, HD, M, R = 16, 8, 32, 2
    PAIRS = H // 2
    TRIPS = g.NB // 2
    d = g.d
    with ExitStack() as stack:
        m = Memory(nc, stack, "la")
        wqkv = m.sb("wqkv", [C, 3 * C])
        bqkv = m.sb("bqkv", [T, 3 * C])
        wout = m.sb("wout", [C, C])
        bout = m.sb("bout", [T, C])
        omega = m.sb("omega", [C, PAIRS, 2, R, M])
        node = m.sb("node", [128, 1])
        fscale = m.sb("fscale", [128, 1])
        fbias = m.sb("fbias", [128, 1])
        fweight = m.sb("fweight", [128, 1])
        eps = m.sb("eps", [128, 1])
        lnscale = m.sb("lnscale", [128, 1])
        xin = [m.sb(f"xin{l}", [T, C]) for l in (0, 1)]
        xb = [m.sb(f"xb{l}", [T, C]) for l in (0, 1)]
        stats = [m.sb(f"stats{l}", [T, 6]) for l in (0, 1)]
        mv = [m.sb(f"mv{l}", [T, 2]) for l in (0, 1)]
        rstd = [m.sb(f"rstd{l}", [T, 2]) for l in (0, 1)]
        xn = [m.sb(f"xn{l}", [T, C]) for l in (0, 1)]
        xnT = [m.sb(f"xnT{l}", [C, T]) for l in (0, 1)]
        qkv = [m.sb(f"qkv{l}", [T, 3 * C]) for l in (0, 1)]
        sq = [m.sb(f"sq{l}", [T, 2 * C]) for l in (0, 1)]
        ss = [m.sb(f"ss{l}", [T, 3, 2 * H]) for l in (0, 1)]
        qkT = [m.sb(f"qkT{l}", [C, 2, T]) for l in (0, 1)]
        ef = [m.sb(f"ef{l}", [128, 2, PAIRS, T]) for l in (0, 1)]
        qf = [m.sb(f"qf{l}", [128, PAIRS, 2, T]) for l in (0, 1)]
        sm = [m.sb(f"sm{l}", [T, H, T]) for l in (0, 1)]
        vpad = [m.sb(f"vpad{l}", [T, H, C + H]) for l in (0, 1)]
        den = [m.sb(f"den{l}", [T, 2, H]) for l in (0, 1)]
        att = [m.sb(f"att{l}", [T, C]) for l in (0, 1)]
        attT = [m.sb(f"attT{l}", [C, T]) for l in (0, 1)]
        ps = [m.ps(f"ps{l}", [128, 4, 512]) for l in (0, 1)]

        loaded, zeroed, prep = m.sem("loaded"), m.sem("zeroed"), m.sem("prep")
        x_in = [m.sem(f"x_in{l}") for l in (0, 1)]
        vec = Steps(m.lanes("vec_done"), ["stats mv", "xn", "qkv sq ss ssm", "qkn", "qf0 qf1 kf",
                                        "mask0 mask1 mask2 mask3", "den rden att", "x"])
        act = Steps(m.lanes("act_done"), ["lnv rstd", "xnT", "lnn rn", "qkT", "eq ek", "attT"])
        pe = Steps(m.lanes("pe_done"), ["xnT", "qkv", "qkT", "fq fk", "scores", "pv", "attT", "y"])
        pool = Steps(m.lanes("pool_done"), ["xb", "v", "kfw"])

        with nc.Block() as block:
            @block.sync
            def _(sp):
                sp.dma_start(wqkv[:], d["L0_attn_Wqkv"]).then_inc(loaded, 16)
                sp.dma_start(bqkv[:], row_bc(d["L0_attn_bqkv"])).then_inc(loaded, 16)
                sp.dma_start(wout[:], d["L0_attn_Wout"]).then_inc(loaded, 16)
                sp.dma_start(bout[:], row_bc(d["L0_attn_bout"])).then_inc(loaded, 16)
                for p in range(4):
                    r = p % 2
                    rows = slice(32 * p, 32 * p + 32)
                    sp.dma_start(node[rows, :], row_bc(d["L0_attn_quad_nodes"][r:r + 1], 32)).then_inc(loaded, 16)
                    sp.dma_start(fweight[rows, :], row_bc(d["L0_attn_quad_weights"][r:r + 1], 32)).then_inc(loaded, 16)
                sp.wait_ge(zeroed, 1)
                for h in range(H):
                    sp.dma_start(omega[HD * h:HD * h + HD, h // 2, h % 2, :, :],
                                 d["L0_attn_omega"][:, h].rearrange("r d m -> d r m")).then_inc(loaded, 16)
                with sp.Fori(0, TRIPS) as trip:
                    for l in (0, 1):
                        src = flat(g.x[:, bass.ds(sp.snap(trip * 2 + l), 1), :])
                        sp.wait_ge(*vec.at("xn", trip, l, ago=1))
                        sp.dma_start(xin[l][:], src).then_inc(x_in[l], 16)

            @block.gpsimd
            def _(gp):
                gp.memset(omega[:], 0.0).then_inc(zeroed, 1)
                for l in (0, 1):
                    gp.memset(vpad[l][:], 0.0).then_inc(zeroed, 1)
                    gp.memset(qf[l][:], 0.0).then_inc(zeroed, 1)
                gp.memset(eps[:], LN_EPS).then_inc(zeroed, 1)
                gp.memset(lnscale[:], 10.0 * float(np.log(2.0))).then_inc(zeroed, 1)
                gp.wait_ge(zeroed, 7)
                for l in (0, 1):
                    for h in range(H):
                        gp.memset(vpad[l][:, h, C + h:C + h + 1], 1.0).then_inc(zeroed, 1)
                pool.start(gp)
                gp.wait_ge(loaded, 16 * (12 + H))
                gp.wait_ge(prep, 3)
                with gp.Fori(0, TRIPS) as trip:
                    for l in (0, 1):
                        gp.wait_ge(x_in[l], trip * 16 + 16)
                        gp.wait_ge(*vec.at("x", trip, l, ago=1))
                        gp.tensor_tensor(xb[l][:], xin[l][:], bout[:], ALU.add).then_inc(*pool.did("xb", l))
                    for l in (0, 1):
                        gp.wait_ge(*vec.at("qkv", trip, l))
                        gp.tensor_tensor(diagonal(vpad[l], H, C + H + HD, HD),
                                         qkv[l][:, 2 * C:3 * C].rearrange("p (h e) -> p h e", h=H),
                                         g.ones[:].rearrange("p (h e) -> p h e", h=H), ALU.mult).then_inc(*pool.did("v", l))
                    for l in (0, 1):
                        gp.wait_ge(*vec.at("kf", trip, l))
                        gp.tensor_tensor(ef[l][:, 1], ef[l][:, 1],
                                         fweight[:].unsqueeze(2).to_broadcast([128, PAIRS, T]), ALU.mult).then_inc(*pool.did("kfw", l))

            @block.scalar
            def _(sc):
                sc.wait_ge(prep, 1)
                sc.activation(fscale[:], fscale[:], ACT.Sqrt).then_inc(prep, 1)
                sc.preload_act_table_set("natural_log_exp_and_others")
                act.start(sc)
                sc.wait_ge(zeroed, 7)
                sc.wait_ge(prep, 3)
                with sc.Fori(0, TRIPS) as trip:
                    for l in (0, 1):
                        sc.wait_ge(*vec.at("mv", trip, l))
                        rsqrt_of_variance(sc, act, trip, l, rstd[l], mv[l], eps)
                    for l in (0, 1):
                        sc.wait_ge(*pe.at("xnT", trip, l))
                        sc.activation(xnT[l][:], ps[l][:, 0, 0:T], ACT.Copy).then_inc(*act.did("xnT", l))
                    for l in (0, 1):
                        sc.wait_ge(*vec.at("ssm", trip, l))
                        sc.activation(ss[l][:, 1], ss[l][:, 0], ACT.Ln, scale=2.0 ** 20).then_inc(*act.did("lnn", l))
                        sc.wait_ge(*act.at("lnn", trip, l))
                        sc.activation(ss[l][:, 2], ss[l][:, 1], ACT.Exp, scale=-0.5, bias=lnscale[:]
                                      ).then_inc(*act.did("rn", l))
                    for l in (0, 1):
                        sc.wait_ge(*pe.at("qkT", trip, l))
                        sc.activation(qkT[l][:], ps[l][:, 0, 0:2 * T].rearrange("p (a t) -> p a t", a=2), ACT.Copy
                                      ).then_inc(*act.did("qkT", l))
                    for l in (0, 1):
                        sc.wait_ge(*pe.at("fq", trip, l))
                        sc.activation(ef[l][:, 0].rearrange("p a t -> p (a t)"),
                                      ps[l][:, 2:4].rearrange("p a t -> p (a t)"), ACT.Exp,
                                      bias=fbias[:, 0:1], scale=fscale[:, 0:1]).then_inc(*act.did("eq", l))
                        sc.wait_ge(*pe.at("fk", trip, l))
                        sc.activation(ef[l][:, 1].rearrange("p a t -> p (a t)"),
                                      ps[l][:, 0:2].rearrange("p a t -> p (a t)"), ACT.Exp,
                                      bias=fbias[:, 0:1], scale=fscale[:, 0:1]).then_inc(*act.did("ek", l))
                    for l in (0, 1):
                        sc.wait_ge(*pe.at("attT", trip, l))
                        sc.activation(attT[l][:], ps[l][:, 1, 0:T], ACT.Copy).then_inc(*act.did("attT", l))

            @block.tensor
            def _(te):
                pe.start(te)
                te.wait_ge(loaded, 16 * (12 + H))
                te.wait_ge(zeroed, 7 + 2 * H)
                with te.Fori(0, TRIPS) as trip:
                    for l in (0, 1):
                        te.wait_ge(*vec.at("xn", trip, l))
                        te.transpose(ps[l][:, 0, 0:T], xn[l][:], g.ident[:]).then_inc(*pe.did("xnT", l))
                    for l in (0, 1):
                        te.wait_ge(*act.at("xnT", trip, l))
                        te.matmul(ps[l][:, 1, 0:3 * C], xnT[l][:], wqkv[:], start=True, stop=True
                                  ).then_inc(*pe.did("qkv", l))
                    for l in (0, 1):
                        te.wait_ge(*vec.at("qkn", trip, l))
                        te.transpose(ps[l][:, 0, 0:T], qkv[l][:, 0:C], g.ident[:])
                        te.transpose(ps[l][:, 0, T:2 * T], qkv[l][:, C:2 * C], g.ident[:]).then_inc(*pe.did("qkT", l))
                    for l in (0, 1):
                        te.wait_ge(*act.at("qkT", trip, l))
                        for side, bank, step in ((0, 2, "fq"), (1, 0, "fk")):
                            for j in range(PAIRS):
                                mm = te.matmul(ps[l][:, bank + j // 4, T * (j % 4):T * (j % 4) + T],
                                               omega[:, j].rearrange("p a r m -> p (a r m)"),
                                               qkT[l][:, side], start=True, stop=True)
                            mm.then_inc(*pe.did(step, l))
                    for l in (0, 1):
                        te.wait_ge(*pool.at("kfw", trip, l))
                        te.wait_ge(*vec.at("qf1", trip, l))
                        for j in range(PAIRS):
                            mm = te.matmul(ps[l][:, j // 2, 2 * T * (j % 2):2 * T * (j % 2) + 2 * T],
                                           ef[l][:, 1, j], qf[l][:, j].rearrange("p a t -> p (a t)"),
                                           start=True, stop=True)
                        mm.then_inc(*pe.did("scores", l))
                    for l in (0, 1):
                        te.wait_ge(*vec.at("mask3", trip, l))
                        te.wait_ge(*pool.at("v", trip, l))
                        for h in range(H):
                            mm = te.matmul(ps[l][:, 0, 0:C + H], sm[l][:, h], vpad[l][:, h],
                                           start=(h == 0), stop=(h == H - 1))
                        mm.then_inc(*pe.did("pv", l))
                    for l in (0, 1):
                        te.wait_ge(*vec.at("att", trip, l))
                        te.transpose(ps[l][:, 1, 0:T], att[l][:], g.ident[:]).then_inc(*pe.did("attT", l))
                    for l in (0, 1):
                        te.wait_ge(*act.at("attT", trip, l))
                        te.matmul(ps[l][:, 2, 0:C], attT[l][:], wout[:], start=True, stop=True
                                  ).then_inc(*pe.did("y", l))

            @block.vector
            def _(v):
                v.wait_ge(loaded, 16 * (12 + H))
                v.tensor_scalar(fscale[:], node[:], 0.0, 2.0, ALU.max, ALU.mult).then_inc(prep, 1)
                v.tensor_scalar(fbias[:], node[:], -1.0, None, ALU.mult).then_inc(prep, 1)
                v.wait_ge(prep, 3)
                v.tensor_scalar(fweight[:], fweight[:], 0.0, 1.0 / M, ALU.max, ALU.mult).then_inc(prep, 1)
                vec.start(v)
                v.wait_ge(prep, 4)
                with v.Fori(0, TRIPS) as trip:
                    for l in (0, 1):
                        v.wait_ge(x_in[l], trip * 16 + 16)
                        v.wait_ge(*vec.at("x", trip, l, ago=1))
                        row_statistics(v, vec, trip, l, stats[l][:], mv[l], rstd[l][:, 1:2], xin[l][:])
                    for l in (0, 1):
                        v.wait_ge(*pool.at("xb", trip, l))
                        v.wait_ge(*act.at("rstd", trip, l))
                        v.tensor_scalar(xn[l][:], xin[l][:], mv[l][:, 0:1], rstd[l][:, 1:2], ALU.subtract, ALU.mult
                                        ).then_inc(*vec.did("xn", l))
                    for l in (0, 1):
                        v.wait_ge(*pe.at("qkv", trip, l))
                        v.tensor_tensor(qkv[l][:], ps[l][:, 1, 0:3 * C], bqkv[:], ALU.add).then_inc(*vec.did("qkv", l))
                        v.wait_ge(*vec.at("qkv", trip, l))
                        v.tensor_tensor(sq[l][:], qkv[l][:, 0:2 * C], qkv[l][:, 0:2 * C], ALU.mult
                                        ).then_inc(*vec.did("sq", l))
                        v.wait_ge(*vec.at("sq", trip, l))
                        v.tensor_reduce(ss[l][:, 0], sq[l][:].rearrange("p (h e) -> p h e", e=HD), AX, ALU.add
                                        ).then_inc(*vec.did("ss", l))
                        v.wait_ge(*vec.at("ss", trip, l))
                        v.tensor_scalar(ss[l][:, 0], ss[l][:, 0], 1e-24, None, ALU.max).then_inc(*vec.did("ssm", l))
                    for l in (0, 1):
                        v.wait_ge(*act.at("rn", trip, l))
                        qk = qkv[l][:, 0:2 * C].rearrange("p (h e) -> p h e", e=HD)
                        v.tensor_tensor(qk, qk, ss[l][:, 2].unsqueeze(2).to_broadcast([T, 2 * H, HD]), ALU.mult
                                        ).then_inc(*vec.did("qkn", l))
                    for l in (0, 1):
                        hi, lo = float(np.exp(np.float64(20.0))), float(np.exp(np.float64(-20.0)))
                        v.wait_ge(*act.at("eq", trip, l))
                        for a in (0, 1):
                            rows = slice(64 * a, 64 * a + 64)
                            v.tensor_scalar(qf[l][rows, :, a, :], ef[l][rows, 0], hi, lo, ALU.min, ALU.max
                                            ).then_inc(*vec.did(f"qf{a}", l))
                        v.wait_ge(*act.at("ek", trip, l))
                        v.tensor_scalar(ef[l][:, 1], ef[l][:, 1], hi, lo, ALU.min, ALU.max
                                        ).then_inc(*vec.did("kf", l))
                    for l in (0, 1):
                        v.wait_ge(*pe.at("scores", trip, l))
                        for c in range(4):
                            v.tensor_tensor(sm[l][:, 4 * c:4 * c + 4],
                                            ps[l][:, c].rearrange("p (h t) -> p h t", h=4),
                                            g.tri[:].unsqueeze(1).to_broadcast([T, 4, T]), ALU.mult
                                            ).then_inc(*vec.did(f"mask{c}", l))
                    for l in (0, 1):
                        v.wait_ge(*pe.at("pv", trip, l))
                        v.tensor_scalar(den[l][:, 0], ps[l][:, 0, C:C + H], 1e-6, None, ALU.max
                                        ).then_inc(*vec.did("den", l))
                        v.wait_ge(*vec.at("den", trip, l))
                        v.reciprocal(den[l][:, 1], den[l][:, 0]).then_inc(*vec.did("rden", l))
                        v.wait_ge(*vec.at("rden", trip, l))
                        v.tensor_tensor(att[l][:].rearrange("p (h e) -> p h e", e=HD),
                                        ps[l][:, 0, 0:C].rearrange("p (h e) -> p h e", e=HD),
                                        den[l][:, 1].unsqueeze(2).to_broadcast([T, H, HD]), ALU.mult
                                        ).then_inc(*vec.did("att", l))
                    for l in (0, 1):
                        v.wait_ge(*pe.at("y", trip, l))
                        v.tensor_tensor(flat(g.x[:, bass.ds(trip * 2 + l, 1), :]), xb[l][:], ps[l][:, 2, 0:C], ALU.add
                                        ).then_inc(*vec.did("x", l))


def cross_attention(nc, g):
    H, HD, CD, S = 16, 64, g.d["ctx_512"].shape[2], g.d["ctx_512"].shape[1]
    PAIRS = H // 2
    TRIPS = g.NB // 2
    d = g.d
    with ExitStack() as stack:
        m = Memory(nc, stack, "ca")
        wqk = m.sb("wqk", [C, PAIRS, 2, CD])
        wvo = m.sb("wvo", [2 * CD, PAIRS, C])
        with ExitStack() as once:
            mo = Memory(nc, once, "cw")
            wq = mo.sb("wq", [C, H * HD])
            wk = mo.sb("wk", [CD, H * HD])
            wv = mo.sb("wv", [CD, H * HD])
            wo = mo.sb("wo", [2 * HD, PAIRS, C])
            wqT = mo.sb("wqT", [2 * HD, PAIRS, C])
            wkT = mo.sb("wkT", [2 * HD, PAIRS, CD])
            wvT = mo.sb("wvT", [2 * HD, PAIRS, CD])
            pw = mo.ps("pw", [128, 4, 512])
            pp = mo.ps("pp", [128, 4, 512])
            loaded, turned, copied, product = (mo.sem(n) for n in ("loaded", "turned", "copied", "product"))
            done = mo.sem("done")
            with nc.Block() as block:
                @block.sync
                def _(sp):
                    sp.dma_start(wq[:], d["L0_xattn_Wq"]).then_inc(loaded, 16)
                    sp.dma_start(wk[:], d["L0_xattn_Wk"]).then_inc(loaded, 16)
                    sp.dma_start(wv[:], d["L0_xattn_Wv"]).then_inc(loaded, 16)
                    sp.dma_start(wo[:], d["L0_xattn_Wo"].rearrange("(j p) n -> p j n", p=128)).then_inc(loaded, 16)

                @block.tensor
                def _(te):
                    te.wait_ge(loaded, 64)
                    for j in range(PAIRS):
                        mm = te.transpose(pw[:, j // 4, C * (j % 4):C * (j % 4) + C], wq[:, 128 * j:128 * j + 128],
                                          g.ident[:])
                    mm.then_inc(turned, 1)
                    for i, w in enumerate((wk, wv)):
                        for j in range(PAIRS):
                            mm = te.transpose(pw[:, 2 + i, CD * j:CD * j + CD], w[:, 128 * j:128 * j + 128],
                                              g.ident[0:CD, 0:CD])
                        mm.then_inc(turned, 1)
                    te.wait_ge(copied, 3)
                    for h in range(H):
                        rows = slice(64 * (h % 2), 64 * (h % 2) + 64)
                        mm = te.matmul(pp[:, h % 2, CD * (h // 2):CD * (h // 2) + CD], wqT[rows, h // 2],
                                       wkT[rows, h // 2], start=True, stop=True)
                    mm.then_inc(product, 1)
                    for h in range(H):
                        rows = slice(64 * (h % 2), 64 * (h % 2) + 64)
                        j = h // 2
                        if h == PAIRS:
                            te.wait_ge(done, 1)
                        bank = 2 + h % 2 if h < PAIRS else h % 2
                        mm = te.matmul(pp[rows, bank, C * (j % 4):C * (j % 4) + C],
                                       wvT[rows, j], wo[rows, j], start=True, stop=True)
                    mm.then_inc(product, 1)

                @block.vector
                def _(v):
                    v.wait_ge(turned, 1)
                    v.tensor_copy(wqT[:].rearrange("p j c -> p (j c)"), pw[:, 0:2].rearrange("p a c -> p (a c)")
                                  ).then_inc(copied, 1)
                    for i, w in enumerate((wkT, wvT)):
                        v.wait_ge(turned, 2 + i)
                        v.tensor_copy(w[:].rearrange("p j c -> p (j c)"), pw[:, 2 + i, 0:PAIRS * CD]
                                      ).then_inc(copied, 1)
                    v.wait_ge(product, 1)
                    v.tensor_scalar(wqk[:].rearrange("p j a c -> p a j c"),
                                    pp[:, 0:2, 0:PAIRS * CD].rearrange("p a (j c) -> p a j c", c=CD),
                                    HD ** -0.5, None, ALU.mult).then_inc(done, 1)
                    v.wait_ge(product, 2)
                    for a in (0, 1):
                        rows = slice(64 * a, 64 * a + 64)
                        for half in (0, 1):
                            bank = 2 + a if half == 0 else a
                            v.tensor_copy(wvo[rows, 4 * half:4 * half + 4],
                                          pp[rows, bank, 0:4 * C].rearrange("p (j c) -> p j c", c=C)
                                          ).then_inc(done, 1)

        bo = m.sb("bo", [T, C])
        eps = m.sb("eps", [128, 1])
        xin, xb, xn = (both(m, n, [T, C]) for n in ("xin", "xb", "xn"))
        stats, mv, rstd = both(m, "stats", [T, 6]), both(m, "mv", [T, 2]), both(m, "rstd", [T, 2])
        xnT = both(m, "xnT", [C, T])
        ctx = both(m, "ctx", [128, 2, CD])
        ctxT = both(m, "ctxT", [2 * CD, 2, S])
        gT = both(m, "gT", [2 * CD, PAIRS, T])
        prob = both(m, "prob", [T, H, S])
        mx, sm = both(m, "mx", [T, H]), both(m, "sm", [T, 2, H])
        probT = both(m, "probT", [128, H, T])
        oT = both(m, "oT", [2 * CD, PAIRS, T])
        ps = [m.ps(f"ps{l}", [128, 4, 512]) for l in (0, 1)]
        loaded, zeroed = m.sem("loaded"), m.sem("zeroed")
        x_in = [m.sem(f"x_in{l}") for l in (0, 1)]
        c_in = [m.sem(f"c_in{l}") for l in (0, 1)]
        vec = Steps(m.lanes("vec_done"), ["stats mv", "xn", "mx sub", "sum rsum", "pT", "oT", "x"])
        act = Steps(m.lanes("act_done"), ["lnv rstd", "xnT cT0 cT1", "gT", "exp", "pT", "oT"])
        pe = Steps(m.lanes("pe_done"), ["xnT", "g", "s", "pT", "o", "y"])
        pool = Steps(m.lanes("pool_done"), ["xb", "norm"])
        NZERO = 7

        with nc.Block() as block:
            @block.sync
            def _(sp):
                sp.dma_start(bo[:], row_bc(d["L0_xattn_bo"])).then_inc(loaded, 16)
                sp.wait_ge(zeroed, NZERO)
                with sp.Fori(0, TRIPS) as trip:
                    for l in (0, 1):
                        b = sp.snap(trip * 2 + l)
                        src = flat(g.x[:, bass.ds(b, 1), :])
                        csrc = d["ctx_512"][bass.ds(b, 1)].rearrange("b s c -> (b s) c")
                        sp.wait_ge(*vec.at("xn", trip, l, ago=1))
                        sp.dma_start(xin[l][:], src).then_inc(x_in[l], 16)
                        sp.wait_ge(*pe.at("o", trip, l, ago=1))
                        for a in (0, 1):
                            sp.dma_start(ctx[l][0:S, a], csrc).then_inc(c_in[l], 16)

            @block.gpsimd
            def _(gp):
                for l in (0, 1):
                    gp.memset(ctx[l][:], 0.0).then_inc(zeroed, 1)
                    gp.memset(ctxT[l][:], 0.0).then_inc(zeroed, 1)
                    gp.memset(probT[l][:], 0.0).then_inc(zeroed, 1)
                gp.memset(eps[:], LN_EPS).then_inc(zeroed, 1)
                pool.start(gp)
                gp.wait_ge(loaded, 16)
                with gp.Fori(0, TRIPS) as trip:
                    for l in (0, 1):
                        gp.wait_ge(x_in[l], trip * 16 + 16)
                        gp.wait_ge(*vec.at("x", trip, l, ago=1))
                        gp.tensor_tensor(xb[l][:], xin[l][:], bo[:], ALU.add).then_inc(*pool.did("xb", l))
                    for l in (0, 1):
                        gp.wait_ge(*vec.at("rsum", trip, l))
                        gp.tensor_tensor(prob[l][:], prob[l][:], sm[l][:, 1].unsqueeze(2).to_broadcast([T, H, S]),
                                         ALU.mult).then_inc(*pool.did("norm", l))

            @block.scalar
            def _(sc):
                sc.preload_act_table_set("natural_log_exp_and_others")
                act.start(sc)
                sc.wait_ge(zeroed, NZERO)
                with sc.Fori(0, TRIPS) as trip:
                    for l in (0, 1):
                        sc.wait_ge(*vec.at("mv", trip, l))
                        rsqrt_of_variance(sc, act, trip, l, rstd[l], mv[l], eps)
                    for l in (0, 1):
                        sc.wait_ge(*pe.at("xnT", trip, l))
                        sc.activation(xnT[l][:], ps[l][:, 0, 0:T], ACT.Copy).then_inc(*act.did("xnT", l))
                        for a in (0, 1):
                            rows = slice(CD * a, CD * a + CD)
                            sc.activation(ctxT[l][rows, a], ps[l][rows, 0, T:T + S], ACT.Copy
                                          ).then_inc(*act.did(f"cT{a}", l))
                    for l in (0, 1):
                        sc.wait_ge(*pe.at("g", trip, l))
                        sc.activation(gT[l][:].rearrange("p j t -> p (j t)"),
                                      ps[l][:, 2:4].rearrange("p a t -> p (a t)"), ACT.Copy).then_inc(*act.did("gT", l))
                    for l in (0, 1):
                        sc.wait_ge(*vec.at("sub", trip, l))
                        sc.activation(prob[l][:], prob[l][:], ACT.Exp).then_inc(*act.did("exp", l))
                    for l in (0, 1):
                        sc.wait_ge(*pe.at("pT", trip, l))
                        sc.activation(probT[l][0:S, 0:8].rearrange("p h t -> p (h t)"),
                                      ps[l][0:S, 0:2].rearrange("p a t -> p (a t)"), ACT.Copy).then_inc(*act.did("pT", l))
                    for l in (0, 1):
                        sc.wait_ge(*pe.at("o", trip, l))
                        sc.activation(oT[l][0:CD], ps[l][0:CD].rearrange("p a (j e t) -> p (a j) e t", e=2, t=T)[:, :, 0],
                                      ACT.Copy).then_inc(*act.did("oT", l))

            @block.tensor
            def _(te):
                pe.start(te)
                te.wait_ge(zeroed, NZERO)
                with te.Fori(0, TRIPS) as trip:
                    for l in (0, 1):
                        te.wait_ge(c_in[l], trip * 32 + 32)
                        te.wait_ge(*vec.at("xn", trip, l))
                        te.transpose(ps[l][:, 0, 0:T], xn[l][:], g.ident[:])
                        te.transpose(ps[l][:, 0, T:2 * T], ctx[l][:].rearrange("p a c -> p (a c)"), g.ident[:]
                                     ).then_inc(*pe.did("xnT", l))
                    for l in (0, 1):
                        te.wait_ge(*act.at("cT1", trip, l))
                        for j in range(PAIRS):
                            mm = te.matmul(ps[l][:, 2 + j // 4, T * (j % 4):T * (j % 4) + T],
                                           wqk[:, j].rearrange("p a c -> p (a c)"), xnT[l][:], start=True, stop=True)
                        mm.then_inc(*pe.did("g", l))
                    for l in (0, 1):
                        te.wait_ge(*act.at("gT", trip, l))
                        for j in range(PAIRS):
                            mm = te.matmul(ps[l][:, j // 2, 2 * S * (j % 2):2 * S * (j % 2) + 2 * S],
                                           gT[l][:, j], ctxT[l][:].rearrange("p a s -> p (a s)"),
                                           start=True, stop=True)
                        mm.then_inc(*pe.did("s", l))
                    for l in (0, 1):
                        te.wait_ge(*pool.at("norm", trip, l))
                        for h in range(H):
                            mm = te.transpose(ps[l][0:S, h // 4, T * (h % 4):T * (h % 4) + T], prob[l][:, h],
                                              g.ident[:])
                        mm.then_inc(*pe.did("pT", l))
                    for l in (0, 1):
                        te.wait_ge(*act.at("pT", trip, l))
                        te.wait_ge(*vec.at("pT", trip, l))
                        for c in range(4):
                            mm = te.matmul(ps[l][:, c], ctx[l][:].rearrange("p a c -> p (a c)"),
                                           probT[l][:, 4 * c:4 * c + 4].rearrange("p h t -> p (h t)"),
                                           start=True, stop=True)
                        mm.then_inc(*pe.did("o", l))
                    for l in (0, 1):
                        te.wait_ge(*act.at("oT", trip, l))
                        te.wait_ge(*vec.at("oT", trip, l))
                        for j in range(PAIRS):
                            mm = te.matmul(ps[l][:, 0, 0:C], oT[l][:, j], wvo[:, j],
                                           start=(j == 0), stop=(j == PAIRS - 1))
                        mm.then_inc(*pe.did("y", l))

            @block.vector
            def _(v):
                vec.start(v)
                with v.Fori(0, TRIPS) as trip:
                    for l in (0, 1):
                        v.wait_ge(x_in[l], trip * 16 + 16)
                        v.wait_ge(*vec.at("x", trip, l, ago=1))
                        row_statistics(v, vec, trip, l, stats[l][:], mv[l], rstd[l][:, 1:2], xin[l][:])
                    for l in (0, 1):
                        v.wait_ge(*pool.at("xb", trip, l))
                        v.wait_ge(*act.at("rstd", trip, l))
                        v.tensor_scalar(xn[l][:], xin[l][:], mv[l][:, 0:1], rstd[l][:, 1:2], ALU.subtract, ALU.mult
                                        ).then_inc(*vec.did("xn", l))
                    for l in (0, 1):
                        scores = ps[l][:, :, 0:4 * S].rearrange("p a (h s) -> p a h s", s=S)
                        four = lambda ap: ap.rearrange("p (a h) -> p a h", a=4)
                        v.wait_ge(*pe.at("s", trip, l))
                        v.tensor_reduce(four(mx[l][:]), scores, AX, ALU.max).then_inc(*vec.did("mx", l))
                        v.wait_ge(*vec.at("mx", trip, l))
                        v.tensor_tensor(prob[l][:].rearrange("p (a h) s -> p a h s", a=4), scores,
                                        four(mx[l][:]).unsqueeze(3).to_broadcast([T, 4, 4, S]), ALU.subtract
                                        ).then_inc(*vec.did("sub", l))
                    for l in (0, 1):
                        v.wait_ge(*act.at("exp", trip, l))
                        v.tensor_reduce(sm[l][:, 0], prob[l][:], AX, ALU.add).then_inc(*vec.did("sum", l))
                        v.wait_ge(*vec.at("sum", trip, l))
                        v.reciprocal(sm[l][:, 1], sm[l][:, 0]).then_inc(*vec.did("rsum", l))
                    for l in (0, 1):
                        v.wait_ge(*pe.at("pT", trip, l))
                        v.tensor_copy(probT[l][0:S, 8:16].rearrange("p h t -> p (h t)"),
                                      ps[l][0:S, 2:4].rearrange("p a t -> p (a t)")).then_inc(*vec.did("pT", l))
                    for l in (0, 1):
                        v.wait_ge(*pe.at("o", trip, l))
                        v.tensor_copy(oT[l][CD:2 * CD],
                                      ps[l][CD:2 * CD].rearrange("p a (j e t) -> p (a j) e t", e=2, t=T)[:, :, 1]
                                      ).then_inc(*vec.did("oT", l))
                    for l in (0, 1):
                        v.wait_ge(*pe.at("y", trip, l))
                        v.tensor_tensor(flat(g.x[:, bass.ds(trip * 2 + l, 1), :]), xb[l][:], ps[l][:, 0, 0:C], ALU.add
                                        ).then_inc(*vec.did("x", l))


QK_SCALE = 8.0
ROT_DIM = 64


def shape_tables():
    window, half = 64, np.arange(0, ROT_DIM, 2, dtype=np.float32)
    t = np.arange(T, dtype=np.float32)
    freqs = t[:, None] * (np.float32(1.0) / np.float32(10000.0) ** (half / ROT_DIM))[None, :]
    base = (half + 0.4 * ROT_DIM) / (1.4 * ROT_DIM)
    scale = base[None, :] ** ((t - T // 2) / float(window // 2))[:, None]
    rot = np.zeros((T, 2, 2, ROT_DIM), np.float32)
    for side, s in enumerate((scale * QK_SCALE, 1.0 / scale)):
        rot[:, side, 0] = np.concatenate([np.cos(freqs) * s] * 2, axis=-1)
        rot[:, side, 1] = np.concatenate([-np.sin(freqs) * s, np.sin(freqs) * s], axis=-1)
    return {"rot": rot}


def local_attention(nc, g, layer):
    H, HD = 8, ROT_DIM
    PAIRS, INNER, HALF = H // 2, H * HD, C // 2
    PH = H - 3
    TRIPS = g.NB // 2
    d = g.d
    first = layer == 0
    with ExitStack() as stack:
        m = Memory(nc, stack, f"l{layer}")
        wqkv = m.sb("wqkv", [C, 3, INNER])
        wo = m.sb("wo", [2 * HD, PAIRS, C])
        rot = m.sb("rot", [T, 2, 2, HD])
        qks = m.sb("qks", [T, 2, 2, HD])
        eps, lnscale = m.sb("eps", [128, 1]), m.sb("lnscale", [128, 1])
        xin, yc, ynew = (both(m, n, [T, C]) for n in ("xin", "yc", "ynew"))
        stats, mv, rstd = both(m, "stats", [T, 12]), both(m, "mv", [T, 2]), both(m, "rstd", [T, 2])
        stats0, mv0, rstd0 = both(m, "stats0", [T, 6]), both(m, "mv0", [T, 2]), both(m, "rstd0", [T, 2])
        hT = both(m, "hT", [C, T])
        sq, rc = both(m, "sq", [T, 2 * H, HD]), both(m, "rc", [T, 2, H, HD])
        rs = both(m, "rs", [T, 2, H, HD])
        ss = both(m, "ss", [T, 3, 2 * H])
        val = both(m, "val", [T, INNER])
        qT = both(m, "qT", [2 * HD, PAIRS, T])
        kT = both(m, "kT", [2 * HD, PAIRS, 2, T])
        prob = both(m, "prob", [T, H, T])
        mx, sm = both(m, "mx", [T, H]), both(m, "sm", [T, 2, H])
        probT = both(m, "probT", [T, H, T])
        oT = both(m, "oT", [2 * HD, PAIRS, T])
        ps = [m.ps(f"ps{l}", [128, 4, 512]) for l in (0, 1)]
        loaded, zeroed, prep = m.sem("loaded"), m.sem("zeroed"), m.sem("prep")
        y_in = [m.sem(f"y_in{l}") for l in (0, 1)]
        vec_ahead = Steps(m.lanes("vec_ahead_done"), ["stats mv", "y0"])
        act_ahead = Steps(m.lanes("act_ahead_done"), ["lnv0 rstd0", "hT"] if first else ["hT"])
        pe_ahead = Steps(m.lanes("pe_ahead_done"), ["hT"])
        vec = Steps(m.lanes("vec_done"), ["ss ssm cos sin0 sin1 krot kn", "kT", " ".join(f"s{h}" for h in range(H)) + " mx",
                                        "rsum norm", "pT", "ynew y", "st1 st2 mv2", "hn0 hn1"])
        act = Steps(m.lanes("act_done"), ["sq v lnn rn", "qT kT", " ".join(f"exp{h}" for h in range(H)), "pT", "oT",
                                        "lnv rstd"])
        pe = Steps(m.lanes("pe_done"), ["qk v", "qkT", "s", "pT", "o", "ao", "sh"])
        pool = Steps(m.lanes("pool_done"), ["qrot", "norm"])
        NZERO, NLOAD = 4, 16 * (3 + 2 + 4)

        with nc.Block() as block:
            @block.sync
            def _(sp):
                sp.dma_start(wqkv[:], d["L0_ffn_wqkv"][layer].rearrange("c (a n) -> c a n", a=3)).then_inc(loaded, 16)
                sp.dma_start(wo[:], d["L0_ffn_wo"][layer].rearrange("(j p) n -> p j n", p=128)).then_inc(loaded, 16)
                sp.dma_start(rot[:], d["rot"]).then_inc(loaded, 16)
                for side, name in enumerate(("L0_ffn_q_scale", "L0_ffn_k_scale")):
                    row = d[name][layer]
                    sp.dma_start(qks[:, side, 0], row_bc(row)).then_inc(loaded, 16)
                    sp.dma_start(qks[:, side, 1, 0:HD // 2], row_bc(row[HD // 2:HD])).then_inc(loaded, 16)
                    sp.dma_start(qks[:, side, 1, HD // 2:HD], row_bc(row[0:HD // 2])).then_inc(loaded, 16)
                with sp.Fori(0, TRIPS) as trip:
                    for l in (0, 1):
                        src = flat((g.x if first else g.y)[:, bass.ds(sp.snap(trip * 2 + l), 1), :])
                        sp.wait_ge(*(vec_ahead.at("y0", trip, l, ago=1) if first else pe_ahead.at("hT", trip, l, ago=1)))
                        sp.dma_start((xin if first else yc)[l][:], src).then_inc(y_in[l], 16)

            @block.gpsimd
            def _(gp):
                gp.memset(eps[:], LN_EPS).then_inc(zeroed, 1)
                gp.memset(lnscale[:], 10.0 * float(np.log(2.0))).then_inc(zeroed, 1)
                for l in (0, 1):
                    gp.memset(kT[l][:], 0.0).then_inc(zeroed, 1)
                pool.start(gp)
                with gp.Fori(0, TRIPS) as trip:
                    for l in (0, 1):
                        gp.wait_ge(*vec.at("sin1", trip, l))
                        gp.tensor_tensor(rc[l][:, 0], rc[l][:, 0], rs[l][:, 0], ALU.add).then_inc(*pool.did("qrot", l))
                    for l in (0, 1):
                        gp.wait_ge(*vec.at("rsum", trip, l))
                        gp.tensor_tensor(prob[l][:, PH:H], prob[l][:, PH:H],
                                         sm[l][:, 1, PH:H].unsqueeze(2).to_broadcast([T, H - PH, T]), ALU.mult
                                         ).then_inc(*pool.did("norm", l))

            @block.scalar
            def _(sc):
                sc.preload_act_table_set("natural_log_exp_and_others")
                act.start(sc)
                act_ahead.start(sc)
                sc.wait_ge(zeroed, NZERO)

                def normalise(trip):
                    for l in ((0, 1) if first else ()):
                        sc.wait_ge(*vec_ahead.at("mv", trip, l))
                        rsqrt_of_variance(sc, act_ahead, trip, l, rstd0[l], mv0[l], eps, "lnv0", "rstd0")

                def turn(trip):
                    for l in (0, 1):
                        sc.wait_ge(*pe_ahead.at("hT", trip, l))
                        sc.activation(hT[l][:], ps[l][:, 0, 0:T], ACT.Copy).then_inc(*act_ahead.did("hT", l))

                def attend(trip, more):
                    for l in (0, 1):
                        sc.wait_ge(*pe.at("qk", trip, l))
                        sc.activation(sq[l][:].rearrange("p h e -> p (h e)"),
                                      ps[l][:, 1:3].rearrange("p a n -> p (a n)"), ACT.Square).then_inc(*act.did("sq", l))
                        sc.wait_ge(*pe.at("v", trip, l))
                        sc.activation(val[l][:], ps[l][:, 3], ACT.Copy).then_inc(*act.did("v", l))
                        sc.wait_ge(*vec.at("ssm", trip, l))
                        sc.activation(ss[l][:, 1], ss[l][:, 0], ACT.Ln, scale=2.0 ** 20).then_inc(*act.did("lnn", l))
                        sc.wait_ge(*act.at("lnn", trip, l))
                        sc.activation(ss[l][:, 2], ss[l][:, 1], ACT.Exp, scale=-0.5, bias=lnscale[:]
                                      ).then_inc(*act.did("rn", l))
                    for l in (0, 1):
                        sc.wait_ge(*pe.at("qkT", trip, l))
                        sc.activation(qT[l][:].rearrange("p j t -> p (j t)"), ps[l][:, 0], ACT.Copy
                                      ).then_inc(*act.did("qT", l))
                        sc.activation(kT[l][0:HD, :, 0], ps[l][0:HD, 1].rearrange("p (j t) -> p j t", t=T), ACT.Copy
                                      ).then_inc(*act.did("kT", l))
                    for l in (0, 1):
                        sc.wait_ge(*vec.at("mx", trip, l))
                        for h in range(H):
                            sc.activation(prob[l][:, h], prob[l][:, h], ACT.Exp, bias=mx[l][:, h:h + 1],
                                          accum_out=sm[l][:, 0, h:h + 1]).then_inc(*act.did(f"exp{h}", l))
                    for l in (0, 1):
                        sc.wait_ge(*pe.at("pT", trip, l))
                        sc.activation(probT[l][:, 0:4].rearrange("p h t -> p (h t)"), ps[l][:, 0], ACT.Copy
                                      ).then_inc(*act.did("pT", l))
                    for l in (0, 1):
                        sc.wait_ge(*pe.at("o", trip, l))
                        sc.activation(oT[l][:].rearrange("p j t -> p (j t)"), ps[l][:, 2], ACT.Copy
                                      ).then_inc(*act.did("oT", l))
                    if more:
                        normalise(trip + 1)
                    if more:
                        turn(trip + 1)
                    for l in (0, 1):
                        sc.wait_ge(*vec.at("mv2", trip, l))
                        rsqrt_of_variance(sc, act, trip, l, rstd[l], mv[l], eps)

                normalise(0)
                turn(0)
                with sc.Fori(0, TRIPS - 1) as trip:
                    attend(trip, True)
                attend(TRIPS - 1, False)

            @block.tensor
            def _(te):
                pe.start(te)
                pe_ahead.start(te)
                te.wait_ge(loaded, NLOAD)
                te.wait_ge(zeroed, NZERO)

                def turn(trip):
                    for l in (0, 1):
                        if first:
                            te.wait_ge(*vec_ahead.at("y0", trip, l))
                        else:
                            te.wait_ge(y_in[l], trip * 16 + 16)
                        te.wait_ge(*vec.at("y", trip, l, ago=1))
                        te.transpose(ps[l][:, 0, 0:T], yc[l][:], g.ident[:])
                        te.matmul(ps[l][HALF:C, 0, 0:T], yc[l][:, HALF:C], g.shift[:], start=True, stop=True
                                  ).then_inc(*pe_ahead.did("hT", l))

                def attend(trip, more):
                    for l in (0, 1):
                        te.wait_ge(*act_ahead.at("hT", trip, l))
                        for a in (0, 1):
                            mm = te.matmul(ps[l][:, 1 + a], hT[l][:], wqkv[:, a], start=True, stop=True)
                        mm.then_inc(*pe.did("qk", l))
                        te.wait_ge(*vec.at("hn1", trip, l, ago=1))
                        te.matmul(ps[l][:, 3], hT[l][:], wqkv[:, 2], start=True, stop=True).then_inc(*pe.did("v", l))
                    for l in (0, 1):
                        te.wait_ge(*pool.at("qrot", trip, l))
                        te.wait_ge(*vec.at("kn", trip, l))
                        for a in (0, 1):
                            for j in range(PAIRS):
                                mm = te.transpose(ps[l][:, a, T * j:T * j + T],
                                                  rc[l][:, a, 2 * j:2 * j + 2].rearrange("p h e -> p (h e)"), g.ident[:])
                        mm.then_inc(*pe.did("qkT", l))
                        te.wait_ge(*act.at("kT", trip, l))
                        te.wait_ge(*vec.at("kT", trip, l))
                        for j in range(PAIRS):
                            mm = te.matmul(ps[l][:, 2 + j // 2, 2 * T * (j % 2):2 * T * (j % 2) + 2 * T], qT[l][:, j],
                                           kT[l][:, j].rearrange("p a t -> p (a t)"), start=True, stop=True)
                        mm.then_inc(*pe.did("s", l))
                    for l in (0, 1):
                        te.wait_ge(*pool.at("norm", trip, l))
                        te.wait_ge(*vec.at("norm", trip, l))
                        for h in range(H):
                            mm = te.transpose(ps[l][:, h // 4, T * (h % 4):T * (h % 4) + T], prob[l][:, h], g.ident[:])
                        mm.then_inc(*pe.did("pT", l))
                    for l in (0, 1):
                        te.wait_ge(*act.at("pT", trip, l))
                        te.wait_ge(*vec.at("pT", trip, l))
                        for h in range(H):
                            rows = slice(64 * (h % 2), 64 * (h % 2) + 64)
                            mm = te.matmul(ps[l][rows, 2, T * (h // 2):T * (h // 2) + T], val[l][:, HD * h:HD * h + HD],
                                           probT[l][:, h], start=True, stop=True)
                        mm.then_inc(*pe.did("o", l))
                    for l in (0, 1):
                        te.wait_ge(*act.at("oT", trip, l))
                        for j in range(PAIRS):
                            mm = te.matmul(ps[l][:, 3, 0:C], oT[l][:, j], wo[:, j],
                                           start=(j == 0), stop=(j == PAIRS - 1))
                        mm.then_inc(*pe.did("ao", l))
                    if more:
                        turn(trip + 1)
                    for l in (0, 1):
                        te.wait_ge(*vec.at("y", trip, l))
                        te.matmul(ps[l][:, 3, C:C + HALF], g.shift[:], ynew[l][:, HALF:C], start=True, stop=True
                                  ).then_inc(*pe.did("sh", l))

                turn(0)
                with te.Fori(0, TRIPS - 1) as trip:
                    attend(trip, True)
                attend(TRIPS - 1, False)

            @block.vector
            def _(v):
                v.wait_ge(loaded, NLOAD)
                v.tensor_tensor(rot[:], rot[:], qks[:], ALU.mult).then_inc(prep, 1)
                vec.start(v)
                vec_ahead.start(v)
                v.wait_ge(prep, 1)
                one = lambda ap, trip, l: flat(ap[:, bass.ds(trip * 2 + l, 1), :])

                def measure(trip):
                    for l in ((0, 1) if first else ()):
                        v.wait_ge(y_in[l], trip * 16 + 16)
                        v.wait_ge(*vec_ahead.at("y0", trip, l, ago=1))
                        row_statistics(v, vec_ahead, trip, l, stats0[l][:], mv0[l], rstd0[l][:, 1:2], xin[l][:])

                def normalise(trip):
                    for l in ((0, 1) if first else ()):
                        v.wait_ge(*vec.at("y", trip, l, ago=1))
                        v.wait_ge(*act_ahead.at("rstd0", trip, l))
                        v.tensor_scalar(yc[l][:], xin[l][:], mv0[l][:, 0:1], rstd0[l][:, 1:2], ALU.subtract, ALU.mult
                                        ).then_inc(*vec_ahead.did("y0", l))

                def upper_keys(trip, l):
                    v.wait_ge(*pe.at("qkT", trip, l))
                    v.wait_ge(*act.at("qT", trip, l))
                    v.tensor_copy(kT[l][HD:2 * HD, :, 1], ps[l][HD:2 * HD, 1].rearrange("p (j t) -> p j t", t=T)
                                  ).then_inc(*vec.did("kT", l))

                def attend(trip, more):
                    for l in (0, 1):
                        tab = lambda trig, part: rot[:, :, trig, part].unsqueeze(2).to_broadcast(
                            [T, 2, H, part.stop - part.start])
                        lo, hi, whole = slice(0, HD // 2), slice(HD // 2, HD), slice(0, HD)
                        qk = ps[l][:, 1:3].rearrange("p a (h e) -> p a h e", e=HD)
                        v.wait_ge(*act.at("sq", trip, l))
                        v.tensor_reduce(ss[l][:, 0], sq[l][:], AX, ALU.add).then_inc(*vec.did("ss", l))
                        v.wait_ge(*vec.at("ss", trip, l))
                        v.tensor_scalar(ss[l][:, 0], ss[l][:, 0], 1e-24, None, ALU.max).then_inc(*vec.did("ssm", l))
                        v.tensor_tensor(rc[l][:], qk, tab(0, whole), ALU.mult).then_inc(*vec.did("cos", l))
                        v.tensor_tensor(rs[l][:, :, :, lo], qk[:, :, :, hi], tab(1, lo), ALU.mult
                                        ).then_inc(*vec.did("sin0", l))
                        v.tensor_tensor(rs[l][:, :, :, hi], qk[:, :, :, lo], tab(1, hi), ALU.mult
                                        ).then_inc(*vec.did("sin1", l))
                        if l == 1:
                            upper_keys(trip, 0)
                        v.wait_ge(*vec.at("sin1", trip, l))
                        v.tensor_tensor(rc[l][:, 1], rc[l][:, 1], rs[l][:, 1], ALU.add).then_inc(*vec.did("krot", l))
                        v.wait_ge(*vec.at("krot", trip, l))
                        v.wait_ge(*act.at("rn", trip, l))
                        v.tensor_tensor(rc[l][:, 1], rc[l][:, 1],
                                        ss[l][:, 2, H:2 * H].unsqueeze(2).to_broadcast([T, H, HD]), ALU.mult
                                        ).then_inc(*vec.did("kn", l))
                    upper_keys(trip, 1)
                    for l in (0, 1):
                        v.wait_ge(*pe.at("s", trip, l))
                        for h in range(H):
                            v.scalar_tensor_tensor(out=prob[l][:, h], in0=ps[l][:, 2 + h // 4, T * (h % 4):T * (h % 4) + T],
                                                   scalar=ss[l][:, 2, h:h + 1], in1=g.local[:], op0=ALU.mult,
                                                   op1=ALU.add).then_inc(*vec.did(f"s{h}", l))
                        v.wait_ge(*vec.at(f"s{H - 1}", trip, l))
                        v.tensor_reduce(mx[l][:], prob[l][:], AX, ALU.max, negate=True).then_inc(*vec.did("mx", l))
                    for l in (0, 1):
                        v.wait_ge(*act.at(f"exp{H - 1}", trip, l))
                        v.reciprocal(sm[l][:, 1], sm[l][:, 0]).then_inc(*vec.did("rsum", l))
                        v.wait_ge(*vec.at("rsum", trip, l))
                        v.tensor_tensor(prob[l][:, 0:PH], prob[l][:, 0:PH],
                                        sm[l][:, 1, 0:PH].unsqueeze(2).to_broadcast([T, PH, T]), ALU.mult
                                        ).then_inc(*vec.did("norm", l))
                    for l in (0, 1):
                        v.wait_ge(*pe.at("pT", trip, l))
                        v.tensor_copy(probT[l][:, 4:8].rearrange("p h t -> p (h t)"), ps[l][:, 1]
                                      ).then_inc(*vec.did("pT", l))
                    if more:
                        measure(trip + 1)
                    for l in (0, 1):
                        y = yc[l][:] if first else one(g.y, trip, l)
                        v.wait_ge(*pe.at("ao", trip, l))
                        v.tensor_tensor(ynew[l][:], y, ps[l][:, 3, 0:C], ALU.add).then_inc(*vec.did("ynew", l))
                        v.wait_ge(*vec.at("ynew", trip, l))
                        v.tensor_tensor(one(g.y, trip, l), y, ps[l][:, 3, 0:C], ALU.add).then_inc(*vec.did("y", l))
                    if more:
                        normalise(trip + 1)
                    for l in (0, 1):
                        v.wait_ge(*vec.at("ynew", trip, l))
                        v.bn_stats(stats[l][:, 0:6], ynew[l][:, 0:HALF]).then_inc(*vec.did("st1", l))
                        v.wait_ge(*pe.at("sh", trip, l))
                        v.bn_stats(stats[l][:, 6:12], ps[l][:, 3, C:C + HALF]).then_inc(*vec.did("st2", l))
                        v.wait_ge(*vec.at("st2", trip, l))
                        v.memset(rstd[l][:, 1:2], 0.0)
                        v.bn_aggr(mv[l][:], stats[l][:]).then_inc(*vec.did("mv2", l))
                    for l in (0, 1):
                        v.wait_ge(*act.at("rstd", trip, l))
                        v.tensor_scalar(one(g.hn[:, :, 0:HALF], trip, l), ynew[l][:, 0:HALF], mv[l][:, 0:1], rstd[l][:, 1:2],
                                        ALU.subtract, ALU.mult).then_inc(*vec.did("hn0", l))
                        v.tensor_scalar(one(g.hn[:, :, HALF:C], trip, l), ps[l][:, 3, C:C + HALF], mv[l][:, 0:1],
                                        rstd[l][:, 1:2], ALU.subtract, ALU.mult).then_inc(*vec.did("hn1", l))

                measure(0)
                normalise(0)
                with v.Fori(0, TRIPS - 1) as trip:
                    attend(trip, True)
                attend(TRIPS - 1, False)


def gated_mlp(nc, g, layer):
    HID = g.d["L0_ffn_w2"].shape[1]
    CH = -(-HID // 128)
    M = [min(128, HID - 128 * c) for c in range(CH)]
    N = 2 * T
    TRIPS = g.NB // 4
    d = g.d
    last = layer == 1
    with ExitStack() as stack:
        m = Memory(nc, stack, f"m{layer}")
        w1 = m.sb("w1", [C, 2, HID])
        b1 = m.sb("b1", [128, 2, CH])
        w2 = m.sb("w2", [128, CH, C])
        b2 = m.sb("b2", [T, C])
        lng, lnb = m.sb("lng", [C, 1]), m.sb("lnb", [C, 1])
        hin, ysum = (both(m, n, [T, 2, C]) for n in ("hin", "ysum"))
        hT = both(m, "hT", [C, N])
        gl, u = both(m, "gl", [128, CH, N]), both(m, "u", [128, CH, N])
        ps = [m.ps(f"ps{l}", [128, 4, 512]) for l in (0, 1)]
        loaded, zeroed = m.sem("loaded"), m.sem("zeroed")
        h_in = [m.sem(f"h_in{l}") for l in (0, 1)]
        vec = Steps(m.lanes("vec_done"), ["hT", " ".join(f"u{c}" for c in range(CH)), "yb yx y" if last else "yb y"])
        act = Steps(m.lanes("act_done"), [" ".join(f"g{c}" for c in range(CH))])
        pe = Steps(m.lanes("pe_done"), ["hT", "ag", "o"])
        NZERO, NLOAD = 5, 16 * (6 + 2 * CH)

        with nc.Block() as block:
            @block.sync
            def _(sp):
                sp.wait_ge(zeroed, NZERO)
                sp.dma_start(w1[:], d["L0_ffn_w1"][layer].rearrange("c (a n) -> c a n", a=2)).then_inc(loaded, 16)
                sp.dma_start(b2[:], row_bc(d["L0_ffn_b2"][layer])).then_inc(loaded, 16)
                sp.dma_start(lng[:], d["L0_ffn_ln_g"][layer].unsqueeze(1)).then_inc(loaded, 16)
                sp.dma_start(lnb[:], d["L0_ffn_ln_b"][layer].unsqueeze(1)).then_inc(loaded, 16)
                whole = (CH - 1) * 128
                sp.dma_start(w2[:, 0:CH - 1], d["L0_ffn_w2"][layer, 0:whole].rearrange("(c p) n -> p c n", p=128)
                             ).then_inc(loaded, 16)
                sp.dma_start(w2[0:M[-1], CH - 1], d["L0_ffn_w2"][layer, whole:HID]).then_inc(loaded, 16)
                for c in range(CH):
                    for a in (0, 1):
                        row = d["L0_ffn_b1"][layer, HID * a + 128 * c:HID * a + 128 * c + M[c]]
                        sp.dma_start(b1[0:M[c], a, c:c + 1], row.unsqueeze(1)).then_inc(loaded, 16)
                with sp.Fori(0, TRIPS) as trip:
                    for l in (0, 1):
                        b = sp.snap(trip * 4 + 2 * l)
                        src = g.hn[:, bass.ds(b, 2), :]
                        sp.wait_ge(*pe.at("hT", trip, l, ago=1))
                        sp.dma_start(hin[l][:], src).then_inc(h_in[l], 16)

            @block.gpsimd
            def _(gp):
                gp.memset(w2[:], 0.0).then_inc(zeroed, 1)
                for l in (0, 1):
                    gp.memset(u[l][:, CH - 1], 0.0).then_inc(zeroed, 1)
                    gp.memset(gl[l][:, CH - 1], 0.0).then_inc(zeroed, 1)

            @block.scalar
            def _(sc):
                act.start(sc)
                sc.wait_ge(zeroed, NZERO)
                sc.wait_ge(loaded, NLOAD)
                with sc.Fori(0, TRIPS) as trip:
                    for l in (0, 1):
                        sc.wait_ge(*pe.at("ag", trip, l))
                        for c in range(CH):
                            sc.activation(gl[l][0:M[c], c], ps[l][0:M[c], c, N:2 * N], ACT.Gelu, bias=b1[0:M[c], 1, c:c + 1]
                                          ).then_inc(*act.did(f"g{c}", l))

            @block.tensor
            def _(te):
                pe.start(te)
                te.wait_ge(loaded, NLOAD)
                te.wait_ge(zeroed, NZERO)
                with te.Fori(0, TRIPS) as trip:
                    for l in (0, 1):
                        te.wait_ge(h_in[l], trip * 16 + 16)
                        te.wait_ge(*vec.at("y", trip, l, ago=1))
                        for i in (0, 1):
                            mm = te.transpose(ps[l][:, 3, T * i:T * i + T], hin[l][:, i], g.ident[:])
                        mm.then_inc(*pe.did("hT", l))
                    for l in (0, 1):
                        te.wait_ge(*vec.at("hT", trip, l))
                        for c in range(CH):
                            for a in (0, 1):
                                mm = te.matmul(ps[l][0:M[c], c, N * a:N * a + N], w1[:, a, 128 * c:128 * c + M[c]],
                                               hT[l][:], start=True, stop=True)
                        mm.then_inc(*pe.did("ag", l))
                    for l in (0, 1):
                        te.wait_ge(*vec.at(f"u{CH - 1}", trip, l))
                        for i in (0, 1):
                            for c in range(CH):
                                mm = te.matmul(ps[l][:, 3, N + T * i:N + T * i + T], u[l][:, c, T * i:T * i + T], w2[:, c],
                                               start=(c == 0), stop=(c == CH - 1))
                        mm.then_inc(*pe.did("o", l))

            @block.vector
            def _(v):
                vec.start(v)
                v.wait_ge(loaded, NLOAD)
                v.wait_ge(zeroed, NZERO)
                with v.Fori(0, TRIPS) as trip:
                    for l in (0, 1):
                        v.wait_ge(*pe.at("hT", trip, l))
                        v.tensor_scalar(hT[l][:], ps[l][:, 3, 0:N], lng[:, 0:1], lnb[:, 0:1], ALU.mult, ALU.add
                                        ).then_inc(*vec.did("hT", l))
                    for l in (0, 1):
                        for c in range(CH):
                            v.wait_ge(*act.at(f"g{c}", trip, l))
                            v.scalar_tensor_tensor(out=u[l][0:M[c], c], in0=ps[l][0:M[c], c, 0:N],
                                                   scalar=b1[0:M[c], 0, c:c + 1], in1=gl[l][0:M[c], c],
                                                   op0=ALU.add, op1=ALU.mult).then_inc(*vec.did(f"u{c}", l))
                    for l in (0, 1):
                        v.wait_ge(*pe.at("o", trip, l))
                        two = lambda ap: ap[:, bass.ds(trip * 4 + 2 * l, 2), :]
                        v.tensor_tensor(ysum[l][:], ps[l][:, 3, N:2 * N].rearrange("p (i c) -> p i c", c=C),
                                        b2[:].unsqueeze(1).to_broadcast([T, 2, C]), ALU.add).then_inc(*vec.did("yb", l))
                        v.wait_ge(*vec.at("yb", trip, l))
                        if last:
                            v.tensor_tensor(ysum[l][:], ysum[l][:], two(g.y), ALU.add).then_inc(*vec.did("yx", l))
                            v.wait_ge(*vec.at("yx", trip, l))
                        residual = g.x if last else g.y
                        v.tensor_tensor(two(residual), two(residual), ysum[l][:], ALU.add).then_inc(*vec.did("y", l))


def local_transformer(nc, g):
    with ExitStack() as stack:
        m = Memory(nc, stack, "lt")
        g.y, g.hn = m.sb("y", [T, g.NB, C]), m.sb("hn", [T, g.NB, C])
        for layer in (0, 1):
            local_attention(nc, g, layer)
            gated_mlp(nc, g, layer)


def mamba(nc, g):
    DIRS, TAPS, NH, HD, DS = 2, 4, 4, 64, 128
    DI = NH * HD
    PAIRS = DI // 128
    HEADS = DIRS * NH
    PAD = TAPS - 1
    TERMS = 7
    TRIPS = g.NB // 2
    d = g.d
    names = ("L1_attn_fwd_", "L1_attn_bwd_")
    with ExitStack() as stack:
        m = Memory(nc, stack, "mb")
        wx = m.sb("wx", [C, DIRS, TAPS, DI])
        wbc = m.sb("wbc", [C, DIRS, TAPS, 2, DS])
        wz = m.sb("wz", [C, DIRS, PAIRS, 128])
        wdt = m.sb("wdt", [C, HEADS])
        wout = m.sb("wout", [128, DIRS, PAIRS, C])
        cbx, cbbc = m.sb("cbx", [T, DIRS, DI]), m.sb("cbbc", [DS, DIRS, 2])
        dtb, nega = m.sb("dtb", [T, HEADS]), m.sb("nega", [T, HEADS])
        dcol, ddiag = m.sb("dcol", [T, HEADS]), m.sb("ddiag", [T, HEADS, T])
        beyond, upto = m.sb("beyond", [T, DIRS, T]), m.sb("upto", [T, DIRS, T])
        projb = m.sb("projb", [T, C])
        eps = m.sb("eps", [128, 1])

        with ExitStack() as once:
            mo = Memory(nc, once, "mw")
            win = mo.sb("win", [128, DIRS, 6, C])
            wind = mo.sb("wind", [NH, DIRS, C])
            cw = mo.sb("cw", [128, DIRS, 4, TAPS])
            tapped = mo.sb("tapped", [128, DIRS, 4, TAPS, C])
            nw, ow = mo.sb("nw", [C, 1]), mo.sb("ow", [128, DIRS, PAIRS])
            wo, proj, projT = mo.sb("wo", [C, DIRS, DI]), mo.sb("proj", [C, DIRS, C]), mo.sb("projT", [C, DIRS, C])
            pw = mo.ps("pw", [128, 8, 512])
            loaded, made, masks = mo.sem("loaded"), mo.sem("made"), mo.sem("masks")
            tap, turned, kept = mo.sem("tap"), mo.sem("turned"), mo.sem("kept")
            NL = 16 * (2 + DIRS + DIRS * 12)

            with nc.Block() as block:
                @block.sync
                def _(sp):
                    sp.dma_start(nw[:], d["L1_attn_norm_weight"].unsqueeze(1)).then_inc(loaded, 16)
                    sp.dma_start(projb[:], row_bc(d["L1_attn_proj_b"])).then_inc(loaded, 16)
                    for k in range(DIRS):
                        sp.dma_start(proj[:, k], d["L1_attn_proj_W"][:, C * k:C * k + C]).then_inc(loaded, 16)
                    for k, n in enumerate(names):
                        sp.dma_start(win[:, k], d[n + "W_in"][0:768].rearrange("(a p) c -> p a c", p=128)
                                     ).then_inc(loaded, 16)
                        sp.dma_start(wind[:, k], d[n + "W_in"][768:768 + NH]).then_inc(loaded, 16)
                        sp.dma_start(cw[:, k], d[n + "conv_w"].rearrange("(a p) j -> p a j", p=128)).then_inc(loaded, 16)
                        sp.dma_start(cbx[:, k], row_bc(d[n + "conv_b"][0:DI])).then_inc(loaded, 16)
                        for a in (0, 1):
                            sp.dma_start(cbbc[:, k, a:a + 1],
                                         d[n + "conv_b"][DI + DS * a:DI + DS * a + DS].unsqueeze(1)).then_inc(loaded, 16)
                            sp.dma_start(ow[:, k, a:a + 1], d[n + "norm_w"][128 * a:128 * a + 128].unsqueeze(1)
                                         ).then_inc(loaded, 16)
                        heads = slice(NH * k, NH * k + NH)
                        sp.dma_start(dtb[:, heads], row_bc(d[n + "dt_bias"])).then_inc(loaded, 16)
                        sp.dma_start(nega[:, heads], row_bc(d[n + "A_log"])).then_inc(loaded, 16)
                        sp.dma_start(dcol[:, heads], row_bc(d[n + "D"])).then_inc(loaded, 16)
                        sp.dma_start(wo[:, k], d[n + "W_out"]).then_inc(loaded, 16)

                @block.gpsimd
                def _(gp):
                    gp.memset(beyond[:], 1.0).then_inc(masks, 1)
                    gp.memset(upto[:], 1.0).then_inc(masks, 1)
                    gp.memset(eps[:], LN_EPS).then_inc(masks, 1)
                    gp.wait_ge(masks, 3)
                    for k, sign in enumerate((1, -1)):
                        gp.affine_select(out=beyond[:, k], in_=beyond[:, k], compare_op=ALU.is_gt, fill=0.0, base=0,
                                         pattern=[[-sign, T]], channel_multiplier=sign).then_inc(masks, 1)
                        gp.affine_select(out=upto[:, k], in_=upto[:, k], compare_op=ALU.is_ge, fill=0.0, base=0,
                                         pattern=[[sign, T]], channel_multiplier=-sign).then_inc(masks, 1)

                @block.scalar
                def _(sc):
                    sc.preload_act_table_set("natural_log_exp_and_others")
                    sc.wait_ge(loaded, NL)
                    sc.activation(nega[:], nega[:], ACT.Exp).then_inc(made, 1)
                    sc.wait_ge(made, 1)
                    sc.mul(nega[:], nega[:], -1.0).then_inc(made, 1)

                @block.vector
                def _(v):
                    v.wait_ge(loaded, NL)
                    for k in range(DIRS):
                        for a in range(4):
                            for j in range(TAPS):
                                v.tensor_scalar(tapped[:, k, a, j], win[:, k, 2 + a], cw[:, k, a, j:j + 1], None,
                                                ALU.mult).then_inc(tap, 1)
                    for h in range(HEADS):
                        v.tensor_scalar(ddiag[:, h], g.ident[:], dcol[:, h:h + 1], None, ALU.mult).then_inc(kept, 1)
                    bank = lambda b: pw[:, b].rearrange("p (a c) -> p a c", c=128)
                    v.wait_ge(turned, 1)
                    for k in range(DIRS):
                        for j in range(TAPS):
                            src = bank(4 * k + j)
                            v.tensor_scalar(wx[:, k, j].rearrange("p (a c) -> p a c", c=128), src[:, 0:2], nw[:, 0:1],
                                            None, ALU.mult).then_inc(kept, 1)
                            v.tensor_scalar(wbc[:, k, j], src[:, 2:4], nw[:, 0:1], None, ALU.mult).then_inc(kept, 1)
                    v.wait_ge(turned, 2)
                    v.tensor_scalar(wz[:].rearrange("p k a c -> p (k a) c"), bank(0), nw[:, 0:1], None, ALU.mult
                                    ).then_inc(kept, 1)
                    v.tensor_scalar(wdt[:], pw[:, 1, 0:HEADS], nw[:, 0:1], None, ALU.mult).then_inc(kept, 1)
                    v.tensor_copy(projT[:], bank(2)[:, 0:2]).then_inc(kept, 1)
                    v.wait_ge(turned, 3)
                    for k in range(DIRS):
                        for a in range(PAIRS):
                            v.tensor_scalar(wout[:, k, a], bank(3)[:, 2 * k + a], ow[:, k, a:a + 1], None, ALU.mult
                                            ).then_inc(kept, 1)

                @block.tensor
                def _(te):
                    KEPT = HEADS + 2 * DIRS * TAPS
                    te.wait_ge(tap, DIRS * 4 * TAPS)
                    for k in range(DIRS):
                        for j in range(TAPS):
                            for a in range(4):
                                mm = te.transpose(pw[:, 4 * k + j, 128 * a:128 * a + 128], tapped[:, k, a, j], g.ident[:])
                    mm.then_inc(turned, 1)
                    te.wait_ge(kept, KEPT)
                    for k in range(DIRS):
                        for a in range(PAIRS):
                            te.transpose(pw[:, 0, 128 * (2 * k + a):128 * (2 * k + a) + 128], win[:, k, a], g.ident[:])
                        te.transpose(pw[:, 1, NH * k:NH * k + NH], wind[:, k], g.ident[0:NH, 0:NH])
                        mm = te.transpose(pw[:, 2, C * k:C * k + C], proj[:, k], g.ident[:])
                    mm.then_inc(turned, 1)
                    te.wait_ge(kept, KEPT + 3)
                    for k in range(DIRS):
                        for a in range(PAIRS):
                            mm = te.matmul(pw[:, 3, 128 * (2 * k + a):128 * (2 * k + a) + 128],
                                           wo[:, k, 128 * a:128 * a + 128], projT[:, k], start=True, stop=True)
                    mm.then_inc(turned, 1)

        xin, xr, r, xn = (both(m, n, [T, C]) for n in ("xin", "xr", "r", "xn"))
        stats, mv, rstd = both(m, "stats", [T, 6]), both(m, "mv", [T, 2]), both(m, "rstd", [T, 2])
        rms = both(m, "rms", [T, 3])
        xT = both(m, "xT", [C, PAD + T + PAD])
        dts = both(m, "dts", [T, 8, HEADS])
        dt, dta = both(m, "dt", [T, HEADS]), both(m, "dta", [T, HEADS])
        xs = both(m, "xs", [T, DIRS, DI])
        bc = both(m, "bc", [DS, DIRS, 2, T])
        zs = both(m, "zs", [128, DIRS * PAIRS, T])
        steps_a = both(m, "steps_a", [T, HEADS, T])
        gm, km = both(m, "gm", [T, DIRS, T]), both(m, "km", [T, HEADS, T])
        decay = both(m, "decay", [T, HEADS, T])
        u, usq = both(m, "u", [128, DIRS * PAIRS, T]), both(m, "usq", [128, DIRS * PAIRS, T])
        scale = both(m, "scale", [T, 2, DIRS])
        acc = both(m, "acc", [T, C])
        ps = [m.ps(f"ps{l}", [128, 4, 512]) for l in (0, 1)]
        zeroed = m.sem("zeroed")
        x_in = [m.sem(f"x_in{l}") for l in (0, 1)]
        series = " ".join(f"p{n}" for n in range(TERMS, 0, -1))
        vec = Steps(m.lanes("vec_done"), [
            "stats mv", "q", "r xn", "xb v av", f"den rden z z2 {series} pz relu dt dta",
            " ".join(f"a{h}" for h in range(HEADS)), "gm " + " ".join(f"k{h}" for h in range(HEADS)),
            "m", "u", "acc x"])
        act = Steps(m.lanes("act_done"), ["lnv rstd", "lnq rms", "xT", "eu", "sx sb0 sb1 sb2 sb3 sz", "decay", "usq",
                                        "lns rs"])
        pe = Steps(m.lanes("pe_done"), ["xT", "dt x bc z", "g seg", "y", "out"])
        pool = Steps(m.lanes("pool_done"), ["xp xr"])

        with nc.Block() as block:
            @block.sync
            def _(sp):
                with sp.Fori(0, TRIPS) as trip:
                    for l in (0, 1):
                        src = flat(g.x[:, bass.ds(sp.snap(trip * 2 + l), 1), :])
                        sp.wait_ge(*vec.at("acc", trip, l, ago=1))
                        sp.dma_start(xin[l][:], src).then_inc(x_in[l], 16)

            @block.gpsimd
            def _(gp):
                for l in (0, 1):
                    gp.memset(xT[l][:], 0.0).then_inc(zeroed, 1)
                pool.start(gp)
                with gp.Fori(0, TRIPS) as trip:
                    for l in (0, 1):
                        gp.wait_ge(*vec.at("r", trip, l))
                        gp.tensor_tensor(xr[l][:], xin[l][:], projb[:], ALU.add).then_inc(*pool.did("xp", l))
                        gp.wait_ge(*pool.at("xp", trip, l))
                        gp.tensor_tensor(xr[l][:], xr[l][:], r[l][:], ALU.add).then_inc(*pool.did("xr", l))

            @block.scalar
            def _(sc):
                act.start(sc)
                sc.wait_ge(zeroed, 2)
                two = lambda ap: ap.rearrange("p a c -> p (a c)")
                with sc.Fori(0, TRIPS) as trip:
                    for l in (0, 1):
                        sc.wait_ge(*vec.at("mv", trip, l))
                        rsqrt_of_variance(sc, act, trip, l, rstd[l], mv[l], eps)
                    for l in (0, 1):
                        sc.wait_ge(*vec.at("q", trip, l))
                        sc.activation(rms[l][:, 1:2], rms[l][:, 0:1], ACT.Ln, bias=eps[:]).then_inc(*act.did("lnq", l))
                        sc.wait_ge(*act.at("lnq", trip, l))
                        sc.activation(rms[l][:, 2:3], rms[l][:, 1:2], ACT.Exp, scale=-0.5).then_inc(*act.did("rms", l))
                    for l in (0, 1):
                        sc.wait_ge(*pe.at("xT", trip, l))
                        sc.activation(xT[l][:, PAD:PAD + T], ps[l][:, 3, 0:T], ACT.Copy).then_inc(*act.did("xT", l))
                    for l in (0, 1):
                        sc.wait_ge(*vec.at("av", trip, l))
                        sc.activation(dts[l][:, 2], dts[l][:, 1], ACT.Exp).then_inc(*act.did("eu", l))
                    sc.preload_act_table_set("silu_and_others")
                    for l in (0, 1):
                        sc.wait_ge(*vec.at("xb", trip, l))
                        sc.activation(two(xs[l][:]), two(xs[l][:]), ACT.Silu).then_inc(*act.did("sx", l))
                        sc.wait_ge(*pe.at("bc", trip, l))
                        for i in range(4):
                            k, a = i // 2, i % 2
                            sc.activation(bc[l][:, k, a], ps[l][:, 1, T * i:T * i + T], ACT.Silu,
                                          bias=cbbc[:, k, a:a + 1]).then_inc(*act.did(f"sb{i}", l))
                        sc.wait_ge(*pe.at("z", trip, l))
                        sc.activation(two(zs[l][:]), ps[l][:, 2], ACT.Silu).then_inc(*act.did("sz", l))
                    sc.preload_act_table_set("natural_log_exp_and_others")
                    for l in (0, 1):
                        sc.wait_ge(*pe.at("seg", trip, l))
                        sc.activation(two(decay[l][:]), two(ps[l][:, 0:2]), ACT.Exp).then_inc(*act.did("decay", l))
                    for l in (0, 1):
                        sc.wait_ge(*vec.at("u", trip, l))
                        sc.activation(two(usq[l][:]), two(u[l][:]), ACT.Square).then_inc(*act.did("usq", l))
                    for l in (0, 1):
                        sc.wait_ge(*pe.at("out", trip, l))
                        sc.activation(scale[l][:, 0], ps[l][:, 3, 0:2 * C:C], ACT.Ln, bias=eps[:], scale=1.0 / DI
                                      ).then_inc(*act.did("lns", l))
                        sc.wait_ge(*act.at("lns", trip, l))
                        sc.activation(scale[l][:, 1], scale[l][:, 0], ACT.Exp, scale=-0.5).then_inc(*act.did("rs", l))

            @block.tensor
            def _(te):
                pe.start(te)
                te.wait_ge(zeroed, 2)
                starts = [[j for j in range(TAPS)], [2 * PAD - j for j in range(TAPS)]]
                with te.Fori(0, TRIPS) as trip:
                    for l in (0, 1):
                        te.wait_ge(*vec.at("xn", trip, l))
                        te.transpose(ps[l][:, 3, 0:T], xn[l][:], g.ident[:]).then_inc(*pe.did("xT", l))
                    for l in (0, 1):
                        here = xT[l][:, PAD:PAD + T]
                        te.wait_ge(*act.at("xT", trip, l))
                        te.matmul(ps[l][:, 3, T:T + HEADS], here, wdt[:], start=True, stop=True).then_inc(*pe.did("dt", l))
                        for k in range(DIRS):
                            for j in range(TAPS):
                                s = starts[k][j]
                                mm = te.matmul(ps[l][:, 0, DI * k:DI * k + DI], xT[l][:, s:s + T], wx[:, k, j],
                                               start=(j == 0), stop=(j == TAPS - 1))
                        mm.then_inc(*pe.did("x", l))
                        for i in range(4):
                            k, a = i // 2, i % 2
                            for j in range(TAPS):
                                s = starts[k][j]
                                mm = te.matmul(ps[l][:, 1, T * i:T * i + T], wbc[:, k, j, a], xT[l][:, s:s + T],
                                               start=(j == 0), stop=(j == TAPS - 1))
                        mm.then_inc(*pe.did("bc", l))
                        for i in range(4):
                            mm = te.matmul(ps[l][:, 2, T * i:T * i + T], wz[:, i // 2, i % 2], here,
                                           start=True, stop=True)
                        mm.then_inc(*pe.did("z", l))
                    for l in (0, 1):
                        te.wait_ge(*act.at("sb3", trip, l))
                        for k in range(DIRS):
                            mm = te.matmul(ps[l][:, 3, 256 + T * k:256 + T * k + T], bc[l][:, k, 0], bc[l][:, k, 1],
                                           start=True, stop=True)
                        mm.then_inc(*pe.did("g", l))
                        te.wait_ge(*vec.at(f"a{HEADS - 1}", trip, l))
                        for h in range(HEADS):
                            mm = te.matmul(ps[l][:, h // NH, T * (h % NH):T * (h % NH) + T], steps_a[l][:, h],
                                           upto[:, h // NH], start=True, stop=True)
                        mm.then_inc(*pe.did("seg", l))
                    for l in (0, 1):
                        te.wait_ge(*act.at("sz", trip, l))
                        te.wait_ge(*vec.at("m", trip, l))
                        for h in range(HEADS):
                            rows = slice(64 * (h % 2), 64 * (h % 2) + 64)
                            mm = te.matmul(ps[l][rows, 2, T * (h // 2):T * (h // 2) + T],
                                           xs[l][:, h // NH, HD * (h % NH):HD * (h % NH) + HD], decay[l][:, h],
                                           start=True, stop=True)
                        mm.then_inc(*pe.did("y", l))
                    for l in (0, 1):
                        te.wait_ge(*act.at("usq", trip, l))
                        for k in range(DIRS):
                            for a in range(PAIRS):
                                te.matmul(ps[l][:, 3, C * k:C * k + C], usq[l][:, 2 * k + a], g.ones[:],
                                          start=(a == 0), stop=(a == PAIRS - 1))
                        for k in range(DIRS):
                            for a in range(PAIRS):
                                mm = te.matmul(ps[l][:, 3, C * (2 + k):C * (2 + k) + C], u[l][:, 2 * k + a],
                                               wout[:, k, a], start=(a == 0), stop=(a == PAIRS - 1))
                        mm.then_inc(*pe.did("out", l))

            @block.vector
            def _(v):
                vec.start(v)
                v.wait_ge(zeroed, 2)
                coefficient = lambda n: 1.0 / (2 * n + 1)
                two = lambda ap: ap.rearrange("p a c -> p (a c)")
                with v.Fori(0, TRIPS) as trip:
                    for l in (0, 1):
                        v.wait_ge(x_in[l], trip * 16 + 16)
                        v.wait_ge(*vec.at("x", trip, l, ago=1))
                        row_statistics(v, vec, trip, l, stats[l][:], mv[l], rstd[l][:, 1:2], xin[l][:])
                    for l in (0, 1):
                        v.wait_ge(*act.at("rstd", trip, l))
                        v.scalar_tensor_tensor(out=rms[l][:, 0:1], in0=rstd[l][:, 1:2], scalar=rstd[l][:, 1:2],
                                               in1=mv[l][:, 1:2], op0=ALU.mult, op1=ALU.mult).then_inc(*vec.did("q", l))
                    for l in (0, 1):
                        v.tensor_scalar(r[l][:], xin[l][:], mv[l][:, 0:1], rstd[l][:, 1:2], ALU.subtract, ALU.mult
                                        ).then_inc(*vec.did("r", l))
                        v.wait_ge(*vec.at("r", trip, l))
                        v.wait_ge(*act.at("rms", trip, l))
                        v.tensor_scalar(xn[l][:], r[l][:], rms[l][:, 2:3], None, ALU.mult).then_inc(*vec.did("xn", l))
                    for l in (0, 1):
                        v.wait_ge(*pe.at("x", trip, l))
                        v.tensor_tensor(two(xs[l][:]), ps[l][:, 0], two(cbx[:]), ALU.add).then_inc(*vec.did("xb", l))
                        v.tensor_tensor(dts[l][:, 0], ps[l][:, 3, T:T + HEADS], dtb[:], ALU.add
                                        ).then_inc(*vec.did("v", l))
                        v.wait_ge(*vec.at("v", trip, l))
                        v.scalar_tensor_tensor(out=dts[l][:, 1], in0=dts[l][:, 0], scalar=-1.0, in1=dts[l][:, 0],
                                               op0=ALU.mult, op1=ALU.min).then_inc(*vec.did("av", l))
                    for l in (0, 1):
                        row = lambda n: dts[l][:, n]
                        v.wait_ge(*act.at("eu", trip, l))
                        v.tensor_scalar(row(3), row(2), 2.0, None, ALU.add).then_inc(*vec.did("den", l))
                        v.wait_ge(*vec.at("den", trip, l))
                        v.reciprocal(row(4), row(3)).then_inc(*vec.did("rden", l))
                        v.wait_ge(*vec.at("rden", trip, l))
                        v.tensor_tensor(row(5), row(2), row(4), ALU.mult).then_inc(*vec.did("z", l))
                        v.wait_ge(*vec.at("z", trip, l))
                        v.tensor_tensor(row(6), row(5), row(5), ALU.mult).then_inc(*vec.did("z2", l))
                        v.wait_ge(*vec.at("z2", trip, l))
                        v.tensor_scalar(row(7), row(6), coefficient(TERMS), None, ALU.mult
                                        ).then_inc(*vec.did(f"p{TERMS}", l))
                        for n in range(TERMS - 1, 0, -1):
                            v.wait_ge(*vec.at(f"p{n + 1}", trip, l))
                            v.scalar_tensor_tensor(out=row(7), in0=row(7), scalar=coefficient(n), in1=row(6),
                                                   op0=ALU.add, op1=ALU.mult).then_inc(*vec.did(f"p{n}", l))
                        v.wait_ge(*vec.at("p1", trip, l))
                        v.scalar_tensor_tensor(out=row(7), in0=row(7), scalar=1.0, in1=row(5), op0=ALU.add,
                                               op1=ALU.mult).then_inc(*vec.did("pz", l))
                        v.tensor_scalar(row(3), row(0), 0.0, None, ALU.max).then_inc(*vec.did("relu", l))
                        v.wait_ge(*vec.at("relu", trip, l))
                        v.scalar_tensor_tensor(out=dt[l][:], in0=row(7), scalar=2.0, in1=row(3), op0=ALU.mult,
                                               op1=ALU.add).then_inc(*vec.did("dt", l))
                        v.wait_ge(*vec.at("dt", trip, l))
                        v.tensor_tensor(dta[l][:], dt[l][:], nega[:], ALU.mult).then_inc(*vec.did("dta", l))
                    for l in (0, 1):
                        v.wait_ge(*vec.at("dta", trip, l))
                        for h in range(HEADS):
                            v.tensor_scalar(steps_a[l][:, h], beyond[:, h // NH], dta[l][:, h:h + 1], None, ALU.mult
                                            ).then_inc(*vec.did(f"a{h}", l))
                    for l in (0, 1):
                        v.wait_ge(*pe.at("g", trip, l))
                        v.tensor_tensor(gm[l][:], ps[l][:, 3, 256:512].rearrange("p (k t) -> p k t", t=T), upto[:],
                                        ALU.mult).then_inc(*vec.did("gm", l))
                        v.wait_ge(*vec.at("gm", trip, l))
                        for h in range(HEADS):
                            v.scalar_tensor_tensor(out=km[l][:, h], in0=gm[l][:, h // NH], scalar=dt[l][:, h:h + 1],
                                                   in1=ddiag[:, h], op0=ALU.mult, op1=ALU.add
                                                   ).then_inc(*vec.did(f"k{h}", l))
                    for l in (0, 1):
                        v.wait_ge(*vec.at(f"k{HEADS - 1}", trip, l))
                        v.wait_ge(*act.at("decay", trip, l))
                        v.tensor_tensor(two(decay[l][:]), two(decay[l][:]), two(km[l][:]), ALU.mult
                                        ).then_inc(*vec.did("m", l))
                    for l in (0, 1):
                        v.wait_ge(*pe.at("y", trip, l))
                        v.tensor_tensor(two(u[l][:]), ps[l][:, 2], two(zs[l][:]), ALU.mult).then_inc(*vec.did("u", l))
                    for l in (0, 1):
                        v.wait_ge(*pool.at("xr", trip, l))
                        v.wait_ge(*act.at("rs", trip, l))
                        v.scalar_tensor_tensor(out=acc[l][:], in0=ps[l][:, 3, 2 * C:3 * C], scalar=scale[l][:, 1, 0:1],
                                               in1=xr[l][:], op0=ALU.mult, op1=ALU.add).then_inc(*vec.did("acc", l))
                        v.wait_ge(*vec.at("acc", trip, l))
                        v.scalar_tensor_tensor(out=flat(g.x[:, bass.ds(trip * 2 + l, 1), :]),
                                               in0=ps[l][:, 3, 3 * C:4 * C], scalar=scale[l][:, 1, 1:2],
                                               in1=acc[l][:], op0=ALU.mult, op1=ALU.add).then_inc(*vec.did("x", l))


def context_attention(nc, g):
    H, HD, CD, S = 16, 8, g.d["ctx_512"].shape[2], g.d["ctx_512"].shape[1]
    TRIPS = g.NB // 2
    SCALE = float(HD) ** -0.5
    d = g.d
    with ExitStack() as stack:
        m = Memory(nc, stack, "xa")
        wq, wk, wv, wo = m.sb("wq", [C, C]), m.sb("wk", [CD, C]), m.sb("wv", [CD, C]), m.sb("wo", [C, C])
        bq, bk = m.sb("bq", [C, 1]), m.sb("bk", [C, 1])
        bv, bo = m.sb("bv", [T, C]), m.sb("bo", [T, C])
        hmask = m.sb("hmask", [C, H])
        eps = m.sb("eps", [128, 1])
        xin, xb, xn = (both(m, n, [T, C]) for n in ("xin", "xb", "xn"))
        stats, mv, rstd = both(m, "stats", [T, 6]), both(m, "mv", [T, 2]), both(m, "rstd", [T, 2])
        xnT, qT = both(m, "xnT", [C, T]), both(m, "qT", [C, T])
        ctx, ctxT = both(m, "ctx", [S, CD]), both(m, "ctxT", [CD, S])
        kT = both(m, "kT", [C, S])
        kblock = both(m, "kblock", [C, H, S])
        vpad = both(m, "vpad", [128, H, C])
        prob = both(m, "prob", [T, H, S])
        mx, sm = both(m, "mx", [T, H]), both(m, "sm", [T, 2, H])
        probT = both(m, "probT", [128, H, T])
        att, attT = both(m, "att", [T, C]), both(m, "attT", [C, T])
        ps = [m.ps(f"ps{l}", [128, 4, 512]) for l in (0, 1)]
        loaded, zeroed, prep, scaled = (m.sem(n) for n in ("loaded", "zeroed", "prep", "scaled"))
        x_in = [m.sem(f"x_in{l}") for l in (0, 1)]
        c_in = [m.sem(f"c_in{l}") for l in (0, 1)]
        vec = Steps(m.lanes("vec_done"), ["stats mv", "xn", "v", "mx sub", "sum rsum", "pT", "att", "x"])
        act = Steps(m.lanes("act_done"), ["lnv rstd", "xnT cT", "qT kT", "exp", "pT", "attT"])
        pe = Steps(m.lanes("pe_done"), ["xnT", "qkv", "s", "pT", "pv", "attT", "y"])
        pool = Steps(m.lanes("pool_done"), ["xb", "kb"])
        NZERO, NLOAD = 6, 8 * 16

        with nc.Block() as block:
            @block.sync
            def _(sp):
                for buf, src in ((wq, d["L1_xattn_Wq"]), (wk, d["L1_xattn_Wk"]), (wv, d["L1_xattn_Wv"]),
                                 (wo, d["L1_xattn_Wo"]), (bq, d["L1_xattn_bq"].unsqueeze(1)),
                                 (bk, d["L1_xattn_bk"].unsqueeze(1)),
                                 (bv, row_bc(d["L1_xattn_bv"])), (bo, row_bc(d["L1_xattn_bo"]))):
                    sp.dma_start(buf[:], src).then_inc(loaded, 16)
                with sp.Fori(0, TRIPS) as trip:
                    for l in (0, 1):
                        b = sp.snap(trip * 2 + l)
                        src = flat(g.x[:, bass.ds(b, 1), :])
                        csrc = d["ctx_512"][bass.ds(b, 1)].rearrange("b s c -> (b s) c")
                        sp.wait_ge(*vec.at("xn", trip, l, ago=1))
                        sp.dma_start(xin[l][:], src).then_inc(x_in[l], 16)
                        sp.wait_ge(*pe.at("xnT", trip, l, ago=1))
                        sp.dma_start(ctx[l][:], csrc).then_inc(c_in[l], 16)

            @block.gpsimd
            def _(gp):
                for l in (0, 1):
                    gp.memset(vpad[l][:], 0.0).then_inc(zeroed, 1)
                    gp.memset(probT[l][:], 0.0).then_inc(zeroed, 1)
                gp.memset(eps[:], LN_EPS).then_inc(zeroed, 1)
                gp.memset(hmask[:], 1.0).then_inc(zeroed, 1)
                gp.wait_ge(zeroed, NZERO)
                gp.affine_select(out=hmask[:], in_=hmask[:], compare_op=ALU.is_ge, fill=0.0, base=0,
                                 pattern=[[-HD, H]], channel_multiplier=1).then_inc(prep, 1)
                gp.wait_ge(prep, 1)
                gp.affine_select(out=hmask[:], in_=hmask[:], compare_op=ALU.is_ge, fill=0.0, base=HD - 1,
                                 pattern=[[HD, H]], channel_multiplier=-1).then_inc(prep, 1)
                pool.start(gp)
                gp.wait_ge(loaded, NLOAD)
                gp.wait_ge(prep, 2)
                with gp.Fori(0, TRIPS) as trip:
                    for l in (0, 1):
                        gp.wait_ge(x_in[l], trip * 16 + 16)
                        gp.wait_ge(*vec.at("x", trip, l, ago=1))
                        gp.tensor_tensor(xb[l][:], xin[l][:], bo[:], ALU.add).then_inc(*pool.did("xb", l))
                    for l in (0, 1):
                        gp.wait_ge(*act.at("kT", trip, l))
                        gp.tensor_tensor(kblock[l][:], kT[l][:].unsqueeze(1).to_broadcast([C, H, S]),
                                         hmask[:].unsqueeze(2).to_broadcast([C, H, S]), ALU.mult
                                         ).then_inc(*pool.did("kb", l))

            @block.scalar
            def _(sc):
                sc.preload_act_table_set("natural_log_exp_and_others")
                act.start(sc)
                sc.wait_ge(zeroed, NZERO)
                sc.wait_ge(loaded, NLOAD)
                sc.activation(bq[:], bq[:], ACT.Copy, scale=SCALE).then_inc(scaled, 1)
                sc.wait_ge(scaled, 1)
                with sc.Fori(0, TRIPS) as trip:
                    for l in (0, 1):
                        sc.wait_ge(*vec.at("mv", trip, l))
                        rsqrt_of_variance(sc, act, trip, l, rstd[l], mv[l], eps)
                    for l in (0, 1):
                        sc.wait_ge(*pe.at("xnT", trip, l))
                        sc.activation(xnT[l][:], ps[l][:, 0, 0:T], ACT.Copy).then_inc(*act.did("xnT", l))
                        sc.activation(ctxT[l][:], ps[l][0:CD, 0, T:T + S], ACT.Copy).then_inc(*act.did("cT", l))
                    for l in (0, 1):
                        sc.wait_ge(*pe.at("qkv", trip, l))
                        sc.activation(qT[l][:], ps[l][:, 1, 0:T], ACT.Identity, bias=bq[:, 0:1], scale=SCALE
                                      ).then_inc(*act.did("qT", l))
                        sc.activation(kT[l][:], ps[l][:, 1, T:T + S], ACT.Identity, bias=bk[:, 0:1]
                                      ).then_inc(*act.did("kT", l))
                    for l in (0, 1):
                        sc.wait_ge(*vec.at("sub", trip, l))
                        sc.activation(prob[l][:], prob[l][:], ACT.Exp).then_inc(*act.did("exp", l))
                    for l in (0, 1):
                        sc.wait_ge(*pe.at("pT", trip, l))
                        sc.activation(probT[l][0:S, 0:8].rearrange("p h t -> p (h t)"),
                                      ps[l][0:S, 0:2].rearrange("p a t -> p (a t)"), ACT.Copy).then_inc(*act.did("pT", l))
                    for l in (0, 1):
                        sc.wait_ge(*pe.at("attT", trip, l))
                        sc.activation(attT[l][:], ps[l][:, 1, 0:T], ACT.Copy).then_inc(*act.did("attT", l))

            @block.tensor
            def _(te):
                pe.start(te)
                te.wait_ge(zeroed, NZERO)
                te.wait_ge(loaded, NLOAD)
                with te.Fori(0, TRIPS) as trip:
                    for l in (0, 1):
                        te.wait_ge(c_in[l], trip * 16 + 16)
                        te.wait_ge(*vec.at("xn", trip, l))
                        te.transpose(ps[l][:, 0, 0:T], xn[l][:], g.ident[:])
                        te.transpose(ps[l][0:CD, 0, T:T + S], ctx[l][:], g.ident[0:S, 0:S]).then_inc(*pe.did("xnT", l))
                    for l in (0, 1):
                        te.wait_ge(*act.at("cT", trip, l))
                        te.matmul(ps[l][:, 1, 0:T], wq[:], xnT[l][:], start=True, stop=True)
                        te.matmul(ps[l][:, 1, T:T + S], wk[:], ctxT[l][:], start=True, stop=True)
                        te.matmul(ps[l][0:S, 2, 0:C], ctxT[l][:], wv[:], start=True, stop=True
                                  ).then_inc(*pe.did("qkv", l))
                    for l in (0, 1):
                        te.wait_ge(*pool.at("kb", trip, l))
                        te.wait_ge(*vec.at("v", trip, l))
                        for c in range(4):
                            mm = te.matmul(ps[l][:, c, 0:4 * S], qT[l][:],
                                           kblock[l][:, 4 * c:4 * c + 4].rearrange("p h s -> p (h s)"),
                                           start=True, stop=True)
                        mm.then_inc(*pe.did("s", l))
                    for l in (0, 1):
                        te.wait_ge(*act.at("exp", trip, l))
                        for h in range(H):
                            mm = te.transpose(ps[l][0:S, h // 4, T * (h % 4):T * (h % 4) + T], prob[l][:, h],
                                              g.ident[:])
                        mm.then_inc(*pe.did("pT", l))
                    for l in (0, 1):
                        te.wait_ge(*act.at("pT", trip, l))
                        te.wait_ge(*vec.at("pT", trip, l))
                        for h in range(H):
                            mm = te.matmul(ps[l][:, 0, 0:C], probT[l][:, h], vpad[l][:, h],
                                           start=(h == 0), stop=(h == H - 1))
                        mm.then_inc(*pe.did("pv", l))
                    for l in (0, 1):
                        te.wait_ge(*vec.at("att", trip, l))
                        te.transpose(ps[l][:, 1, 0:T], att[l][:], g.ident[:]).then_inc(*pe.did("attT", l))
                    for l in (0, 1):
                        te.wait_ge(*act.at("attT", trip, l))
                        te.matmul(ps[l][:, 2, 0:C], attT[l][:], wo[:], start=True, stop=True).then_inc(*pe.did("y", l))

            @block.vector
            def _(v):
                vec.start(v)
                v.wait_ge(loaded, NLOAD)
                v.wait_ge(zeroed, NZERO)
                with v.Fori(0, TRIPS) as trip:
                    for l in (0, 1):
                        v.wait_ge(x_in[l], trip * 16 + 16)
                        v.wait_ge(*vec.at("x", trip, l, ago=1))
                        row_statistics(v, vec, trip, l, stats[l][:], mv[l], rstd[l][:, 1:2], xin[l][:])
                    for l in (0, 1):
                        v.wait_ge(*pool.at("xb", trip, l))
                        v.wait_ge(*act.at("rstd", trip, l))
                        v.tensor_scalar(xn[l][:], xin[l][:], mv[l][:, 0:1], rstd[l][:, 1:2], ALU.subtract, ALU.mult
                                        ).then_inc(*vec.did("xn", l))
                    for l in (0, 1):
                        v.wait_ge(*pe.at("qkv", trip, l))
                        v.tensor_tensor(diagonal(vpad[l], H, C + HD, HD, rows=S),
                                        ps[l][0:S, 2, 0:C].rearrange("p (h e) -> p h e", e=HD),
                                        bv[0:S].rearrange("p (h e) -> p h e", e=HD), ALU.add).then_inc(*vec.did("v", l))
                    for l in (0, 1):
                        scores = ps[l][:, :, 0:4 * S].rearrange("p a (h s) -> p a h s", s=S)
                        four = lambda ap: ap.rearrange("p (a h) -> p a h", a=4)
                        v.wait_ge(*pe.at("s", trip, l))
                        v.tensor_reduce(four(mx[l][:]), scores, AX, ALU.max).then_inc(*vec.did("mx", l))
                        v.wait_ge(*vec.at("mx", trip, l))
                        v.tensor_tensor(prob[l][:].rearrange("p (a h) s -> p a h s", a=4), scores,
                                        four(mx[l][:]).unsqueeze(3).to_broadcast([T, 4, 4, S]), ALU.subtract
                                        ).then_inc(*vec.did("sub", l))
                    for l in (0, 1):
                        v.wait_ge(*act.at("exp", trip, l))
                        v.tensor_reduce(sm[l][:, 0], prob[l][:], AX, ALU.add).then_inc(*vec.did("sum", l))
                        v.wait_ge(*vec.at("sum", trip, l))
                        v.reciprocal(sm[l][:, 1], sm[l][:, 0]).then_inc(*vec.did("rsum", l))
                    for l in (0, 1):
                        v.wait_ge(*pe.at("pT", trip, l))
                        v.tensor_copy(probT[l][0:S, 8:16].rearrange("p h t -> p (h t)"),
                                      ps[l][0:S, 2:4].rearrange("p a t -> p (a t)")).then_inc(*vec.did("pT", l))
                    for l in (0, 1):
                        v.wait_ge(*pe.at("pv", trip, l))
                        v.wait_ge(*vec.at("rsum", trip, l))
                        v.tensor_tensor(att[l][:].rearrange("p (h e) -> p h e", e=HD),
                                        ps[l][:, 0, 0:C].rearrange("p (h e) -> p h e", e=HD),
                                        sm[l][:, 1].unsqueeze(2).to_broadcast([T, H, HD]), ALU.mult
                                        ).then_inc(*vec.did("att", l))
                    for l in (0, 1):
                        v.wait_ge(*pe.at("y", trip, l))
                        v.tensor_tensor(flat(g.x[:, bass.ds(trip * 2 + l, 1), :]), xb[l][:], ps[l][:, 2, 0:C], ALU.add
                                        ).then_inc(*vec.did("x", l))


def experts(nc, g):
    E, HID, K = 16, 64, 2
    N = E * HID
    CH = N // 128
    TRIPS = g.NB // 2
    LOW, HIGH = -3.0e38, 3.0e38
    d = g.d
    with ExitStack() as stack:
        m = Memory(nc, stack, "mo")
        w1 = m.sb("w1", [C, E, HID])
        w2 = m.sb("w2", [128, CH, C])
        b2 = m.sb("b2", [128, C])
        wr = m.sb("wr", [C, E])
        b1, br = m.sb("b1", [T, N]), m.sb("br", [T, E])
        eps = m.sb("eps", [128, 1])
        xin, xn = (both(m, n, [T, C]) for n in ("xin", "xn"))
        stats, mv, rstd = both(m, "stats", [T, 6]), both(m, "mv", [T, 2]), both(m, "rstd", [T, 2])
        xnT = both(m, "xnT", [C, T])
        hid = both(m, "hid", [T, E, HID])
        logit = both(m, "logit", [T, E + 8])
        left = both(m, "left", [T, E + 8])
        top, chosen = both(m, "top", [T, 8]), both(m, "chosen", [T, 8])
        carrier = both(m, "carrier", [T, 2])
        gate = both(m, "gate", [T, E])
        hidT = both(m, "hidT", [128, CH, T])
        gateT = both(m, "gateT", [128, T])
        ps = [m.ps(f"ps{l}", [128, 4, 512]) for l in (0, 1)]
        loaded, zeroed = m.sem("loaded"), m.sem("zeroed")
        x_in = [m.sem(f"x_in{l}") for l in (0, 1)]
        vec = Steps(m.lanes("vec_done"), ["stats mv", "xn", "logit top chosen left mask plus gate hb hid", "x"])
        act = Steps(m.lanes("act_done"), ["lnv rstd", "xnT", "hT gT"])
        pool = Steps(m.lanes("pool_done"), ["xr"])
        pe = Steps(m.lanes("pe_done"), ["xnT", "r h", "hT", "y"])
        NZERO, NLOAD = 8, 6 * 16

        with nc.Block() as block:
            @block.sync
            def _(sp):
                sp.dma_start(w1[:], d["L1_ffn_W1"].rearrange("e c h -> c e h")).then_inc(loaded, 16)
                sp.dma_start(w2[:], d["L1_ffn_W2"].rearrange("(j e) h n -> (e h) j n", e=2)).then_inc(loaded, 16)
                sp.dma_start(wr[:], d["L1_ffn_Wr"]).then_inc(loaded, 16)
                sp.dma_start(b1[:], row_bc(d["L1_ffn_b1"].rearrange("e h -> (e h)"))).then_inc(loaded, 16)
                sp.dma_start(br[:], row_bc(d["L1_ffn_br"])).then_inc(loaded, 16)
                sp.wait_ge(zeroed, 1)
                sp.dma_start(b2[0:E], d["L1_ffn_b2"]).then_inc(loaded, 16)
                with sp.Fori(0, TRIPS) as trip:
                    for l in (0, 1):
                        src = flat(g.x[:, bass.ds(sp.snap(trip * 2 + l), 1), :])
                        sp.wait_ge(*vec.at("x", trip, l, ago=1))
                        sp.dma_start(xin[l][:], src).then_inc(x_in[l], 16)

            @block.gpsimd
            def _(gp):
                gp.memset(b2[:], 0.0).then_inc(zeroed, 1)
                gp.memset(eps[:], LN_EPS).then_inc(zeroed, 1)
                for l in (0, 1):
                    gp.memset(gateT[l][:], 0.0).then_inc(zeroed, 1)
                    gp.memset(logit[l][:], LOW).then_inc(zeroed, 1)
                    gp.memset(chosen[l][:], LOW).then_inc(zeroed, 1)
                pool.start(gp)
                with gp.Fori(0, TRIPS) as trip:
                    for l in (0, 1):
                        gp.wait_ge(*vec.at("xn", trip, l))
                        gp.tensor_tensor(xin[l][:], xin[l][:], xn[l][:], ALU.add).then_inc(*pool.did("xr", l))

            @block.scalar
            def _(sc):
                sc.preload_act_table_set("natural_log_exp_and_others")
                act.start(sc)
                sc.wait_ge(zeroed, NZERO)
                with sc.Fori(0, TRIPS) as trip:
                    for l in (0, 1):
                        sc.wait_ge(*vec.at("mv", trip, l))
                        rsqrt_of_variance(sc, act, trip, l, rstd[l], mv[l], eps)
                    for l in (0, 1):
                        sc.wait_ge(*pe.at("xnT", trip, l))
                        sc.activation(xnT[l][:], ps[l][:, 0, 0:T], ACT.Copy).then_inc(*act.did("xnT", l))
                    for l in (0, 1):
                        sc.wait_ge(*pe.at("hT", trip, l))
                        sc.activation(hidT[l][:].rearrange("p j t -> p (j t)"),
                                      ps[l][:, 0:2].rearrange("p a t -> p (a t)"), ACT.Copy).then_inc(*act.did("hT", l))
                        sc.activation(gateT[l][0:E], ps[l][0:E, 2, 0:T], ACT.Copy).then_inc(*act.did("gT", l))

            @block.tensor
            def _(te):
                pe.start(te)
                te.wait_ge(zeroed, NZERO)
                te.wait_ge(loaded, NLOAD)
                with te.Fori(0, TRIPS) as trip:
                    for l in (0, 1):
                        te.wait_ge(*vec.at("xn", trip, l))
                        te.transpose(ps[l][:, 0, 0:T], xn[l][:], g.ident[:]).then_inc(*pe.did("xnT", l))
                    for l in (0, 1):
                        te.wait_ge(*act.at("xnT", trip, l))
                        te.matmul(ps[l][:, 1, 0:E], xnT[l][:], wr[:], start=True, stop=True).then_inc(*pe.did("r", l))
                        for a in (0, 1):
                            mm = te.matmul(ps[l][:, 2 + a], xnT[l][:],
                                           w1[:, 8 * a:8 * a + 8].rearrange("p e h -> p (e h)"), start=True, stop=True)
                        mm.then_inc(*pe.did("h", l))
                    for l in (0, 1):
                        te.wait_ge(*vec.at("hid", trip, l))
                        for j in range(CH):
                            te.transpose(ps[l][:, j // 4, T * (j % 4):T * (j % 4) + T],
                                         hid[l][:, 2 * j:2 * j + 2].rearrange("p e h -> p (e h)"), g.ident[:])
                        te.transpose(ps[l][0:E, 2, 0:T], gate[l][:], g.ident[:]).then_inc(*pe.did("hT", l))
                    for l in (0, 1):
                        te.wait_ge(*act.at("gT", trip, l))
                        for j in range(CH):
                            te.matmul(ps[l][:, 3, 0:C], hidT[l][:, j], w2[:, j], start=(j == 0), stop=False)
                        te.matmul(ps[l][:, 3, 0:C], gateT[l][:], b2[:], start=False, stop=True).then_inc(*pe.did("y", l))

            @block.vector
            def _(v):
                vec.start(v)
                v.wait_ge(loaded, NLOAD)
                v.wait_ge(zeroed, NZERO)
                with v.Fori(0, TRIPS) as trip:
                    for l in (0, 1):
                        v.wait_ge(x_in[l], trip * 16 + 16)
                        row_statistics(v, vec, trip, l, stats[l][:], mv[l], rstd[l][:, 1:2], xin[l][:])
                    for l in (0, 1):
                        v.wait_ge(*act.at("rstd", trip, l))
                        v.tensor_scalar(xn[l][:], xin[l][:], mv[l][:, 0:1], rstd[l][:, 1:2], ALU.subtract, ALU.mult
                                        ).then_inc(*vec.did("xn", l))
                    for l in (0, 1):
                        v.wait_ge(*pe.at("r", trip, l))
                        v.tensor_tensor(logit[l][:, 0:E], ps[l][:, 1, 0:E], br[:], ALU.add).then_inc(*vec.did("logit", l))
                        v.wait_ge(*vec.at("logit", trip, l))
                        v.memset(carrier[l][:, 0:1], 0.0)
                        v.max(top[l][:], logit[l][:, 0:E]).then_inc(*vec.did("top", l))
                        v.wait_ge(*vec.at("top", trip, l))
                        v.tensor_copy(chosen[l][:, 0:K], top[l][:, 0:K]).then_inc(*vec.did("chosen", l))
                        v.wait_ge(*vec.at("chosen", trip, l))
                        v.memset(carrier[l][:, 1:2], 0.0)
                        v.match_replace(left[l][:], chosen[l][:], logit[l][:], HIGH).then_inc(*vec.did("left", l))
                        v.wait_ge(*vec.at("left", trip, l))
                        v.tensor_tensor(gate[l][:], left[l][:, 0:E], logit[l][:, 0:E], ALU.not_equal
                                        ).then_inc(*vec.did("mask", l))
                        v.wait_ge(*vec.at("mask", trip, l))
                        v.tensor_tensor(gate[l][:], gate[l][:], logit[l][:, 0:E], ALU.add).then_inc(*vec.did("plus", l))
                        v.wait_ge(*vec.at("plus", trip, l))
                        v.tensor_tensor(gate[l][:], gate[l][:], logit[l][:, 0:E], ALU.subtract
                                        ).then_inc(*vec.did("gate", l))
                        v.wait_ge(*pe.at("h", trip, l))
                        v.tensor_tensor(hid[l][:].rearrange("p e h -> p (e h)"),
                                        ps[l][:, 2:4].rearrange("p a t -> p (a t)"), b1[:], ALU.add
                                        ).then_inc(*vec.did("hb", l))
                        v.wait_ge(*vec.at("hb", trip, l))
                        v.scalar_tensor_tensor(out=hid[l][:], in0=hid[l][:], scalar=0.0,
                                               in1=gate[l][:].unsqueeze(2).to_broadcast([T, E, HID]),
                                               op0=ALU.max, op1=ALU.mult).then_inc(*vec.did("hid", l))
                    for l in (0, 1):
                        v.wait_ge(*pool.at("xr", trip, l))
                        v.wait_ge(*pe.at("y", trip, l))
                        v.tensor_tensor(flat(g.x[:, bass.ds(trip * 2 + l, 1), :]), xin[l][:], ps[l][:, 3, 0:C], ALU.add
                                        ).then_inc(*vec.did("x", l))


PHASES = [linear_attention, cross_attention, local_transformer, mamba, context_attention, experts]


def store(nc, g):
    with ExitStack() as stack:
        stored = Memory(nc, stack, "st").sem("stored")
        with nc.Block() as block:
            @block.sync
            def _(sp):
                sp.dma_start(g.out.rearrange("b t c -> t b c"), g.x[:]).then_inc(stored, 16)
                sp.wait_ge(stored, 16)


class Globals:
    pass


def decoder(nc, inputs, out):
    g = Globals()
    g.d, g.out, g.NB = inputs, out, inputs["x"].shape[0]
    with ExitStack() as scope:
        constants(nc, g, scope)
        for phase in PHASES:
            phase(nc, g)
        store(nc, g)


def kernel(**inputs):
    import concourse.bacc as bacc
    from concourse.bass_utils import run_bass_kernel_spmd

    nc = bacc.Bacc("TRN2", target_bir_lowering=False, num_devices=1)
    arrays = {name: np.ascontiguousarray(a) for name, a in inputs.items()}
    arrays.update(shape_tables())
    dram = {name: nc.dram_tensor(f"in_{name}", a.shape, mybir.dt.from_np(a.dtype), kind="ExternalInput").ap()
            for name, a in arrays.items()}
    out = nc.dram_tensor("out_x", arrays["x"].shape, F32, kind="ExternalOutput").ap()
    decoder(nc, dram, out)
    r = run_bass_kernel_spmd(nc, [{f"in_{name}": a for name, a in arrays.items()}], core_ids=[0])
    return r.results[0]["out_x"]
```

```python
from contextlib import ExitStack

import numpy as np

import concourse.bass as bass
from concourse import mybir

F32 = mybir.dt.float32
ALU = mybir.AluOpType
ACT = mybir.ActivationFunctionType
AX = mybir.AxisListType.X

T = 128
C = 128
LN_EPS = 1e-5


class Steps:

    def __init__(self, sems, groups):
        self.sems = sems
        lanes = [(0, 1)] if len(sems) == 1 else [(0,), (1,)]
        self.orders = [[(name, lane) for group in groups for lane in ls for name in group.split()] for ls in lanes]
        self.per_trip = len(self.orders[0])
        assert len(set(self.orders[0])) == self.per_trip, "a step's name stands twice"
        self.next = [0] * len(sems)

    def start(self, eng):
        for sem in self.sems:
            eng.sem_inc(sem, self.per_trip)

    def did(self, name, lane):
        n = lane % len(self.sems)
        order = self.orders[n]
        assert order[self.next[n]] == (name, lane), (order[self.next[n]], name, lane)
        self.next[n] = (self.next[n] + 1) % self.per_trip
        return self.sems[n], 1

    def at(self, name, trip, lane, ago=0):
        n = lane % len(self.sems)
        place = self.orders[n].index((name, lane)) + 1
        return self.sems[n], trip * self.per_trip + (self.per_trip * (1 - ago) + place)


class Memory:

    def __init__(self, nc, stack, prefix):
        self.nc, self.stack, self.prefix = nc, stack, prefix

    def sb(self, name, shape):
        return self.stack.enter_context(self.nc.sbuf_tensor(f"{self.prefix}_{name}", shape, F32))

    def ps(self, name, shape):
        return self.stack.enter_context(self.nc.psum_tensor(f"{self.prefix}_{name}", shape, F32))

    def sem(self, name):
        return self.stack.enter_context(self.nc.semaphore(f"{self.prefix}_{name}"))

    def lanes(self, name):
        return [self.sem(f"{name}{lane}") for lane in (0, 1)]


def flat(ap):
    return ap.rearrange("p b c -> p (b c)")


def row_bc(dram, n=128):
    return dram.partition_broadcast(n)


def diagonal(buf, blocks, step, width, rows=128):
    whole = buf[:]
    return bass.AP(tensor=whole.tensor, offset=whole.offset,
                   ap=[[whole.ap[0][0], rows], [step, blocks], [1, width]])


def constants(nc, g, block_scope):
    m = Memory(nc, block_scope, "k")
    g.ident = m.sb("ident", [128, 128])
    g.tri = m.sb("tri", [128, 128])
    g.after = m.sb("after", [128, 128])
    g.shift = m.sb("shift", [128, 128])
    g.local = m.sb("local", [128, 128])
    g.ones = m.sb("ones", [128, 128])
    g.x = m.sb("x", [T, g.NB, C])
    made, xload = m.sem("made"), m.sem("xload")
    with nc.Block() as block:
        @block.sync
        def _(sp):
            sp.dma_start(g.x[:], g.d["x"].rearrange("b t c -> t b c")).then_inc(xload, 16)
            sp.wait_ge(xload, 16)

        @block.gpsimd
        def _(pool):
            for i, (buf, value) in enumerate([(g.ident, 0.0), (g.shift, 0.0), (g.tri, 1.0), (g.after, 1.0),
                                              (g.local, 0.0), (g.ones, 1.0)]):
                pool.memset(buf[:], value).then_inc(made, 1)
            pool.wait_ge(made, 6)
            pool.affine_select(out=g.ident[:], in_=g.ident[:], compare_op=ALU.not_equal, fill=1.0,
                               base=0, pattern=[[-1, 128]], channel_multiplier=1).then_inc(made, 1)
            pool.affine_select(out=g.shift[:], in_=g.shift[:], compare_op=ALU.not_equal, fill=1.0,
                               base=1, pattern=[[-1, 128]], channel_multiplier=1).then_inc(made, 1)
            pool.affine_select(out=g.tri[:], in_=g.tri[:], compare_op=ALU.is_ge, fill=0.0,
                               base=0, pattern=[[1, 128]], channel_multiplier=-1).then_inc(made, 1)
            pool.affine_select(out=g.after[:], in_=g.after[:], compare_op=ALU.is_gt, fill=0.0,
                               base=0, pattern=[[-1, 128]], channel_multiplier=1).then_inc(made, 1)
            pool.affine_select(out=g.local[:], in_=g.local[:], compare_op=ALU.is_ge, fill=-1e30,
                               base=0, pattern=[[-1, 128]], channel_multiplier=1).then_inc(made, 1)
            pool.wait_ge(made, 11)
            pool.affine_select(out=g.local[:], in_=g.local[:], compare_op=ALU.is_ge, fill=-1e30,
                               base=64, pattern=[[1, 128]], channel_multiplier=-1).then_inc(made, 1)
            pool.wait_ge(made, 12)


def both(m, name, shape):
    return [m.sb(f"{name}{lane}", shape) for lane in (0, 1)]


def row_statistics(v, vec, trip, l, stats, mv, carrier, src):
    v.bn_stats(stats, src).then_inc(*vec.did("stats", l))
    v.wait_ge(*vec.at("stats", trip, l))
    v.memset(carrier, 0.0)
    v.bn_aggr(mv[:], stats).then_inc(*vec.did("mv", l))


def rsqrt_of_variance(sc, act, trip, l, rstd, mv, eps, ln="lnv", exp="rstd"):
    sc.activation(rstd[:, 0:1], mv[:, 1:2], ACT.Ln, bias=eps[:]).then_inc(*act.did(ln, l))
    sc.wait_ge(*act.at(ln, trip, l))
    sc.activation(rstd[:, 1:2], rstd[:, 0:1], ACT.Exp, scale=-0.5).then_inc(*act.did(exp, l))


def linear_attention(nc, g):
    H, HD, M, R = 16, 8, 32, 2
    PAIRS = H // 2
    TRIPS = g.NB // 2
    d = g.d
    with ExitStack() as stack:
        m = Memory(nc, stack, "la")
        wqkv = m.sb("wqkv", [C, 3 * C])
        bqkv = m.sb("bqkv", [T, 3 * C])
        wout = m.sb("wout", [C, C])
        bout = m.sb("bout", [T, C])
        omega = m.sb("omega", [C, PAIRS, 2, R, M])
        node = m.sb("node", [128, 1])
        fscale = m.sb("fscale", [128, 1])
        fbias = m.sb("fbias", [128, 1])
        fweight = m.sb("fweight", [128, 1])
        eps = m.sb("eps", [128, 1])
        lnscale = m.sb("lnscale", [128, 1])
        xin = [m.sb(f"xin{l}", [T, C]) for l in (0, 1)]
        xb = [m.sb(f"xb{l}", [T, C]) for l in (0, 1)]
        stats = [m.sb(f"stats{l}", [T, 6]) for l in (0, 1)]
        mv = [m.sb(f"mv{l}", [T, 2]) for l in (0, 1)]
        rstd = [m.sb(f"rstd{l}", [T, 2]) for l in (0, 1)]
        xn = [m.sb(f"xn{l}", [T, C]) for l in (0, 1)]
        xnT = [m.sb(f"xnT{l}", [C, T]) for l in (0, 1)]
        qkv = [m.sb(f"qkv{l}", [T, 3 * C]) for l in (0, 1)]
        sq = [m.sb(f"sq{l}", [T, 2 * C]) for l in (0, 1)]
        ss = [m.sb(f"ss{l}", [T, 3, 2 * H]) for l in (0, 1)]
        qkT = [m.sb(f"qkT{l}", [C, 2, T]) for l in (0, 1)]
        ef = [m.sb(f"ef{l}", [128, 2, PAIRS, T]) for l in (0, 1)]
        qf = [m.sb(f"qf{l}", [128, PAIRS, 2, T]) for l in (0, 1)]
        sm = [m.sb(f"sm{l}", [T, H, T]) for l in (0, 1)]
        vpad = [m.sb(f"vpad{l}", [T, H, C + H]) for l in (0, 1)]
        den = [m.sb(f"den{l}", [T, 2, H]) for l in (0, 1)]
        att = [m.sb(f"att{l}", [T, C]) for l in (0, 1)]
        attT = [m.sb(f"attT{l}", [C, T]) for l in (0, 1)]
        ps = [m.ps(f"ps{l}", [128, 4, 512]) for l in (0, 1)]

        loaded, zeroed, prep = m.sem("loaded"), m.sem("zeroed"), m.sem("prep")
        x_in = [m.sem(f"x_in{l}") for l in (0, 1)]
        vec = Steps([m.sem("vec_done")], ["qkv sq ss ssm", "qkn", "qf0 qf1 kf", "mask0 mask1 mask2 mask3", "den rden att", "x"])
        vec_ahead = Steps([m.sem("vec_ahead_done")], ["stats mv", "xn"])
        act = Steps([m.sem("act_done")], ["lnn rn", "qkT", "eq ek", "attT"])
        act_ahead = Steps([m.sem("act_ahead_done")], ["lnv rstd", "xnT"])
        pe = Steps([m.sem("pe_done")], ["qkv", "qkT", "fq fk", "scores", "pv", "attT", "y"])
        pe_ahead = Steps([m.sem("pe_ahead_done")], ["xnT"])
        pool = Steps([m.sem("pool_done")], ["xb", "v", "kfw"])

        with nc.Block() as block:
            @block.sync
            def _(sp):
                sp.dma_start(wqkv[:], d["L0_attn_Wqkv"]).then_inc(loaded, 16)
                sp.dma_start(bqkv[:], row_bc(d["L0_attn_bqkv"])).then_inc(loaded, 16)
                sp.dma_start(wout[:], d["L0_attn_Wout"]).then_inc(loaded, 16)
                sp.dma_start(bout[:], row_bc(d["L0_attn_bout"])).then_inc(loaded, 16)
                for p in range(4):
                    r = p % 2
                    rows = slice(32 * p, 32 * p + 32)
                    sp.dma_start(node[rows, :], row_bc(d["L0_attn_quad_nodes"][r:r + 1], 32)).then_inc(loaded, 16)
                    sp.dma_start(fweight[rows, :], row_bc(d["L0_attn_quad_weights"][r:r + 1], 32)).then_inc(loaded, 16)
                sp.wait_ge(zeroed, 1)
                for h in range(H):
                    sp.dma_start(omega[HD * h:HD * h + HD, h // 2, h % 2, :, :],
                                 d["L0_attn_omega"][:, h].rearrange("r d m -> d r m")).then_inc(loaded, 16)
                with sp.Fori(0, TRIPS) as trip:
                    for l in (0, 1):
                        src = flat(g.x[:, bass.ds(sp.snap(trip * 2 + l), 1), :])
                        sp.wait_ge(*vec.at("qkv", trip, l, ago=1))
                        sp.dma_start(xin[l][:], src).then_inc(x_in[l], 16)

            @block.gpsimd
            def _(gp):
                gp.memset(omega[:], 0.0).then_inc(zeroed, 1)
                for l in (0, 1):
                    gp.memset(vpad[l][:], 0.0).then_inc(zeroed, 1)
                    gp.memset(qf[l][:], 0.0).then_inc(zeroed, 1)
                gp.memset(eps[:], LN_EPS).then_inc(zeroed, 1)
                gp.memset(lnscale[:], 10.0 * float(np.log(2.0))).then_inc(zeroed, 1)
                gp.wait_ge(zeroed, 7)
                for l in (0, 1):
                    for h in range(H):
                        gp.memset(vpad[l][:, h, C + h:C + h + 1], 1.0).then_inc(zeroed, 1)
                pool.start(gp)
                gp.wait_ge(loaded, 16 * (12 + H))
                gp.wait_ge(prep, 3)
                with gp.Fori(0, TRIPS) as trip:
                    for l in (0, 1):
                        gp.wait_ge(x_in[l], trip * 16 + 16)
                        gp.wait_ge(*vec.at("x", trip, l, ago=1))
                        gp.tensor_tensor(xb[l][:], xin[l][:], bout[:], ALU.add).then_inc(*pool.did("xb", l))
                    for l in (0, 1):
                        gp.wait_ge(*vec.at("qkv", trip, l))
                        gp.tensor_tensor(diagonal(vpad[l], H, C + H + HD, HD),
                                         qkv[l][:, 2 * C:3 * C].rearrange("p (h e) -> p h e", h=H),
                                         g.ones[:].rearrange("p (h e) -> p h e", h=H), ALU.mult).then_inc(*pool.did("v", l))
                    for l in (0, 1):
                        gp.wait_ge(*vec.at("kf", trip, l))
                        gp.tensor_tensor(ef[l][:, 1], ef[l][:, 1],
                                         fweight[:].unsqueeze(2).to_broadcast([128, PAIRS, T]), ALU.mult).then_inc(*pool.did("kfw", l))

            @block.scalar
            def _(sc):
                sc.wait_ge(prep, 1)
                sc.activation(fscale[:], fscale[:], ACT.Sqrt).then_inc(prep, 1)
                sc.preload_act_table_set("natural_log_exp_and_others")
                act.start(sc)
                act_ahead.start(sc)
                sc.wait_ge(zeroed, 7)
                sc.wait_ge(prep, 3)

                def normalise(trip):
                    for l in (0, 1):
                        sc.wait_ge(*vec_ahead.at("mv", trip, l))
                        rsqrt_of_variance(sc, act_ahead, trip, l, rstd[l], mv[l], eps)

                def turn(trip):
                    for l in (0, 1):
                        sc.wait_ge(*pe_ahead.at("xnT", trip, l))
                        sc.activation(xnT[l][:], ps[l][:, 0, 0:T], ACT.Copy).then_inc(*act_ahead.did("xnT", l))

                def attend(trip, more):
                    for l in (0, 1):
                        sc.wait_ge(*vec.at("ssm", trip, l))
                        sc.activation(ss[l][:, 1], ss[l][:, 0], ACT.Ln, scale=2.0 ** 20).then_inc(*act.did("lnn", l))
                        sc.wait_ge(*act.at("lnn", trip, l))
                        sc.activation(ss[l][:, 2], ss[l][:, 1], ACT.Exp, scale=-0.5, bias=lnscale[:]
                                      ).then_inc(*act.did("rn", l))
                    for l in (0, 1):
                        sc.wait_ge(*pe.at("qkT", trip, l))
                        sc.activation(qkT[l][:], ps[l][:, 0, 0:2 * T].rearrange("p (a t) -> p a t", a=2), ACT.Copy
                                      ).then_inc(*act.did("qkT", l))
                    for l in (0, 1):
                        sc.wait_ge(*pe.at("fq", trip, l))
                        sc.activation(ef[l][:, 0].rearrange("p a t -> p (a t)"),
                                      ps[l][:, 2:4].rearrange("p a t -> p (a t)"), ACT.Exp,
                                      bias=fbias[:, 0:1], scale=fscale[:, 0:1]).then_inc(*act.did("eq", l))
                        sc.wait_ge(*pe.at("fk", trip, l))
                        sc.activation(ef[l][:, 1].rearrange("p a t -> p (a t)"),
                                      ps[l][:, 0:2].rearrange("p a t -> p (a t)"), ACT.Exp,
                                      bias=fbias[:, 0:1], scale=fscale[:, 0:1]).then_inc(*act.did("ek", l))
                    if more:
                        normalise(trip + 1)
                    for l in (0, 1):
                        sc.wait_ge(*pe.at("attT", trip, l))
                        sc.activation(attT[l][:], ps[l][:, 1, 0:T], ACT.Copy).then_inc(*act.did("attT", l))
                    if more:
                        turn(trip + 1)

                normalise(0)
                turn(0)
                with sc.Fori(0, TRIPS - 1) as trip:
                    attend(trip, True)
                attend(TRIPS - 1, False)

            @block.tensor
            def _(te):
                pe.start(te)
                pe_ahead.start(te)
                te.wait_ge(loaded, 16 * (12 + H))
                te.wait_ge(zeroed, 7 + 2 * H)

                def turn(trip):
                    for l in (0, 1):
                        te.wait_ge(*vec_ahead.at("xn", trip, l))
                        te.wait_ge(*vec.at("att", trip, l, ago=1))
                        te.transpose(ps[l][:, 0, 0:T], xn[l][:], g.ident[:]).then_inc(*pe_ahead.did("xnT", l))

                def attend(trip, more):
                    for l in (0, 1):
                        te.wait_ge(*act_ahead.at("xnT", trip, l))
                        te.matmul(ps[l][:, 1, 0:3 * C], xnT[l][:], wqkv[:], start=True, stop=True
                                  ).then_inc(*pe.did("qkv", l))
                    for l in (0, 1):
                        te.wait_ge(*vec.at("qkn", trip, l))
                        te.transpose(ps[l][:, 0, 0:T], qkv[l][:, 0:C], g.ident[:])
                        te.transpose(ps[l][:, 0, T:2 * T], qkv[l][:, C:2 * C], g.ident[:]).then_inc(*pe.did("qkT", l))
                    for l in (0, 1):
                        te.wait_ge(*act.at("qkT", trip, l))
                        for side, bank, step in ((0, 2, "fq"), (1, 0, "fk")):
                            for j in range(PAIRS):
                                mm = te.matmul(ps[l][:, bank + j // 4, T * (j % 4):T * (j % 4) + T],
                                               omega[:, j].rearrange("p a r m -> p (a r m)"),
                                               qkT[l][:, side], start=True, stop=True)
                            mm.then_inc(*pe.did(step, l))
                    for l in (0, 1):
                        te.wait_ge(*pool.at("kfw", trip, l))
                        te.wait_ge(*vec.at("qf1", trip, l))
                        for j in range(PAIRS):
                            mm = te.matmul(ps[l][:, j // 2, 2 * T * (j % 2):2 * T * (j % 2) + 2 * T],
                                           ef[l][:, 1, j], qf[l][:, j].rearrange("p a t -> p (a t)"),
                                           start=True, stop=True)
                        mm.then_inc(*pe.did("scores", l))
                    for l in (0, 1):
                        te.wait_ge(*vec.at("mask3", trip, l))
                        te.wait_ge(*pool.at("v", trip, l))
                        for h in range(H):
                            mm = te.matmul(ps[l][:, 0, 0:C + H], sm[l][:, h], vpad[l][:, h],
                                           start=(h == 0), stop=(h == H - 1))
                        mm.then_inc(*pe.did("pv", l))
                    for l in (0, 1):
                        te.wait_ge(*vec.at("att", trip, l))
                        te.transpose(ps[l][:, 1, 0:T], att[l][:], g.ident[:]).then_inc(*pe.did("attT", l))
                    if more:
                        turn(trip + 1)
                    for l in (0, 1):
                        te.wait_ge(*act.at("attT", trip, l))
                        te.matmul(ps[l][:, 2, 0:C], attT[l][:], wout[:], start=True, stop=True
                                  ).then_inc(*pe.did("y", l))

                turn(0)
                with te.Fori(0, TRIPS - 1) as trip:
                    attend(trip, True)
                attend(TRIPS - 1, False)

            @block.vector
            def _(v):
                v.wait_ge(loaded, 16 * (12 + H))
                v.tensor_scalar(fscale[:], node[:], 0.0, 2.0, ALU.max, ALU.mult).then_inc(prep, 1)
                v.tensor_scalar(fbias[:], node[:], -1.0, None, ALU.mult).then_inc(prep, 1)
                v.wait_ge(prep, 3)
                v.tensor_scalar(fweight[:], fweight[:], 0.0, 1.0 / M, ALU.max, ALU.mult).then_inc(prep, 1)
                vec.start(v)
                vec_ahead.start(v)
                v.wait_ge(prep, 4)

                def normalise(trip):
                    for l in (0, 1):
                        v.wait_ge(x_in[l], trip * 16 + 16)
                        v.wait_ge(*vec_ahead.at("xn", trip, l, ago=1))
                        row_statistics(v, vec_ahead, trip, l, stats[l][:], mv[l], rstd[l][:, 1:2], xin[l][:])
                    for l in (0, 1):
                        v.wait_ge(*act_ahead.at("rstd", trip, l))
                        v.tensor_scalar(xn[l][:], xin[l][:], mv[l][:, 0:1], rstd[l][:, 1:2], ALU.subtract, ALU.mult
                                        ).then_inc(*vec_ahead.did("xn", l))

                def attend(trip, more):
                    for l in (0, 1):
                        v.wait_ge(*pool.at("xb", trip, l))
                        v.wait_ge(*pe.at("qkv", trip, l))
                        v.tensor_tensor(qkv[l][:], ps[l][:, 1, 0:3 * C], bqkv[:], ALU.add).then_inc(*vec.did("qkv", l))
                        v.wait_ge(*vec.at("qkv", trip, l))
                        v.tensor_tensor(sq[l][:], qkv[l][:, 0:2 * C], qkv[l][:, 0:2 * C], ALU.mult
                                        ).then_inc(*vec.did("sq", l))
                        v.wait_ge(*vec.at("sq", trip, l))
                        v.tensor_reduce(ss[l][:, 0], sq[l][:].rearrange("p (h e) -> p h e", e=HD), AX, ALU.add
                                        ).then_inc(*vec.did("ss", l))
                        v.wait_ge(*vec.at("ss", trip, l))
                        v.tensor_scalar(ss[l][:, 0], ss[l][:, 0], 1e-24, None, ALU.max).then_inc(*vec.did("ssm", l))
                    for l in (0, 1):
                        v.wait_ge(*act.at("rn", trip, l))
                        qk = qkv[l][:, 0:2 * C].rearrange("p (h e) -> p h e", e=HD)
                        v.tensor_tensor(qk, qk, ss[l][:, 2].unsqueeze(2).to_broadcast([T, 2 * H, HD]), ALU.mult
                                        ).then_inc(*vec.did("qkn", l))
                    for l in (0, 1):
                        hi, lo = float(np.exp(np.float64(20.0))), float(np.exp(np.float64(-20.0)))
                        v.wait_ge(*act.at("eq", trip, l))
                        for a in (0, 1):
                            rows = slice(64 * a, 64 * a + 64)
                            v.tensor_scalar(qf[l][rows, :, a, :], ef[l][rows, 0], hi, lo, ALU.min, ALU.max
                                            ).then_inc(*vec.did(f"qf{a}", l))
                        v.wait_ge(*act.at("ek", trip, l))
                        v.tensor_scalar(ef[l][:, 1], ef[l][:, 1], hi, lo, ALU.min, ALU.max
                                        ).then_inc(*vec.did("kf", l))
                    for l in (0, 1):
                        v.wait_ge(*pe.at("scores", trip, l))
                        for c in range(4):
                            v.tensor_tensor(sm[l][:, 4 * c:4 * c + 4],
                                            ps[l][:, c].rearrange("p (h t) -> p h t", h=4),
                                            g.tri[:].unsqueeze(1).to_broadcast([T, 4, T]), ALU.mult
                                            ).then_inc(*vec.did(f"mask{c}", l))
                    if more:
                        normalise(trip + 1)
                    for l in (0, 1):
                        v.wait_ge(*pe.at("pv", trip, l))
                        v.tensor_scalar(den[l][:, 0], ps[l][:, 0, C:C + H], 1e-6, None, ALU.max
                                        ).then_inc(*vec.did("den", l))
                        v.wait_ge(*vec.at("den", trip, l))
                        v.reciprocal(den[l][:, 1], den[l][:, 0]).then_inc(*vec.did("rden", l))
                        v.wait_ge(*vec.at("rden", trip, l))
                        v.tensor_tensor(att[l][:].rearrange("p (h e) -> p h e", e=HD),
                                        ps[l][:, 0, 0:C].rearrange("p (h e) -> p h e", e=HD),
                                        den[l][:, 1].unsqueeze(2).to_broadcast([T, H, HD]), ALU.mult
                                        ).then_inc(*vec.did("att", l))
                    for l in (0, 1):
                        v.wait_ge(*pe.at("y", trip, l))
                        v.tensor_tensor(flat(g.x[:, bass.ds(trip * 2 + l, 1), :]), xb[l][:], ps[l][:, 2, 0:C], ALU.add
                                        ).then_inc(*vec.did("x", l))

                normalise(0)
                with v.Fori(0, TRIPS - 1) as trip:
                    attend(trip, True)
                attend(TRIPS - 1, False)


def cross_attention(nc, g):
    H, HD, CD, S = 16, 64, g.d["ctx_512"].shape[2], g.d["ctx_512"].shape[1]
    PAIRS = H // 2
    TRIPS = g.NB // 2
    d = g.d
    with ExitStack() as stack:
        m = Memory(nc, stack, "ca")
        wqk = m.sb("wqk", [C, PAIRS, 2, CD])
        wvo = m.sb("wvo", [2 * CD, PAIRS, C])
        with ExitStack() as once:
            mo = Memory(nc, once, "cw")
            wq = mo.sb("wq", [C, H * HD])
            wk = mo.sb("wk", [CD, H * HD])
            wv = mo.sb("wv", [CD, H * HD])
            wo = mo.sb("wo", [2 * HD, PAIRS, C])
            wqT = mo.sb("wqT", [2 * HD, PAIRS, C])
            wkT = mo.sb("wkT", [2 * HD, PAIRS, CD])
            wvT = mo.sb("wvT", [2 * HD, PAIRS, CD])
            pw = mo.ps("pw", [128, 4, 512])
            pp = mo.ps("pp", [128, 4, 512])
            loaded, turned, copied, product = (mo.sem(n) for n in ("loaded", "turned", "copied", "product"))
            done = mo.sem("done")
            with nc.Block() as block:
                @block.sync
                def _(sp):
                    sp.dma_start(wq[:], d["L0_xattn_Wq"]).then_inc(loaded, 16)
                    sp.dma_start(wk[:], d["L0_xattn_Wk"]).then_inc(loaded, 16)
                    sp.dma_start(wv[:], d["L0_xattn_Wv"]).then_inc(loaded, 16)
                    sp.dma_start(wo[:], d["L0_xattn_Wo"].rearrange("(j p) n -> p j n", p=128)).then_inc(loaded, 16)

                @block.tensor
                def _(te):
                    te.wait_ge(loaded, 64)
                    for j in range(PAIRS):
                        mm = te.transpose(pw[:, j // 4, C * (j % 4):C * (j % 4) + C], wq[:, 128 * j:128 * j + 128],
                                          g.ident[:])
                    mm.then_inc(turned, 1)
                    for i, w in enumerate((wk, wv)):
                        for j in range(PAIRS):
                            mm = te.transpose(pw[:, 2 + i, CD * j:CD * j + CD], w[:, 128 * j:128 * j + 128],
                                              g.ident[0:CD, 0:CD])
                        mm.then_inc(turned, 1)
                    te.wait_ge(copied, 3)
                    for h in range(H):
                        rows = slice(64 * (h % 2), 64 * (h % 2) + 64)
                        mm = te.matmul(pp[:, h % 2, CD * (h // 2):CD * (h // 2) + CD], wqT[rows, h // 2],
                                       wkT[rows, h // 2], start=True, stop=True)
                    mm.then_inc(product, 1)
                    for h in range(H):
                        rows = slice(64 * (h % 2), 64 * (h % 2) + 64)
                        j = h // 2
                        if h == PAIRS:
                            te.wait_ge(done, 1)
                        bank = 2 + h % 2 if h < PAIRS else h % 2
                        mm = te.matmul(pp[rows, bank, C * (j % 4):C * (j % 4) + C],
                                       wvT[rows, j], wo[rows, j], start=True, stop=True)
                    mm.then_inc(product, 1)

                @block.vector
                def _(v):
                    v.wait_ge(turned, 1)
                    v.tensor_copy(wqT[:].rearrange("p j c -> p (j c)"), pw[:, 0:2].rearrange("p a c -> p (a c)")
                                  ).then_inc(copied, 1)
                    for i, w in enumerate((wkT, wvT)):
                        v.wait_ge(turned, 2 + i)
                        v.tensor_copy(w[:].rearrange("p j c -> p (j c)"), pw[:, 2 + i, 0:PAIRS * CD]
                                      ).then_inc(copied, 1)
                    v.wait_ge(product, 1)
                    v.tensor_scalar(wqk[:].rearrange("p j a c -> p a j c"),
                                    pp[:, 0:2, 0:PAIRS * CD].rearrange("p a (j c) -> p a j c", c=CD),
                                    HD ** -0.5, None, ALU.mult).then_inc(done, 1)
                    v.wait_ge(product, 2)
                    for a in (0, 1):
                        rows = slice(64 * a, 64 * a + 64)
                        for half in (0, 1):
                            bank = 2 + a if half == 0 else a
                            v.tensor_copy(wvo[rows, 4 * half:4 * half + 4],
                                          pp[rows, bank, 0:4 * C].rearrange("p (j c) -> p j c", c=C)
                                          ).then_inc(done, 1)

        bo = m.sb("bo", [T, C])
        eps = m.sb("eps", [128, 1])
        xin, xb, xn = (both(m, n, [T, C]) for n in ("xin", "xb", "xn"))
        stats, mv, rstd = both(m, "stats", [T, 6]), both(m, "mv", [T, 2]), both(m, "rstd", [T, 2])
        xnT = both(m, "xnT", [C, T])
        ctx = both(m, "ctx", [128, 2, CD])
        ctxT = both(m, "ctxT", [2 * CD, 2, S])
        gT = both(m, "gT", [2 * CD, PAIRS, T])
        prob = both(m, "prob", [T, H, S])
        mx, sm = both(m, "mx", [T, H]), both(m, "sm", [T, 2, H])
        probT = both(m, "probT", [128, H, T])
        oT = both(m, "oT", [2 * CD, PAIRS, T])
        ps = [m.ps(f"ps{l}", [128, 4, 512]) for l in (0, 1)]
        loaded, zeroed = m.sem("loaded"), m.sem("zeroed")
        x_in = [m.sem(f"x_in{l}") for l in (0, 1)]
        c_in = [m.sem(f"c_in{l}") for l in (0, 1)]
        vec = Steps([m.sem("vec_done")], ["mx sub", "sum rsum norm", "pT", "oT", "x"])
        vec_ahead = Steps([m.sem("vec_ahead_done")], ["stats mv", "xn"])
        act = Steps([m.sem("act_done")], ["gT", "exp", "pT", "oT"])
        act_ahead = Steps([m.sem("act_ahead_done")], ["lnv rstd", "xnT cT0 cT1"])
        pe = Steps([m.sem("pe_done")], ["g", "s", "pT", "o", "y"])
        pe_ahead = Steps([m.sem("pe_ahead_done")], ["xnT"])
        pool = Steps([m.sem("pool_done")], ["xb", "norm"])
        NZERO = 7
        PH = 11

        with nc.Block() as block:
            @block.sync
            def _(sp):
                sp.dma_start(bo[:], row_bc(d["L0_xattn_bo"])).then_inc(loaded, 16)
                sp.wait_ge(zeroed, NZERO)
                with sp.Fori(0, TRIPS) as trip:
                    for l in (0, 1):
                        src = flat(g.x[:, bass.ds(sp.snap(trip * 2 + l), 1), :])
                        sp.wait_ge(*vec.at("mx", trip, l, ago=1))
                        sp.dma_start(xin[l][:], src).then_inc(x_in[l], 16)
                    for l in (0, 1):
                        csrc = d["ctx_512"][bass.ds(sp.snap(trip * 2 + l), 1)].rearrange("b s c -> (b s) c")
                        sp.wait_ge(*pe.at("o", trip, l, ago=1))
                        for a in (0, 1):
                            sp.dma_start(ctx[l][0:S, a], csrc).then_inc(c_in[l], 16)

            @block.gpsimd
            def _(gp):
                for l in (0, 1):
                    gp.memset(ctx[l][:], 0.0).then_inc(zeroed, 1)
                    gp.memset(ctxT[l][:], 0.0).then_inc(zeroed, 1)
                    gp.memset(probT[l][:], 0.0).then_inc(zeroed, 1)
                gp.memset(eps[:], LN_EPS).then_inc(zeroed, 1)
                pool.start(gp)
                gp.wait_ge(loaded, 16)
                with gp.Fori(0, TRIPS) as trip:
                    for l in (0, 1):
                        gp.wait_ge(x_in[l], trip * 16 + 16)
                        gp.wait_ge(*vec.at("x", trip, l, ago=1))
                        gp.tensor_tensor(xb[l][:], xin[l][:], bo[:], ALU.add).then_inc(*pool.did("xb", l))
                    for l in (0, 1):
                        gp.wait_ge(*vec.at("rsum", trip, l))
                        gp.tensor_tensor(prob[l][:, PH:H], prob[l][:, PH:H],
                                         sm[l][:, 1, PH:H].unsqueeze(2).to_broadcast([T, H - PH, S]),
                                         ALU.mult).then_inc(*pool.did("norm", l))

            @block.scalar
            def _(sc):
                sc.preload_act_table_set("natural_log_exp_and_others")
                act.start(sc)
                act_ahead.start(sc)
                sc.wait_ge(zeroed, NZERO)

                def normalise(trip):
                    for l in (0, 1):
                        sc.wait_ge(*vec_ahead.at("mv", trip, l))
                        rsqrt_of_variance(sc, act_ahead, trip, l, rstd[l], mv[l], eps)

                def turn(trip):
                    for l in (0, 1):
                        sc.wait_ge(*pe_ahead.at("xnT", trip, l))
                        sc.activation(xnT[l][:], ps[l][:, 0, 0:T], ACT.Copy).then_inc(*act_ahead.did("xnT", l))
                        for a in (0, 1):
                            rows = slice(CD * a, CD * a + CD)
                            sc.activation(ctxT[l][rows, a], ps[l][rows, 0, T:T + S], ACT.Copy
                                          ).then_inc(*act_ahead.did(f"cT{a}", l))

                def attend(trip, more):
                    for l in (0, 1):
                        sc.wait_ge(*pe.at("g", trip, l))
                        sc.activation(gT[l][:].rearrange("p j t -> p (j t)"),
                                      ps[l][:, 2:4].rearrange("p a t -> p (a t)"), ACT.Copy).then_inc(*act.did("gT", l))
                    for l in (0, 1):
                        sc.wait_ge(*vec.at("sub", trip, l))
                        sc.activation(prob[l][:], prob[l][:], ACT.Exp).then_inc(*act.did("exp", l))
                    if more:
                        normalise(trip + 1)
                    for l in (0, 1):
                        sc.wait_ge(*pe.at("pT", trip, l))
                        sc.activation(probT[l][0:S, 0:8].rearrange("p h t -> p (h t)"),
                                      ps[l][0:S, 0:2].rearrange("p a t -> p (a t)"), ACT.Copy).then_inc(*act.did("pT", l))
                    for l in (0, 1):
                        sc.wait_ge(*pe.at("o", trip, l))
                        sc.activation(oT[l][0:CD], ps[l][0:CD].rearrange("p a (j e t) -> p (a j) e t", e=2, t=T)[:, :, 0],
                                      ACT.Copy).then_inc(*act.did("oT", l))
                    if more:
                        turn(trip + 1)

                normalise(0)
                turn(0)
                with sc.Fori(0, TRIPS - 1) as trip:
                    attend(trip, True)
                attend(TRIPS - 1, False)

            @block.tensor
            def _(te):
                pe.start(te)
                pe_ahead.start(te)
                te.wait_ge(zeroed, NZERO)

                def turn(trip):
                    for l in (0, 1):
                        te.wait_ge(c_in[l], trip * 32 + 32)
                        te.wait_ge(*vec_ahead.at("xn", trip, l))
                        te.transpose(ps[l][:, 0, 0:T], xn[l][:], g.ident[:])
                        te.transpose(ps[l][:, 0, T:2 * T], ctx[l][:].rearrange("p a c -> p (a c)"), g.ident[:]
                                     ).then_inc(*pe_ahead.did("xnT", l))

                def attend(trip, more):
                    for l in (0, 1):
                        te.wait_ge(*act_ahead.at("cT1", trip, l))
                        for j in range(PAIRS):
                            mm = te.matmul(ps[l][:, 2 + j // 4, T * (j % 4):T * (j % 4) + T],
                                           wqk[:, j].rearrange("p a c -> p (a c)"), xnT[l][:], start=True, stop=True)
                        mm.then_inc(*pe.did("g", l))
                    for l in (0, 1):
                        te.wait_ge(*act.at("gT", trip, l))
                        te.wait_ge(*vec.at("x", trip, l, ago=1))
                        for j in range(PAIRS):
                            mm = te.matmul(ps[l][:, j // 2, 2 * S * (j % 2):2 * S * (j % 2) + 2 * S],
                                           gT[l][:, j], ctxT[l][:].rearrange("p a s -> p (a s)"),
                                           start=True, stop=True)
                        mm.then_inc(*pe.did("s", l))
                    for l in (0, 1):
                        te.wait_ge(*pool.at("norm", trip, l))
                        te.wait_ge(*vec.at("norm", trip, l))
                        for h in range(H):
                            mm = te.transpose(ps[l][0:S, h // 4, T * (h % 4):T * (h % 4) + T], prob[l][:, h],
                                              g.ident[:])
                        mm.then_inc(*pe.did("pT", l))
                    for l in (0, 1):
                        te.wait_ge(*act.at("pT", trip, l))
                        te.wait_ge(*vec.at("pT", trip, l))
                        for c in range(4):
                            mm = te.matmul(ps[l][:, c], ctx[l][:].rearrange("p a c -> p (a c)"),
                                           probT[l][:, 4 * c:4 * c + 4].rearrange("p h t -> p (h t)"),
                                           start=True, stop=True)
                        mm.then_inc(*pe.did("o", l))
                    for l in (0, 1):
                        te.wait_ge(*act.at("oT", trip, l))
                        te.wait_ge(*vec.at("oT", trip, l))
                        for j in range(PAIRS):
                            mm = te.matmul(ps[l][:, 1, 0:C], oT[l][:, j], wvo[:, j],
                                           start=(j == 0), stop=(j == PAIRS - 1))
                        mm.then_inc(*pe.did("y", l))
                    if more:
                        turn(trip + 1)

                turn(0)
                with te.Fori(0, TRIPS - 1) as trip:
                    attend(trip, True)
                attend(TRIPS - 1, False)

            @block.vector
            def _(v):
                vec.start(v)
                vec_ahead.start(v)

                def normalise(trip):
                    for l in (0, 1):
                        v.wait_ge(x_in[l], trip * 16 + 16)
                        v.wait_ge(*vec_ahead.at("xn", trip, l, ago=1))
                        row_statistics(v, vec_ahead, trip, l, stats[l][:], mv[l], rstd[l][:, 1:2], xin[l][:])
                    for l in (0, 1):
                        v.wait_ge(*act_ahead.at("rstd", trip, l))
                        v.tensor_scalar(xn[l][:], xin[l][:], mv[l][:, 0:1], rstd[l][:, 1:2], ALU.subtract, ALU.mult
                                        ).then_inc(*vec_ahead.did("xn", l))

                def attend(trip, more):
                    for l in (0, 1):
                        scores = ps[l][:, :, 0:4 * S].rearrange("p a (h s) -> p a h s", s=S)
                        four = lambda ap: ap.rearrange("p (a h) -> p a h", a=4)
                        v.wait_ge(*pool.at("xb", trip, l))
                        v.wait_ge(*pe.at("s", trip, l))
                        v.tensor_reduce(four(mx[l][:]), scores, AX, ALU.max).then_inc(*vec.did("mx", l))
                        v.wait_ge(*vec.at("mx", trip, l))
                        v.tensor_tensor(prob[l][:].rearrange("p (a h) s -> p a h s", a=4), scores,
                                        four(mx[l][:]).unsqueeze(3).to_broadcast([T, 4, 4, S]), ALU.subtract
                                        ).then_inc(*vec.did("sub", l))
                    for l in (0, 1):
                        v.wait_ge(*act.at("exp", trip, l))
                        v.tensor_reduce(sm[l][:, 0], prob[l][:], AX, ALU.add).then_inc(*vec.did("sum", l))
                        v.wait_ge(*vec.at("sum", trip, l))
                        v.reciprocal(sm[l][:, 1], sm[l][:, 0]).then_inc(*vec.did("rsum", l))
                        v.wait_ge(*vec.at("rsum", trip, l))
                        v.tensor_tensor(prob[l][:, 0:PH], prob[l][:, 0:PH],
                                        sm[l][:, 1, 0:PH].unsqueeze(2).to_broadcast([T, PH, S]), ALU.mult
                                        ).then_inc(*vec.did("norm", l))
                    if more:
                        normalise(trip + 1)
                    for l in (0, 1):
                        v.wait_ge(*pe.at("pT", trip, l))
                        v.tensor_copy(probT[l][0:S, 8:16].rearrange("p h t -> p (h t)"),
                                      ps[l][0:S, 2:4].rearrange("p a t -> p (a t)")).then_inc(*vec.did("pT", l))
                    for l in (0, 1):
                        v.wait_ge(*pe.at("o", trip, l))
                        v.tensor_copy(oT[l][CD:2 * CD],
                                      ps[l][CD:2 * CD].rearrange("p a (j e t) -> p (a j) e t", e=2, t=T)[:, :, 1]
                                      ).then_inc(*vec.did("oT", l))
                    for l in (0, 1):
                        v.wait_ge(*pe.at("y", trip, l))
                        v.tensor_tensor(flat(g.x[:, bass.ds(trip * 2 + l, 1), :]), xb[l][:], ps[l][:, 1, 0:C], ALU.add
                                        ).then_inc(*vec.did("x", l))

                normalise(0)
                with v.Fori(0, TRIPS - 1) as trip:
                    attend(trip, True)
                attend(TRIPS - 1, False)


QK_SCALE = 8.0
ROT_DIM = 64


def shape_tables():
    window, half = 64, np.arange(0, ROT_DIM, 2, dtype=np.float32)
    t = np.arange(T, dtype=np.float32)
    freqs = t[:, None] * (np.float32(1.0) / np.float32(10000.0) ** (half / ROT_DIM))[None, :]
    base = (half + 0.4 * ROT_DIM) / (1.4 * ROT_DIM)
    scale = base[None, :] ** ((t - T // 2) / float(window // 2))[:, None]
    rot = np.zeros((T, 2, 2, ROT_DIM), np.float32)
    for side, s in enumerate((scale * QK_SCALE, 1.0 / scale)):
        rot[:, side, 0] = np.concatenate([np.cos(freqs) * s] * 2, axis=-1)
        rot[:, side, 1] = np.concatenate([-np.sin(freqs) * s, np.sin(freqs) * s], axis=-1)
    return {"rot": rot}


def local_attention(nc, g, layer):
    H, HD = 8, ROT_DIM
    PAIRS, INNER, HALF = H // 2, H * HD, C // 2
    PH = H - 3
    TRIPS = g.NB // 2
    d = g.d
    first = layer == 0
    with ExitStack() as stack:
        m = Memory(nc, stack, f"l{layer}")
        wqkv = m.sb("wqkv", [C, 3, INNER])
        wo = m.sb("wo", [2 * HD, PAIRS, C])
        rot = m.sb("rot", [T, 2, 2, HD])
        qks = m.sb("qks", [T, 2, 2, HD])
        eps, lnscale = m.sb("eps", [128, 1]), m.sb("lnscale", [128, 1])
        xin, yc, ynew = (both(m, n, [T, C]) for n in ("xin", "yc", "ynew"))
        stats, mv, rstd = both(m, "stats", [T, 12]), both(m, "mv", [T, 2]), both(m, "rstd", [T, 2])
        stats0, mv0, rstd0 = both(m, "stats0", [T, 6]), both(m, "mv0", [T, 2]), both(m, "rstd0", [T, 2])
        hT = both(m, "hT", [C, T])
        sq, rc = both(m, "sq", [T, 2 * H, HD]), both(m, "rc", [T, 2, H, HD])
        rs = both(m, "rs", [T, 2, H, HD])
        ss = both(m, "ss", [T, 3, 2 * H])
        val = both(m, "val", [T, INNER])
        qT = both(m, "qT", [2 * HD, PAIRS, T])
        kT = both(m, "kT", [2 * HD, PAIRS, 2, T])
        prob = both(m, "prob", [T, H, T])
        mx, sm = both(m, "mx", [T, H]), both(m, "sm", [T, 2, H])
        probT = both(m, "probT", [T, H, T])
        oT = both(m, "oT", [2 * HD, PAIRS, T])
        ps = [m.ps(f"ps{l}", [128, 4, 512]) for l in (0, 1)]
        loaded, zeroed, prep = m.sem("loaded"), m.sem("zeroed"), m.sem("prep")
        y_in = [m.sem(f"y_in{l}") for l in (0, 1)]
        vec_ahead = Steps(m.lanes("vec_ahead_done"), ["stats mv", "y0"])
        act_ahead = Steps(m.lanes("act_ahead_done"), ["lnv0 rstd0", "hT"] if first else ["hT"])
        pe_ahead = Steps(m.lanes("pe_ahead_done"), ["hT"])
        vec = Steps(m.lanes("vec_done"), ["ss ssm cos sin0 sin1 krot kn", "kT", " ".join(f"s{h}" for h in range(H)) + " mx",
                                        "rsum norm", "pT", "ynew y", "st1 st2 mv2", "hn0 hn1"])
        act = Steps(m.lanes("act_done"), ["sq v lnn rn", "qT kT", " ".join(f"exp{h}" for h in range(H)), "pT", "oT",
                                        "lnv rstd"])
        pe = Steps(m.lanes("pe_done"), ["qk v", "qkT", "s", "pT", "o", "ao", "sh"])
        pool = Steps(m.lanes("pool_done"), ["qrot", "norm"])
        NZERO, NLOAD = 4, 16 * (3 + 2 + 4)

        with nc.Block() as block:
            @block.sync
            def _(sp):
                sp.dma_start(wqkv[:], d["L0_ffn_wqkv"][layer].rearrange("c (a n) -> c a n", a=3)).then_inc(loaded, 16)
                sp.dma_start(wo[:], d["L0_ffn_wo"][layer].rearrange("(j p) n -> p j n", p=128)).then_inc(loaded, 16)
                sp.dma_start(rot[:], d["rot"]).then_inc(loaded, 16)
                for side, name in enumerate(("L0_ffn_q_scale", "L0_ffn_k_scale")):
                    row = d[name][layer]
                    sp.dma_start(qks[:, side, 0], row_bc(row)).then_inc(loaded, 16)
                    sp.dma_start(qks[:, side, 1, 0:HD // 2], row_bc(row[HD // 2:HD])).then_inc(loaded, 16)
                    sp.dma_start(qks[:, side, 1, HD // 2:HD], row_bc(row[0:HD // 2])).then_inc(loaded, 16)
                with sp.Fori(0, TRIPS) as trip:
                    for l in (0, 1):
                        src = flat((g.x if first else g.y)[:, bass.ds(sp.snap(trip * 2 + l), 1), :])
                        sp.wait_ge(*(vec_ahead.at("y0", trip, l, ago=1) if first else pe_ahead.at("hT", trip, l, ago=1)))
                        sp.dma_start((xin if first else yc)[l][:], src).then_inc(y_in[l], 16)

            @block.gpsimd
            def _(gp):
                gp.memset(eps[:], LN_EPS).then_inc(zeroed, 1)
                gp.memset(lnscale[:], 10.0 * float(np.log(2.0))).then_inc(zeroed, 1)
                for l in (0, 1):
                    gp.memset(kT[l][:], 0.0).then_inc(zeroed, 1)
                pool.start(gp)
                with gp.Fori(0, TRIPS) as trip:
                    for l in (0, 1):
                        gp.wait_ge(*vec.at("sin1", trip, l))
                        gp.tensor_tensor(rc[l][:, 0], rc[l][:, 0], rs[l][:, 0], ALU.add).then_inc(*pool.did("qrot", l))
                    for l in (0, 1):
                        gp.wait_ge(*vec.at("rsum", trip, l))
                        gp.tensor_tensor(prob[l][:, PH:H], prob[l][:, PH:H],
                                         sm[l][:, 1, PH:H].unsqueeze(2).to_broadcast([T, H - PH, T]), ALU.mult
                                         ).then_inc(*pool.did("norm", l))

            @block.scalar
            def _(sc):
                sc.preload_act_table_set("natural_log_exp_and_others")
                act.start(sc)
                act_ahead.start(sc)
                sc.wait_ge(zeroed, NZERO)

                def normalise(trip):
                    for l in ((0, 1) if first else ()):
                        sc.wait_ge(*vec_ahead.at("mv", trip, l))
                        rsqrt_of_variance(sc, act_ahead, trip, l, rstd0[l], mv0[l], eps, "lnv0", "rstd0")

                def turn(trip):
                    for l in (0, 1):
                        sc.wait_ge(*pe_ahead.at("hT", trip, l))
                        sc.activation(hT[l][:], ps[l][:, 0, 0:T], ACT.Copy).then_inc(*act_ahead.did("hT", l))

                def attend(trip, more):
                    for l in (0, 1):
                        sc.wait_ge(*pe.at("qk", trip, l))
                        sc.activation(sq[l][:].rearrange("p h e -> p (h e)"),
                                      ps[l][:, 1:3].rearrange("p a n -> p (a n)"), ACT.Square).then_inc(*act.did("sq", l))
                        sc.wait_ge(*pe.at("v", trip, l))
                        sc.activation(val[l][:], ps[l][:, 3], ACT.Copy).then_inc(*act.did("v", l))
                        sc.wait_ge(*vec.at("ssm", trip, l))
                        sc.activation(ss[l][:, 1], ss[l][:, 0], ACT.Ln, scale=2.0 ** 20).then_inc(*act.did("lnn", l))
                        sc.wait_ge(*act.at("lnn", trip, l))
                        sc.activation(ss[l][:, 2], ss[l][:, 1], ACT.Exp, scale=-0.5, bias=lnscale[:]
                                      ).then_inc(*act.did("rn", l))
                    for l in (0, 1):
                        sc.wait_ge(*pe.at("qkT", trip, l))
                        sc.activation(qT[l][:].rearrange("p j t -> p (j t)"), ps[l][:, 0], ACT.Copy
                                      ).then_inc(*act.did("qT", l))
                        sc.activation(kT[l][0:HD, :, 0], ps[l][0:HD, 1].rearrange("p (j t) -> p j t", t=T), ACT.Copy
                                      ).then_inc(*act.did("kT", l))
                    for l in (0, 1):
                        sc.wait_ge(*vec.at("mx", trip, l))
                        for h in range(H):
                            sc.activation(prob[l][:, h], prob[l][:, h], ACT.Exp, bias=mx[l][:, h:h + 1],
                                          accum_out=sm[l][:, 0, h:h + 1]).then_inc(*act.did(f"exp{h}", l))
                    for l in (0, 1):
                        sc.wait_ge(*pe.at("pT", trip, l))
                        sc.activation(probT[l][:, 0:4].rearrange("p h t -> p (h t)"), ps[l][:, 0], ACT.Copy
                                      ).then_inc(*act.did("pT", l))
                    for l in (0, 1):
                        sc.wait_ge(*pe.at("o", trip, l))
                        sc.activation(oT[l][:].rearrange("p j t -> p (j t)"), ps[l][:, 2], ACT.Copy
                                      ).then_inc(*act.did("oT", l))
                    if more:
                        normalise(trip + 1)
                    if more:
                        turn(trip + 1)
                    for l in (0, 1):
                        sc.wait_ge(*vec.at("mv2", trip, l))
                        rsqrt_of_variance(sc, act, trip, l, rstd[l], mv[l], eps)

                normalise(0)
                turn(0)
                with sc.Fori(0, TRIPS - 1) as trip:
                    attend(trip, True)
                attend(TRIPS - 1, False)

            @block.tensor
            def _(te):
                pe.start(te)
                pe_ahead.start(te)
                te.wait_ge(loaded, NLOAD)
                te.wait_ge(zeroed, NZERO)

                def turn(trip):
                    for l in (0, 1):
                        if first:
                            te.wait_ge(*vec_ahead.at("y0", trip, l))
                        else:
                            te.wait_ge(y_in[l], trip * 16 + 16)
                        te.wait_ge(*vec.at("y", trip, l, ago=1))
                        te.transpose(ps[l][:, 0, 0:T], yc[l][:], g.ident[:])
                        te.matmul(ps[l][HALF:C, 0, 0:T], yc[l][:, HALF:C], g.shift[:], start=True, stop=True
                                  ).then_inc(*pe_ahead.did("hT", l))

                def attend(trip, more):
                    for l in (0, 1):
                        te.wait_ge(*act_ahead.at("hT", trip, l))
                        for a in (0, 1):
                            mm = te.matmul(ps[l][:, 1 + a], hT[l][:], wqkv[:, a], start=True, stop=True)
                        mm.then_inc(*pe.did("qk", l))
                        te.wait_ge(*vec.at("hn1", trip, l, ago=1))
                        te.matmul(ps[l][:, 3], hT[l][:], wqkv[:, 2], start=True, stop=True).then_inc(*pe.did("v", l))
                    for l in (0, 1):
                        te.wait_ge(*pool.at("qrot", trip, l))
                        te.wait_ge(*vec.at("kn", trip, l))
                        for a in (0, 1):
                            for j in range(PAIRS):
                                mm = te.transpose(ps[l][:, a, T * j:T * j + T],
                                                  rc[l][:, a, 2 * j:2 * j + 2].rearrange("p h e -> p (h e)"), g.ident[:])
                        mm.then_inc(*pe.did("qkT", l))
                        te.wait_ge(*act.at("kT", trip, l))
                        te.wait_ge(*vec.at("kT", trip, l))
                        for j in range(PAIRS):
                            mm = te.matmul(ps[l][:, 2 + j // 2, 2 * T * (j % 2):2 * T * (j % 2) + 2 * T], qT[l][:, j],
                                           kT[l][:, j].rearrange("p a t -> p (a t)"), start=True, stop=True)
                        mm.then_inc(*pe.did("s", l))
                    for l in (0, 1):
                        te.wait_ge(*pool.at("norm", trip, l))
                        te.wait_ge(*vec.at("norm", trip, l))
                        for h in range(H):
                            mm = te.transpose(ps[l][:, h // 4, T * (h % 4):T * (h % 4) + T], prob[l][:, h], g.ident[:])
                        mm.then_inc(*pe.did("pT", l))
                    for l in (0, 1):
                        te.wait_ge(*act.at("pT", trip, l))
                        te.wait_ge(*vec.at("pT", trip, l))
                        for h in range(H):
                            rows = slice(64 * (h % 2), 64 * (h % 2) + 64)
                            mm = te.matmul(ps[l][rows, 2, T * (h // 2):T * (h // 2) + T], val[l][:, HD * h:HD * h + HD],
                                           probT[l][:, h], start=True, stop=True)
                        mm.then_inc(*pe.did("o", l))
                    for l in (0, 1):
                        te.wait_ge(*act.at("oT", trip, l))
                        for j in range(PAIRS):
                            mm = te.matmul(ps[l][:, 3, 0:C], oT[l][:, j], wo[:, j],
                                           start=(j == 0), stop=(j == PAIRS - 1))
                        mm.then_inc(*pe.did("ao", l))
                    if more:
                        turn(trip + 1)
                    for l in (0, 1):
                        te.wait_ge(*vec.at("y", trip, l))
                        te.matmul(ps[l][:, 3, C:C + HALF], g.shift[:], ynew[l][:, HALF:C], start=True, stop=True
                                  ).then_inc(*pe.did("sh", l))

                turn(0)
                with te.Fori(0, TRIPS - 1) as trip:
                    attend(trip, True)
                attend(TRIPS - 1, False)

            @block.vector
            def _(v):
                v.wait_ge(loaded, NLOAD)
                v.tensor_tensor(rot[:], rot[:], qks[:], ALU.mult).then_inc(prep, 1)
                vec.start(v)
                vec_ahead.start(v)
                v.wait_ge(prep, 1)
                one = lambda ap, trip, l: flat(ap[:, bass.ds(trip * 2 + l, 1), :])

                def measure(trip):
                    for l in ((0, 1) if first else ()):
                        v.wait_ge(y_in[l], trip * 16 + 16)
                        v.wait_ge(*vec_ahead.at("y0", trip, l, ago=1))
                        row_statistics(v, vec_ahead, trip, l, stats0[l][:], mv0[l], rstd0[l][:, 1:2], xin[l][:])

                def normalise(trip):
                    for l in ((0, 1) if first else ()):
                        v.wait_ge(*vec.at("y", trip, l, ago=1))
                        v.wait_ge(*act_ahead.at("rstd0", trip, l))
                        v.tensor_scalar(yc[l][:], xin[l][:], mv0[l][:, 0:1], rstd0[l][:, 1:2], ALU.subtract, ALU.mult
                                        ).then_inc(*vec_ahead.did("y0", l))

                def upper_keys(trip, l):
                    v.wait_ge(*pe.at("qkT", trip, l))
                    v.wait_ge(*act.at("qT", trip, l))
                    v.tensor_copy(kT[l][HD:2 * HD, :, 1], ps[l][HD:2 * HD, 1].rearrange("p (j t) -> p j t", t=T)
                                  ).then_inc(*vec.did("kT", l))

                def attend(trip, more):
                    for l in (0, 1):
                        tab = lambda trig, part: rot[:, :, trig, part].unsqueeze(2).to_broadcast(
                            [T, 2, H, part.stop - part.start])
                        lo, hi, whole = slice(0, HD // 2), slice(HD // 2, HD), slice(0, HD)
                        qk = ps[l][:, 1:3].rearrange("p a (h e) -> p a h e", e=HD)
                        v.wait_ge(*act.at("sq", trip, l))
                        v.tensor_reduce(ss[l][:, 0], sq[l][:], AX, ALU.add).then_inc(*vec.did("ss", l))
                        v.wait_ge(*vec.at("ss", trip, l))
                        v.tensor_scalar(ss[l][:, 0], ss[l][:, 0], 1e-24, None, ALU.max).then_inc(*vec.did("ssm", l))
                        v.tensor_tensor(rc[l][:], qk, tab(0, whole), ALU.mult).then_inc(*vec.did("cos", l))
                        v.tensor_tensor(rs[l][:, :, :, lo], qk[:, :, :, hi], tab(1, lo), ALU.mult
                                        ).then_inc(*vec.did("sin0", l))
                        v.tensor_tensor(rs[l][:, :, :, hi], qk[:, :, :, lo], tab(1, hi), ALU.mult
                                        ).then_inc(*vec.did("sin1", l))
                        if l == 1:
                            upper_keys(trip, 0)
                        v.wait_ge(*vec.at("sin1", trip, l))
                        v.tensor_tensor(rc[l][:, 1], rc[l][:, 1], rs[l][:, 1], ALU.add).then_inc(*vec.did("krot", l))
                        v.wait_ge(*vec.at("krot", trip, l))
                        v.wait_ge(*act.at("rn", trip, l))
                        v.tensor_tensor(rc[l][:, 1], rc[l][:, 1],
                                        ss[l][:, 2, H:2 * H].unsqueeze(2).to_broadcast([T, H, HD]), ALU.mult
                                        ).then_inc(*vec.did("kn", l))
                    upper_keys(trip, 1)
                    for l in (0, 1):
                        v.wait_ge(*pe.at("s", trip, l))
                        for h in range(H):
                            v.scalar_tensor_tensor(out=prob[l][:, h], in0=ps[l][:, 2 + h // 4, T * (h % 4):T * (h % 4) + T],
                                                   scalar=ss[l][:, 2, h:h + 1], in1=g.local[:], op0=ALU.mult,
                                                   op1=ALU.add).then_inc(*vec.did(f"s{h}", l))
                        v.wait_ge(*vec.at(f"s{H - 1}", trip, l))
                        v.tensor_reduce(mx[l][:], prob[l][:], AX, ALU.max, negate=True).then_inc(*vec.did("mx", l))
                    for l in (0, 1):
                        v.wait_ge(*act.at(f"exp{H - 1}", trip, l))
                        v.reciprocal(sm[l][:, 1], sm[l][:, 0]).then_inc(*vec.did("rsum", l))
                        v.wait_ge(*vec.at("rsum", trip, l))
                        v.tensor_tensor(prob[l][:, 0:PH], prob[l][:, 0:PH],
                                        sm[l][:, 1, 0:PH].unsqueeze(2).to_broadcast([T, PH, T]), ALU.mult
                                        ).then_inc(*vec.did("norm", l))
                    for l in (0, 1):
                        v.wait_ge(*pe.at("pT", trip, l))
                        v.tensor_copy(probT[l][:, 4:8].rearrange("p h t -> p (h t)"), ps[l][:, 1]
                                      ).then_inc(*vec.did("pT", l))
                    if more:
                        measure(trip + 1)
                    for l in (0, 1):
                        y = yc[l][:] if first else one(g.y, trip, l)
                        v.wait_ge(*pe.at("ao", trip, l))
                        v.tensor_tensor(ynew[l][:], y, ps[l][:, 3, 0:C], ALU.add).then_inc(*vec.did("ynew", l))
                        v.wait_ge(*vec.at("ynew", trip, l))
                        v.tensor_tensor(one(g.y, trip, l), y, ps[l][:, 3, 0:C], ALU.add).then_inc(*vec.did("y", l))
                    if more:
                        normalise(trip + 1)
                    for l in (0, 1):
                        v.wait_ge(*vec.at("ynew", trip, l))
                        v.bn_stats(stats[l][:, 0:6], ynew[l][:, 0:HALF]).then_inc(*vec.did("st1", l))
                        v.wait_ge(*pe.at("sh", trip, l))
                        v.bn_stats(stats[l][:, 6:12], ps[l][:, 3, C:C + HALF]).then_inc(*vec.did("st2", l))
                        v.wait_ge(*vec.at("st2", trip, l))
                        v.memset(rstd[l][:, 1:2], 0.0)
                        v.bn_aggr(mv[l][:], stats[l][:]).then_inc(*vec.did("mv2", l))
                    for l in (0, 1):
                        v.wait_ge(*act.at("rstd", trip, l))
                        v.tensor_scalar(one(g.hn[:, :, 0:HALF], trip, l), ynew[l][:, 0:HALF], mv[l][:, 0:1], rstd[l][:, 1:2],
                                        ALU.subtract, ALU.mult).then_inc(*vec.did("hn0", l))
                        v.tensor_scalar(one(g.hn[:, :, HALF:C], trip, l), ps[l][:, 3, C:C + HALF], mv[l][:, 0:1],
                                        rstd[l][:, 1:2], ALU.subtract, ALU.mult).then_inc(*vec.did("hn1", l))

                measure(0)
                normalise(0)
                with v.Fori(0, TRIPS - 1) as trip:
                    attend(trip, True)
                attend(TRIPS - 1, False)


def gated_mlp(nc, g, layer):
    HID = g.d["L0_ffn_w2"].shape[1]
    CH = -(-HID // 128)
    M = [min(128, HID - 128 * c) for c in range(CH)]
    N = 2 * T
    TRIPS = g.NB // 4
    d = g.d
    last = layer == 1
    with ExitStack() as stack:
        m = Memory(nc, stack, f"m{layer}")
        w1 = m.sb("w1", [C, 2, HID])
        b1 = m.sb("b1", [128, 2, CH])
        w2 = m.sb("w2", [128, CH, C])
        b2 = m.sb("b2", [T, C])
        lng, lnb = m.sb("lng", [C, 1]), m.sb("lnb", [C, 1])
        hin, ysum = (both(m, n, [T, 2, C]) for n in ("hin", "ysum"))
        hT = both(m, "hT", [C, N])
        gl, u = both(m, "gl", [128, CH, N]), both(m, "u", [128, CH, N])
        ps = [m.ps(f"ps{l}", [128, 4, 512]) for l in (0, 1)]
        loaded, zeroed = m.sem("loaded"), m.sem("zeroed")
        h_in = [m.sem(f"h_in{l}") for l in (0, 1)]
        vec = Steps([m.sem("vec_done")], ["hT", " ".join(f"u{c}" for c in range(CH)), "yb yx y" if last else "yb y"])
        act = Steps([m.sem("act_done")], [" ".join(f"g{c}" for c in range(CH))])
        pe = Steps([m.sem("pe_done")], ["hT", "ag", "o"])
        NZERO, NLOAD = 5, 16 * (6 + 2 * CH)

        with nc.Block() as block:
            @block.sync
            def _(sp):
                sp.wait_ge(zeroed, NZERO)
                sp.dma_start(w1[:], d["L0_ffn_w1"][layer].rearrange("c (a n) -> c a n", a=2)).then_inc(loaded, 16)
                sp.dma_start(b2[:], row_bc(d["L0_ffn_b2"][layer])).then_inc(loaded, 16)
                sp.dma_start(lng[:], d["L0_ffn_ln_g"][layer].unsqueeze(1)).then_inc(loaded, 16)
                sp.dma_start(lnb[:], d["L0_ffn_ln_b"][layer].unsqueeze(1)).then_inc(loaded, 16)
                whole = (CH - 1) * 128
                sp.dma_start(w2[:, 0:CH - 1], d["L0_ffn_w2"][layer, 0:whole].rearrange("(c p) n -> p c n", p=128)
                             ).then_inc(loaded, 16)
                sp.dma_start(w2[0:M[-1], CH - 1], d["L0_ffn_w2"][layer, whole:HID]).then_inc(loaded, 16)
                for c in range(CH):
                    for a in (0, 1):
                        row = d["L0_ffn_b1"][layer, HID * a + 128 * c:HID * a + 128 * c + M[c]]
                        sp.dma_start(b1[0:M[c], a, c:c + 1], row.unsqueeze(1)).then_inc(loaded, 16)
                with sp.Fori(0, TRIPS) as trip:
                    for l in (0, 1):
                        b = sp.snap(trip * 4 + 2 * l)
                        src = g.hn[:, bass.ds(b, 2), :]
                        sp.wait_ge(*pe.at("hT", trip, l, ago=1))
                        sp.dma_start(hin[l][:], src).then_inc(h_in[l], 16)

            @block.gpsimd
            def _(gp):
                gp.memset(w2[:], 0.0).then_inc(zeroed, 1)
                for l in (0, 1):
                    gp.memset(u[l][:, CH - 1], 0.0).then_inc(zeroed, 1)
                    gp.memset(gl[l][:, CH - 1], 0.0).then_inc(zeroed, 1)

            @block.scalar
            def _(sc):
                act.start(sc)
                sc.wait_ge(zeroed, NZERO)
                sc.wait_ge(loaded, NLOAD)
                with sc.Fori(0, TRIPS) as trip:
                    for l in (0, 1):
                        sc.wait_ge(*pe.at("ag", trip, l))
                        for c in range(CH):
                            sc.activation(gl[l][0:M[c], c], ps[l][0:M[c], c, N:2 * N], ACT.Gelu, bias=b1[0:M[c], 1, c:c + 1]
                                          ).then_inc(*act.did(f"g{c}", l))

            @block.tensor
            def _(te):
                pe.start(te)
                te.wait_ge(loaded, NLOAD)
                te.wait_ge(zeroed, NZERO)
                with te.Fori(0, TRIPS) as trip:
                    for l in (0, 1):
                        te.wait_ge(h_in[l], trip * 16 + 16)
                        te.wait_ge(*vec.at("y", trip, l, ago=1))
                        for i in (0, 1):
                            mm = te.transpose(ps[l][:, 3, T * i:T * i + T], hin[l][:, i], g.ident[:])
                        mm.then_inc(*pe.did("hT", l))
                    for l in (0, 1):
                        te.wait_ge(*vec.at("hT", trip, l))
                        for c in range(CH):
                            for a in (0, 1):
                                mm = te.matmul(ps[l][0:M[c], c, N * a:N * a + N], w1[:, a, 128 * c:128 * c + M[c]],
                                               hT[l][:], start=True, stop=True)
                        mm.then_inc(*pe.did("ag", l))
                    for l in (0, 1):
                        te.wait_ge(*vec.at(f"u{CH - 1}", trip, l))
                        for i in (0, 1):
                            for c in range(CH):
                                mm = te.matmul(ps[l][:, 3, N + T * i:N + T * i + T], u[l][:, c, T * i:T * i + T], w2[:, c],
                                               start=(c == 0), stop=(c == CH - 1))
                        mm.then_inc(*pe.did("o", l))

            @block.vector
            def _(v):
                vec.start(v)
                v.wait_ge(loaded, NLOAD)
                v.wait_ge(zeroed, NZERO)
                with v.Fori(0, TRIPS) as trip:
                    for l in (0, 1):
                        v.wait_ge(*pe.at("hT", trip, l))
                        v.tensor_scalar(hT[l][:], ps[l][:, 3, 0:N], lng[:, 0:1], lnb[:, 0:1], ALU.mult, ALU.add
                                        ).then_inc(*vec.did("hT", l))
                    for l in (0, 1):
                        for c in range(CH):
                            v.wait_ge(*act.at(f"g{c}", trip, l))
                            v.scalar_tensor_tensor(out=u[l][0:M[c], c], in0=ps[l][0:M[c], c, 0:N],
                                                   scalar=b1[0:M[c], 0, c:c + 1], in1=gl[l][0:M[c], c],
                                                   op0=ALU.add, op1=ALU.mult).then_inc(*vec.did(f"u{c}", l))
                    for l in (0, 1):
                        v.wait_ge(*pe.at("o", trip, l))
                        two = lambda ap: ap[:, bass.ds(trip * 4 + 2 * l, 2), :]
                        v.tensor_tensor(ysum[l][:], ps[l][:, 3, N:2 * N].rearrange("p (i c) -> p i c", c=C),
                                        b2[:].unsqueeze(1).to_broadcast([T, 2, C]), ALU.add).then_inc(*vec.did("yb", l))
                        v.wait_ge(*vec.at("yb", trip, l))
                        if last:
                            v.tensor_tensor(ysum[l][:], ysum[l][:], two(g.y), ALU.add).then_inc(*vec.did("yx", l))
                            v.wait_ge(*vec.at("yx", trip, l))
                        residual = g.x if last else g.y
                        v.tensor_tensor(two(residual), two(residual), ysum[l][:], ALU.add).then_inc(*vec.did("y", l))


def local_transformer(nc, g):
    with ExitStack() as stack:
        m = Memory(nc, stack, "lt")
        g.y, g.hn = m.sb("y", [T, g.NB, C]), m.sb("hn", [T, g.NB, C])
        for layer in (0, 1):
            local_attention(nc, g, layer)
            gated_mlp(nc, g, layer)


def mamba(nc, g):
    DIRS, TAPS, NH, HD, DS = 2, 4, 4, 64, 128
    DI = NH * HD
    PAIRS = DI // 128
    HEADS = DIRS * NH
    PAD = TAPS - 1
    TERMS = 7
    TRIPS = g.NB // 2
    d = g.d
    names = ("L1_attn_fwd_", "L1_attn_bwd_")
    with ExitStack() as stack:
        m = Memory(nc, stack, "mb")
        wx = m.sb("wx", [C, DIRS, TAPS, DI])
        wbc = m.sb("wbc", [C, DIRS, TAPS, 2, DS])
        wz = m.sb("wz", [C, DIRS, PAIRS, 128])
        wdt = m.sb("wdt", [C, HEADS])
        wout = m.sb("wout", [128, DIRS, PAIRS, C])
        cbx, cbbc = m.sb("cbx", [T, DIRS, DI]), m.sb("cbbc", [DS, DIRS, 2])
        dtb, nega = m.sb("dtb", [T, HEADS]), m.sb("nega", [T, HEADS])
        dcol, ddiag = m.sb("dcol", [T, HEADS]), m.sb("ddiag", [T, HEADS, T])
        beyond, upto = m.sb("beyond", [T, DIRS, T]), m.sb("upto", [T, DIRS, T])
        projb = m.sb("projb", [T, C])
        eps = m.sb("eps", [128, 1])

        with ExitStack() as once:
            mo = Memory(nc, once, "mw")
            win = mo.sb("win", [128, DIRS, 6, C])
            wind = mo.sb("wind", [NH, DIRS, C])
            cw = mo.sb("cw", [128, DIRS, 4, TAPS])
            tapped = mo.sb("tapped", [128, DIRS, 4, TAPS, C])
            nw, ow = mo.sb("nw", [C, 1]), mo.sb("ow", [128, DIRS, PAIRS])
            wo, proj, projT = mo.sb("wo", [C, DIRS, DI]), mo.sb("proj", [C, DIRS, C]), mo.sb("projT", [C, DIRS, C])
            pw = mo.ps("pw", [128, 8, 512])
            loaded, made, masks = mo.sem("loaded"), mo.sem("made"), mo.sem("masks")
            tap, turned, kept = mo.sem("tap"), mo.sem("turned"), mo.sem("kept")
            NL = 16 * (2 + DIRS + DIRS * 12)

            with nc.Block() as block:
                @block.sync
                def _(sp):
                    sp.dma_start(nw[:], d["L1_attn_norm_weight"].unsqueeze(1)).then_inc(loaded, 16)
                    sp.dma_start(projb[:], row_bc(d["L1_attn_proj_b"])).then_inc(loaded, 16)
                    for k in range(DIRS):
                        sp.dma_start(proj[:, k], d["L1_attn_proj_W"][:, C * k:C * k + C]).then_inc(loaded, 16)
                    for k, n in enumerate(names):
                        sp.dma_start(win[:, k], d[n + "W_in"][0:768].rearrange("(a p) c -> p a c", p=128)
                                     ).then_inc(loaded, 16)
                        sp.dma_start(wind[:, k], d[n + "W_in"][768:768 + NH]).then_inc(loaded, 16)
                        sp.dma_start(cw[:, k], d[n + "conv_w"].rearrange("(a p) j -> p a j", p=128)).then_inc(loaded, 16)
                        sp.dma_start(cbx[:, k], row_bc(d[n + "conv_b"][0:DI])).then_inc(loaded, 16)
                        for a in (0, 1):
                            sp.dma_start(cbbc[:, k, a:a + 1],
                                         d[n + "conv_b"][DI + DS * a:DI + DS * a + DS].unsqueeze(1)).then_inc(loaded, 16)
                            sp.dma_start(ow[:, k, a:a + 1], d[n + "norm_w"][128 * a:128 * a + 128].unsqueeze(1)
                                         ).then_inc(loaded, 16)
                        heads = slice(NH * k, NH * k + NH)
                        sp.dma_start(dtb[:, heads], row_bc(d[n + "dt_bias"])).then_inc(loaded, 16)
                        sp.dma_start(nega[:, heads], row_bc(d[n + "A_log"])).then_inc(loaded, 16)
                        sp.dma_start(dcol[:, heads], row_bc(d[n + "D"])).then_inc(loaded, 16)
                        sp.dma_start(wo[:, k], d[n + "W_out"]).then_inc(loaded, 16)

                @block.gpsimd
                def _(gp):
                    gp.memset(beyond[:], 1.0).then_inc(masks, 1)
                    gp.memset(upto[:], 1.0).then_inc(masks, 1)
                    gp.memset(eps[:], LN_EPS).then_inc(masks, 1)
                    gp.wait_ge(masks, 3)
                    for k, sign in enumerate((1, -1)):
                        gp.affine_select(out=beyond[:, k], in_=beyond[:, k], compare_op=ALU.is_gt, fill=0.0, base=0,
                                         pattern=[[-sign, T]], channel_multiplier=sign).then_inc(masks, 1)
                        gp.affine_select(out=upto[:, k], in_=upto[:, k], compare_op=ALU.is_ge, fill=0.0, base=0,
                                         pattern=[[sign, T]], channel_multiplier=-sign).then_inc(masks, 1)

                @block.scalar
                def _(sc):
                    sc.preload_act_table_set("natural_log_exp_and_others")
                    sc.wait_ge(loaded, NL)
                    sc.activation(nega[:], nega[:], ACT.Exp).then_inc(made, 1)
                    sc.wait_ge(made, 1)
                    sc.mul(nega[:], nega[:], -1.0).then_inc(made, 1)

                @block.vector
                def _(v):
                    v.wait_ge(loaded, NL)
                    for k in range(DIRS):
                        for a in range(4):
                            for j in range(TAPS):
                                v.tensor_scalar(tapped[:, k, a, j], win[:, k, 2 + a], cw[:, k, a, j:j + 1], None,
                                                ALU.mult).then_inc(tap, 1)
                    for h in range(HEADS):
                        v.tensor_scalar(ddiag[:, h], g.ident[:], dcol[:, h:h + 1], None, ALU.mult).then_inc(kept, 1)
                    bank = lambda b: pw[:, b].rearrange("p (a c) -> p a c", c=128)
                    v.wait_ge(turned, 1)
                    for k in range(DIRS):
                        for j in range(TAPS):
                            src = bank(4 * k + j)
                            v.tensor_scalar(wx[:, k, j].rearrange("p (a c) -> p a c", c=128), src[:, 0:2], nw[:, 0:1],
                                            None, ALU.mult).then_inc(kept, 1)
                            v.tensor_scalar(wbc[:, k, j], src[:, 2:4], nw[:, 0:1], None, ALU.mult).then_inc(kept, 1)
                    v.wait_ge(turned, 2)
                    v.tensor_scalar(wz[:].rearrange("p k a c -> p (k a) c"), bank(0), nw[:, 0:1], None, ALU.mult
                                    ).then_inc(kept, 1)
                    v.tensor_scalar(wdt[:], pw[:, 1, 0:HEADS], nw[:, 0:1], None, ALU.mult).then_inc(kept, 1)
                    v.tensor_copy(projT[:], bank(2)[:, 0:2]).then_inc(kept, 1)
                    v.wait_ge(turned, 3)
                    for k in range(DIRS):
                        for a in range(PAIRS):
                            v.tensor_scalar(wout[:, k, a], bank(3)[:, 2 * k + a], ow[:, k, a:a + 1], None, ALU.mult
                                            ).then_inc(kept, 1)

                @block.tensor
                def _(te):
                    KEPT = HEADS + 2 * DIRS * TAPS
                    te.wait_ge(tap, DIRS * 4 * TAPS)
                    for k in range(DIRS):
                        for j in range(TAPS):
                            for a in range(4):
                                mm = te.transpose(pw[:, 4 * k + j, 128 * a:128 * a + 128], tapped[:, k, a, j], g.ident[:])
                    mm.then_inc(turned, 1)
                    te.wait_ge(kept, KEPT)
                    for k in range(DIRS):
                        for a in range(PAIRS):
                            te.transpose(pw[:, 0, 128 * (2 * k + a):128 * (2 * k + a) + 128], win[:, k, a], g.ident[:])
                        te.transpose(pw[:, 1, NH * k:NH * k + NH], wind[:, k], g.ident[0:NH, 0:NH])
                        mm = te.transpose(pw[:, 2, C * k:C * k + C], proj[:, k], g.ident[:])
                    mm.then_inc(turned, 1)
                    te.wait_ge(kept, KEPT + 3)
                    for k in range(DIRS):
                        for a in range(PAIRS):
                            mm = te.matmul(pw[:, 3, 128 * (2 * k + a):128 * (2 * k + a) + 128],
                                           wo[:, k, 128 * a:128 * a + 128], projT[:, k], start=True, stop=True)
                    mm.then_inc(turned, 1)

        xin, xr, r, xn = (both(m, n, [T, C]) for n in ("xin", "xr", "r", "xn"))
        stats, mv, rstd = both(m, "stats", [T, 6]), both(m, "mv", [T, 2]), both(m, "rstd", [T, 2])
        rms = both(m, "rms", [T, 3])
        xT = both(m, "xT", [C, PAD + T + PAD])
        dts = both(m, "dts", [T, 8, HEADS])
        dt, dta = both(m, "dt", [T, HEADS]), both(m, "dta", [T, HEADS])
        xs = both(m, "xs", [T, DIRS, DI])
        bc = both(m, "bc", [DS, DIRS, 2, T])
        zs = both(m, "zs", [128, DIRS * PAIRS, T])
        steps_a = both(m, "steps_a", [T, HEADS, T])
        gm, km = both(m, "gm", [T, DIRS, T]), both(m, "km", [T, HEADS, T])
        decay = both(m, "decay", [T, HEADS, T])
        u, usq = both(m, "u", [128, DIRS * PAIRS, T]), both(m, "usq", [128, DIRS * PAIRS, T])
        scale = both(m, "scale", [T, 2, DIRS])
        acc = both(m, "acc", [T, C])
        ps = [m.ps(f"ps{l}", [128, 4, 512]) for l in (0, 1)]
        zeroed = m.sem("zeroed")
        x_in = [m.sem(f"x_in{l}") for l in (0, 1)]
        series = " ".join(f"p{n}" for n in range(TERMS, 0, -1))
        vec = Steps([m.sem("vec_done")], [
            "xb v av", f"den rden z z2 {series} pz relu dt dta",
            " ".join(f"a{h}" for h in range(HEADS)), "gm " + " ".join(f"k{h}" for h in range(HEADS)),
            "m", "u", "acc x"])
        vec_ahead = Steps([m.sem("vec_ahead_done")], ["stats mv", "q", "r xn"])
        act = Steps([m.sem("act_done")], ["eu", "sx sb0 sb1 sb2 sb3 sz", "decay", "usq", "lns rs"])
        act_ahead = Steps([m.sem("act_ahead_done")], ["lnv rstd", "lnq rms", "xT"])
        pe = Steps([m.sem("pe_done")], ["x dt bc z", "g seg", "y", "out"])
        pe_ahead = Steps([m.sem("pe_ahead_done")], ["xT"])
        pool = Steps([m.sem("pool_done")], ["xp xr"])

        with nc.Block() as block:
            @block.sync
            def _(sp):
                with sp.Fori(0, TRIPS) as trip:
                    for l in (0, 1):
                        src = flat(g.x[:, bass.ds(sp.snap(trip * 2 + l), 1), :])
                        sp.wait_ge(*vec.at("xb", trip, l, ago=1))
                        sp.dma_start(xin[l][:], src).then_inc(x_in[l], 16)

            @block.gpsimd
            def _(gp):
                for l in (0, 1):
                    gp.memset(xT[l][:], 0.0).then_inc(zeroed, 1)
                pool.start(gp)
                with gp.Fori(0, TRIPS) as trip:
                    for l in (0, 1):
                        gp.wait_ge(*vec.at("acc", trip, l, ago=1))
                        gp.wait_ge(*vec_ahead.at("r", trip, l))
                        gp.tensor_tensor(xr[l][:], xin[l][:], projb[:], ALU.add).then_inc(*pool.did("xp", l))
                        gp.wait_ge(*pool.at("xp", trip, l))
                        gp.tensor_tensor(xr[l][:], xr[l][:], r[l][:], ALU.add).then_inc(*pool.did("xr", l))

            @block.scalar
            def _(sc):
                act.start(sc)
                act_ahead.start(sc)
                sc.wait_ge(zeroed, 2)
                two = lambda ap: ap.rearrange("p a c -> p (a c)")

                def normalise(trip):
                    for l in (0, 1):
                        sc.wait_ge(*vec_ahead.at("mv", trip, l))
                        rsqrt_of_variance(sc, act_ahead, trip, l, rstd[l], mv[l], eps)
                    for l in (0, 1):
                        sc.wait_ge(*vec_ahead.at("q", trip, l))
                        sc.activation(rms[l][:, 1:2], rms[l][:, 0:1], ACT.Ln, bias=eps[:]).then_inc(*act_ahead.did("lnq", l))
                        sc.wait_ge(*act_ahead.at("lnq", trip, l))
                        sc.activation(rms[l][:, 2:3], rms[l][:, 1:2], ACT.Exp, scale=-0.5).then_inc(*act_ahead.did("rms", l))

                def turn(trip):
                    for l in (0, 1):
                        sc.wait_ge(*pe_ahead.at("xT", trip, l))
                        sc.activation(xT[l][:, PAD:PAD + T], ps[l][:, 1, 0:T], ACT.Copy).then_inc(*act_ahead.did("xT", l))

                def mix(trip, more):
                    for l in (0, 1):
                        sc.wait_ge(*vec.at("av", trip, l))
                        sc.activation(dts[l][:, 2], dts[l][:, 1], ACT.Exp).then_inc(*act.did("eu", l))
                    sc.preload_act_table_set("silu_and_others")
                    for l in (0, 1):
                        sc.wait_ge(*vec.at("xb", trip, l))
                        sc.activation(two(xs[l][:]), two(xs[l][:]), ACT.Silu).then_inc(*act.did("sx", l))
                        sc.wait_ge(*pe.at("bc", trip, l))
                        for i in range(4):
                            k, a = i // 2, i % 2
                            sc.activation(bc[l][:, k, a], ps[l][:, 1, T * i:T * i + T], ACT.Silu,
                                          bias=cbbc[:, k, a:a + 1]).then_inc(*act.did(f"sb{i}", l))
                        sc.wait_ge(*pe.at("z", trip, l))
                        sc.activation(two(zs[l][:]), ps[l][:, 2], ACT.Silu).then_inc(*act.did("sz", l))
                    sc.preload_act_table_set("natural_log_exp_and_others")
                    for l in (0, 1):
                        sc.wait_ge(*pe.at("seg", trip, l))
                        sc.activation(two(decay[l][:]), two(ps[l][:, 0:2]), ACT.Exp).then_inc(*act.did("decay", l))
                    for l in (0, 1):
                        sc.wait_ge(*vec.at("u", trip, l))
                        sc.activation(two(usq[l][:]), two(u[l][:]), ACT.Square).then_inc(*act.did("usq", l))
                    if more:
                        normalise(trip + 1)
                    for l in (0, 1):
                        sc.wait_ge(*pe.at("out", trip, l))
                        sc.activation(scale[l][:, 0], ps[l][:, 3, 0:2 * C:C], ACT.Ln, bias=eps[:], scale=1.0 / DI
                                      ).then_inc(*act.did("lns", l))
                        sc.wait_ge(*act.at("lns", trip, l))
                        sc.activation(scale[l][:, 1], scale[l][:, 0], ACT.Exp, scale=-0.5).then_inc(*act.did("rs", l))
                    if more:
                        turn(trip + 1)

                normalise(0)
                turn(0)
                with sc.Fori(0, TRIPS - 1) as trip:
                    mix(trip, True)
                mix(TRIPS - 1, False)

            @block.tensor
            def _(te):
                pe.start(te)
                pe_ahead.start(te)
                te.wait_ge(zeroed, 2)
                starts = [[j for j in range(TAPS)], [2 * PAD - j for j in range(TAPS)]]

                def turn(trip):
                    for l in (0, 1):
                        te.wait_ge(*vec_ahead.at("xn", trip, l))
                        te.transpose(ps[l][:, 1, 0:T], xn[l][:], g.ident[:]).then_inc(*pe_ahead.did("xT", l))

                def mix(trip, more):
                    for l in (0, 1):
                        here = xT[l][:, PAD:PAD + T]
                        te.wait_ge(*act_ahead.at("xT", trip, l))
                        for k in range(DIRS):
                            for j in range(TAPS):
                                s = starts[k][j]
                                mm = te.matmul(ps[l][:, 0, DI * k:DI * k + DI], xT[l][:, s:s + T], wx[:, k, j],
                                               start=(j == 0), stop=(j == TAPS - 1))
                        mm.then_inc(*pe.did("x", l))
                        te.wait_ge(*vec.at("x", trip, l, ago=1))
                        te.matmul(ps[l][:, 3, T:T + HEADS], here, wdt[:], start=True, stop=True).then_inc(*pe.did("dt", l))
                        for i in range(4):
                            k, a = i // 2, i % 2
                            for j in range(TAPS):
                                s = starts[k][j]
                                mm = te.matmul(ps[l][:, 1, T * i:T * i + T], wbc[:, k, j, a], xT[l][:, s:s + T],
                                               start=(j == 0), stop=(j == TAPS - 1))
                        mm.then_inc(*pe.did("bc", l))
                        for i in range(4):
                            mm = te.matmul(ps[l][:, 2, T * i:T * i + T], wz[:, i // 2, i % 2], here,
                                           start=True, stop=True)
                        mm.then_inc(*pe.did("z", l))
                    for l in (0, 1):
                        te.wait_ge(*act.at("sb3", trip, l))
                        for k in range(DIRS):
                            mm = te.matmul(ps[l][:, 3, 256 + T * k:256 + T * k + T], bc[l][:, k, 0], bc[l][:, k, 1],
                                           start=True, stop=True)
                        mm.then_inc(*pe.did("g", l))
                        te.wait_ge(*vec.at(f"a{HEADS - 1}", trip, l))
                        for h in range(HEADS):
                            mm = te.matmul(ps[l][:, h // NH, T * (h % NH):T * (h % NH) + T], steps_a[l][:, h],
                                           upto[:, h // NH], start=True, stop=True)
                        mm.then_inc(*pe.did("seg", l))
                    for l in (0, 1):
                        te.wait_ge(*act.at("sz", trip, l))
                        te.wait_ge(*vec.at("m", trip, l))
                        for h in range(HEADS):
                            rows = slice(64 * (h % 2), 64 * (h % 2) + 64)
                            mm = te.matmul(ps[l][rows, 2, T * (h // 2):T * (h // 2) + T],
                                           xs[l][:, h // NH, HD * (h % NH):HD * (h % NH) + HD], decay[l][:, h],
                                           start=True, stop=True)
                        mm.then_inc(*pe.did("y", l))
                    for l in (0, 1):
                        te.wait_ge(*act.at("usq", trip, l))
                        for k in range(DIRS):
                            for a in range(PAIRS):
                                te.matmul(ps[l][:, 3, C * k:C * k + C], usq[l][:, 2 * k + a], g.ones[:],
                                          start=(a == 0), stop=(a == PAIRS - 1))
                        for k in range(DIRS):
                            for a in range(PAIRS):
                                mm = te.matmul(ps[l][:, 3, C * (2 + k):C * (2 + k) + C], u[l][:, 2 * k + a],
                                               wout[:, k, a], start=(a == 0), stop=(a == PAIRS - 1))
                        mm.then_inc(*pe.did("out", l))
                    if more:
                        turn(trip + 1)

                turn(0)
                with te.Fori(0, TRIPS - 1) as trip:
                    mix(trip, True)
                mix(TRIPS - 1, False)

            @block.vector
            def _(v):
                vec.start(v)
                vec_ahead.start(v)
                v.wait_ge(zeroed, 2)
                coefficient = lambda n: 1.0 / (2 * n + 1)
                two = lambda ap: ap.rearrange("p a c -> p (a c)")

                def normalise(trip):
                    for l in (0, 1):
                        v.wait_ge(x_in[l], trip * 16 + 16)
                        v.wait_ge(*vec_ahead.at("xn", trip, l, ago=1))
                        row_statistics(v, vec_ahead, trip, l, stats[l][:], mv[l], rstd[l][:, 1:2], xin[l][:])
                    for l in (0, 1):
                        v.wait_ge(*act_ahead.at("rstd", trip, l))
                        v.scalar_tensor_tensor(out=rms[l][:, 0:1], in0=rstd[l][:, 1:2], scalar=rstd[l][:, 1:2],
                                               in1=mv[l][:, 1:2], op0=ALU.mult, op1=ALU.mult).then_inc(*vec_ahead.did("q", l))
                    for l in (0, 1):
                        v.tensor_scalar(r[l][:], xin[l][:], mv[l][:, 0:1], rstd[l][:, 1:2], ALU.subtract, ALU.mult
                                        ).then_inc(*vec_ahead.did("r", l))
                        v.wait_ge(*vec_ahead.at("r", trip, l))
                        v.wait_ge(*act_ahead.at("rms", trip, l))
                        v.tensor_scalar(xn[l][:], r[l][:], rms[l][:, 2:3], None, ALU.mult).then_inc(*vec_ahead.did("xn", l))

                def mix(trip, more):
                    for l in (0, 1):
                        v.wait_ge(*pool.at("xr", trip, l))
                        v.wait_ge(*pe.at("dt", trip, l))
                        v.tensor_tensor(two(xs[l][:]), ps[l][:, 0], two(cbx[:]), ALU.add).then_inc(*vec.did("xb", l))
                        v.tensor_tensor(dts[l][:, 0], ps[l][:, 3, T:T + HEADS], dtb[:], ALU.add
                                        ).then_inc(*vec.did("v", l))
                        v.wait_ge(*vec.at("v", trip, l))
                        v.scalar_tensor_tensor(out=dts[l][:, 1], in0=dts[l][:, 0], scalar=-1.0, in1=dts[l][:, 0],
                                               op0=ALU.mult, op1=ALU.min).then_inc(*vec.did("av", l))
                    for l in (0, 1):
                        row = lambda n: dts[l][:, n]
                        v.wait_ge(*act.at("eu", trip, l))
                        v.tensor_scalar(row(3), row(2), 2.0, None, ALU.add).then_inc(*vec.did("den", l))
                        v.wait_ge(*vec.at("den", trip, l))
                        v.reciprocal(row(4), row(3)).then_inc(*vec.did("rden", l))
                        v.wait_ge(*vec.at("rden", trip, l))
                        v.tensor_tensor(row(5), row(2), row(4), ALU.mult).then_inc(*vec.did("z", l))
                        v.wait_ge(*vec.at("z", trip, l))
                        v.tensor_tensor(row(6), row(5), row(5), ALU.mult).then_inc(*vec.did("z2", l))
                        v.wait_ge(*vec.at("z2", trip, l))
                        v.tensor_scalar(row(7), row(6), coefficient(TERMS), None, ALU.mult
                                        ).then_inc(*vec.did(f"p{TERMS}", l))
                        for n in range(TERMS - 1, 0, -1):
                            v.wait_ge(*vec.at(f"p{n + 1}", trip, l))
                            v.scalar_tensor_tensor(out=row(7), in0=row(7), scalar=coefficient(n), in1=row(6),
                                                   op0=ALU.add, op1=ALU.mult).then_inc(*vec.did(f"p{n}", l))
                        v.wait_ge(*vec.at("p1", trip, l))
                        v.scalar_tensor_tensor(out=row(7), in0=row(7), scalar=1.0, in1=row(5), op0=ALU.add,
                                               op1=ALU.mult).then_inc(*vec.did("pz", l))
                        v.tensor_scalar(row(3), row(0), 0.0, None, ALU.max).then_inc(*vec.did("relu", l))
                        v.wait_ge(*vec.at("relu", trip, l))
                        v.scalar_tensor_tensor(out=dt[l][:], in0=row(7), scalar=2.0, in1=row(3), op0=ALU.mult,
                                               op1=ALU.add).then_inc(*vec.did("dt", l))
                        v.wait_ge(*vec.at("dt", trip, l))
                        v.tensor_tensor(dta[l][:], dt[l][:], nega[:], ALU.mult).then_inc(*vec.did("dta", l))
                    for l in (0, 1):
                        v.wait_ge(*vec.at("dta", trip, l))
                        for h in range(HEADS):
                            v.tensor_scalar(steps_a[l][:, h], beyond[:, h // NH], dta[l][:, h:h + 1], None, ALU.mult
                                            ).then_inc(*vec.did(f"a{h}", l))
                    for l in (0, 1):
                        v.wait_ge(*pe.at("g", trip, l))
                        v.tensor_tensor(gm[l][:], ps[l][:, 3, 256:512].rearrange("p (k t) -> p k t", t=T), upto[:],
                                        ALU.mult).then_inc(*vec.did("gm", l))
                        v.wait_ge(*vec.at("gm", trip, l))
                        for h in range(HEADS):
                            v.scalar_tensor_tensor(out=km[l][:, h], in0=gm[l][:, h // NH], scalar=dt[l][:, h:h + 1],
                                                   in1=ddiag[:, h], op0=ALU.mult, op1=ALU.add
                                                   ).then_inc(*vec.did(f"k{h}", l))
                    for l in (0, 1):
                        v.wait_ge(*vec.at(f"k{HEADS - 1}", trip, l))
                        v.wait_ge(*act.at("decay", trip, l))
                        v.tensor_tensor(two(decay[l][:]), two(decay[l][:]), two(km[l][:]), ALU.mult
                                        ).then_inc(*vec.did("m", l))
                    for l in (0, 1):
                        v.wait_ge(*pe.at("y", trip, l))
                        v.tensor_tensor(two(u[l][:]), ps[l][:, 2], two(zs[l][:]), ALU.mult).then_inc(*vec.did("u", l))
                    if more:
                        normalise(trip + 1)
                    for l in (0, 1):
                        v.wait_ge(*act.at("rs", trip, l))
                        v.scalar_tensor_tensor(out=acc[l][:], in0=ps[l][:, 3, 2 * C:3 * C], scalar=scale[l][:, 1, 0:1],
                                               in1=xr[l][:], op0=ALU.mult, op1=ALU.add).then_inc(*vec.did("acc", l))
                        v.wait_ge(*vec.at("acc", trip, l))
                        v.scalar_tensor_tensor(out=flat(g.x[:, bass.ds(trip * 2 + l, 1), :]),
                                               in0=ps[l][:, 3, 3 * C:4 * C], scalar=scale[l][:, 1, 1:2],
                                               in1=acc[l][:], op0=ALU.mult, op1=ALU.add).then_inc(*vec.did("x", l))

                normalise(0)
                with v.Fori(0, TRIPS - 1) as trip:
                    mix(trip, True)
                mix(TRIPS - 1, False)


def context_attention(nc, g):
    H, HD, CD, S = 16, 8, g.d["ctx_512"].shape[2], g.d["ctx_512"].shape[1]
    TRIPS = g.NB // 2
    SCALE = float(HD) ** -0.5
    d = g.d
    with ExitStack() as stack:
        m = Memory(nc, stack, "xa")
        wq, wk, wv, wo = m.sb("wq", [C, C]), m.sb("wk", [CD, C]), m.sb("wv", [CD, C]), m.sb("wo", [C, C])
        bq, bk = m.sb("bq", [C, 1]), m.sb("bk", [C, 1])
        bv, bo = m.sb("bv", [T, C]), m.sb("bo", [T, C])
        hmask = m.sb("hmask", [C, H])
        eps = m.sb("eps", [128, 1])
        xin, xb, xn = (both(m, n, [T, C]) for n in ("xin", "xb", "xn"))
        stats, mv, rstd = both(m, "stats", [T, 6]), both(m, "mv", [T, 2]), both(m, "rstd", [T, 2])
        xnT, qT = both(m, "xnT", [C, T]), both(m, "qT", [C, T])
        ctx, ctxT = both(m, "ctx", [S, CD]), both(m, "ctxT", [CD, S])
        kT = both(m, "kT", [C, S])
        kblock = both(m, "kblock", [C, H, S])
        vpad = both(m, "vpad", [128, H, C])
        prob = both(m, "prob", [T, H, S])
        mx, sm = both(m, "mx", [T, H]), both(m, "sm", [T, 2, H])
        probT = both(m, "probT", [128, H, T])
        att, attT = both(m, "att", [T, C]), both(m, "attT", [C, T])
        ps = [m.ps(f"ps{l}", [128, 4, 512]) for l in (0, 1)]
        loaded, zeroed, prep, scaled = (m.sem(n) for n in ("loaded", "zeroed", "prep", "scaled"))
        x_in = [m.sem(f"x_in{l}") for l in (0, 1)]
        c_in = [m.sem(f"c_in{l}") for l in (0, 1)]
        vec = Steps([m.sem("vec_done")], ["v", "kb", "mx sub", "pT", "sum rsum", "att", "x"])
        vec_ahead = Steps([m.sem("vec_ahead_done")], ["stats mv", "xn"])
        act = Steps([m.sem("act_done")], ["qT kT", "exp", "pT", "attT"])
        act_ahead = Steps([m.sem("act_ahead_done")], ["lnv rstd", "xnT cT"])
        pe = Steps([m.sem("pe_done")], ["qkv", "s", "pT", "pv", "attT", "y"])
        pe_ahead = Steps([m.sem("pe_ahead_done")], ["xnT"])
        pool = Steps([m.sem("pool_done")], ["xb", "kb"])
        NZERO, NLOAD = 6, 8 * 16
        KP = 11

        with nc.Block() as block:
            @block.sync
            def _(sp):
                for buf, src in ((wq, d["L1_xattn_Wq"]), (wk, d["L1_xattn_Wk"]), (wv, d["L1_xattn_Wv"]),
                                 (wo, d["L1_xattn_Wo"]), (bq, d["L1_xattn_bq"].unsqueeze(1)),
                                 (bk, d["L1_xattn_bk"].unsqueeze(1)),
                                 (bv, row_bc(d["L1_xattn_bv"])), (bo, row_bc(d["L1_xattn_bo"]))):
                    sp.dma_start(buf[:], src).then_inc(loaded, 16)
                with sp.Fori(0, TRIPS) as trip:
                    for l in (0, 1):
                        b = sp.snap(trip * 2 + l)
                        src = flat(g.x[:, bass.ds(b, 1), :])
                        csrc = d["ctx_512"][bass.ds(b, 1)].rearrange("b s c -> (b s) c")
                        sp.wait_ge(*vec.at("v", trip, l, ago=1))
                        sp.dma_start(xin[l][:], src).then_inc(x_in[l], 16)
                        sp.wait_ge(*pe_ahead.at("xnT", trip, l, ago=1))
                        sp.dma_start(ctx[l][:], csrc).then_inc(c_in[l], 16)

            @block.gpsimd
            def _(gp):
                for l in (0, 1):
                    gp.memset(vpad[l][:], 0.0).then_inc(zeroed, 1)
                    gp.memset(probT[l][:], 0.0).then_inc(zeroed, 1)
                gp.memset(eps[:], LN_EPS).then_inc(zeroed, 1)
                gp.memset(hmask[:], 1.0).then_inc(zeroed, 1)
                gp.wait_ge(zeroed, NZERO)
                gp.affine_select(out=hmask[:], in_=hmask[:], compare_op=ALU.is_ge, fill=0.0, base=0,
                                 pattern=[[-HD, H]], channel_multiplier=1).then_inc(prep, 1)
                gp.wait_ge(prep, 1)
                gp.affine_select(out=hmask[:], in_=hmask[:], compare_op=ALU.is_ge, fill=0.0, base=HD - 1,
                                 pattern=[[HD, H]], channel_multiplier=-1).then_inc(prep, 1)
                pool.start(gp)
                gp.wait_ge(loaded, NLOAD)
                gp.wait_ge(prep, 2)
                with gp.Fori(0, TRIPS) as trip:
                    for l in (0, 1):
                        gp.wait_ge(x_in[l], trip * 16 + 16)
                        gp.wait_ge(*vec.at("x", trip, l, ago=1))
                        gp.tensor_tensor(xb[l][:], xin[l][:], bo[:], ALU.add).then_inc(*pool.did("xb", l))
                    for l in (0, 1):
                        gp.wait_ge(*act.at("kT", trip, l))
                        gp.tensor_tensor(kblock[l][:, KP:H], kT[l][:].unsqueeze(1).to_broadcast([C, H - KP, S]),
                                         hmask[:, KP:H].unsqueeze(2).to_broadcast([C, H - KP, S]), ALU.mult
                                         ).then_inc(*pool.did("kb", l))

            @block.scalar
            def _(sc):
                sc.preload_act_table_set("natural_log_exp_and_others")
                act.start(sc)
                act_ahead.start(sc)
                sc.wait_ge(zeroed, NZERO)
                sc.wait_ge(loaded, NLOAD)
                sc.activation(bq[:], bq[:], ACT.Copy, scale=SCALE).then_inc(scaled, 1)
                sc.wait_ge(scaled, 1)

                def normalise(trip):
                    for l in (0, 1):
                        sc.wait_ge(*vec_ahead.at("mv", trip, l))
                        rsqrt_of_variance(sc, act_ahead, trip, l, rstd[l], mv[l], eps)

                def turn(trip):
                    for l in (0, 1):
                        sc.wait_ge(*pe_ahead.at("xnT", trip, l))
                        sc.activation(xnT[l][:], ps[l][:, 0, 0:T], ACT.Copy).then_inc(*act_ahead.did("xnT", l))
                        sc.activation(ctxT[l][:], ps[l][0:CD, 0, T:T + S], ACT.Copy).then_inc(*act_ahead.did("cT", l))

                def attend(trip, more):
                    for l in (0, 1):
                        sc.wait_ge(*pe.at("qkv", trip, l))
                        sc.activation(qT[l][:], ps[l][:, 1, 0:T], ACT.Identity, bias=bq[:, 0:1], scale=SCALE
                                      ).then_inc(*act.did("qT", l))
                        sc.activation(kT[l][:], ps[l][:, 1, T:T + S], ACT.Identity, bias=bk[:, 0:1]
                                      ).then_inc(*act.did("kT", l))
                    for l in (0, 1):
                        sc.wait_ge(*vec.at("sub", trip, l))
                        sc.activation(prob[l][:], prob[l][:], ACT.Exp).then_inc(*act.did("exp", l))
                    for l in (0, 1):
                        sc.wait_ge(*pe.at("pT", trip, l))
                        sc.activation(probT[l][0:S, 0:8].rearrange("p h t -> p (h t)"),
                                      ps[l][0:S, 0:2].rearrange("p a t -> p (a t)"), ACT.Copy).then_inc(*act.did("pT", l))
                    if more:
                        normalise(trip + 1)
                    for l in (0, 1):
                        sc.wait_ge(*pe.at("attT", trip, l))
                        sc.activation(attT[l][:], ps[l][:, 1, 0:T], ACT.Copy).then_inc(*act.did("attT", l))
                    if more:
                        turn(trip + 1)

                normalise(0)
                turn(0)
                with sc.Fori(0, TRIPS - 1) as trip:
                    attend(trip, True)
                attend(TRIPS - 1, False)

            @block.tensor
            def _(te):
                pe.start(te)
                pe_ahead.start(te)
                te.wait_ge(zeroed, NZERO)
                te.wait_ge(loaded, NLOAD)

                def turn(trip):
                    for l in (0, 1):
                        te.wait_ge(c_in[l], trip * 16 + 16)
                        te.wait_ge(*vec_ahead.at("xn", trip, l))
                        te.wait_ge(*vec.at("att", trip, l, ago=1))
                        te.transpose(ps[l][:, 0, 0:T], xn[l][:], g.ident[:])
                        te.transpose(ps[l][0:CD, 0, T:T + S], ctx[l][:], g.ident[0:S, 0:S]).then_inc(*pe_ahead.did("xnT", l))

                def attend(trip, more):
                    for l in (0, 1):
                        te.wait_ge(*act_ahead.at("cT", trip, l))
                        te.wait_ge(*vec.at("x", trip, l, ago=1))
                        te.matmul(ps[l][:, 1, 0:T], wq[:], xnT[l][:], start=True, stop=True)
                        te.matmul(ps[l][:, 1, T:T + S], wk[:], ctxT[l][:], start=True, stop=True)
                        te.matmul(ps[l][0:S, 2, 0:C], ctxT[l][:], wv[:], start=True, stop=True
                                  ).then_inc(*pe.did("qkv", l))
                    for l in (0, 1):
                        te.wait_ge(*pool.at("kb", trip, l))
                        te.wait_ge(*vec.at("kb", trip, l))
                        for c in range(4):
                            mm = te.matmul(ps[l][:, c, 0:4 * S], qT[l][:],
                                           kblock[l][:, 4 * c:4 * c + 4].rearrange("p h s -> p (h s)"),
                                           start=True, stop=True)
                        mm.then_inc(*pe.did("s", l))
                    for l in (0, 1):
                        te.wait_ge(*act.at("exp", trip, l))
                        for h in range(H):
                            mm = te.transpose(ps[l][0:S, h // 4, T * (h % 4):T * (h % 4) + T], prob[l][:, h],
                                              g.ident[:])
                        mm.then_inc(*pe.did("pT", l))
                    for l in (0, 1):
                        te.wait_ge(*act.at("pT", trip, l))
                        te.wait_ge(*vec.at("pT", trip, l))
                        for h in range(H):
                            mm = te.matmul(ps[l][:, 0, 0:C], probT[l][:, h], vpad[l][:, h],
                                           start=(h == 0), stop=(h == H - 1))
                        mm.then_inc(*pe.did("pv", l))
                    for l in (0, 1):
                        te.wait_ge(*vec.at("att", trip, l))
                        te.transpose(ps[l][:, 1, 0:T], att[l][:], g.ident[:]).then_inc(*pe.did("attT", l))
                    if more:
                        turn(trip + 1)
                    for l in (0, 1):
                        te.wait_ge(*act.at("attT", trip, l))
                        te.matmul(ps[l][:, 2, 0:C], attT[l][:], wo[:], start=True, stop=True).then_inc(*pe.did("y", l))

                turn(0)
                with te.Fori(0, TRIPS - 1) as trip:
                    attend(trip, True)
                attend(TRIPS - 1, False)

            @block.vector
            def _(v):
                vec.start(v)
                vec_ahead.start(v)
                v.wait_ge(loaded, NLOAD)
                v.wait_ge(zeroed, NZERO)
                v.wait_ge(prep, 2)

                def normalise(trip):
                    for l in (0, 1):
                        v.wait_ge(x_in[l], trip * 16 + 16)
                        v.wait_ge(*vec_ahead.at("xn", trip, l, ago=1))
                        row_statistics(v, vec_ahead, trip, l, stats[l][:], mv[l], rstd[l][:, 1:2], xin[l][:])
                    for l in (0, 1):
                        v.wait_ge(*act_ahead.at("rstd", trip, l))
                        v.tensor_scalar(xn[l][:], xin[l][:], mv[l][:, 0:1], rstd[l][:, 1:2], ALU.subtract, ALU.mult
                                        ).then_inc(*vec_ahead.did("xn", l))

                def attend(trip, more):
                    for l in (0, 1):
                        v.wait_ge(*pool.at("xb", trip, l))
                        v.wait_ge(*pe.at("qkv", trip, l))
                        v.tensor_tensor(diagonal(vpad[l], H, C + HD, HD, rows=S),
                                        ps[l][0:S, 2, 0:C].rearrange("p (h e) -> p h e", e=HD),
                                        bv[0:S].rearrange("p (h e) -> p h e", e=HD), ALU.add).then_inc(*vec.did("v", l))
                    for l in (0, 1):
                        v.wait_ge(*act.at("kT", trip, l))
                        v.tensor_tensor(kblock[l][:, 0:KP], kT[l][:].unsqueeze(1).to_broadcast([C, KP, S]),
                                        hmask[:, 0:KP].unsqueeze(2).to_broadcast([C, KP, S]), ALU.mult
                                        ).then_inc(*vec.did("kb", l))
                    for l in (0, 1):
                        scores = ps[l][:, :, 0:4 * S].rearrange("p a (h s) -> p a h s", s=S)
                        four = lambda ap: ap.rearrange("p (a h) -> p a h", a=4)
                        v.wait_ge(*pe.at("s", trip, l))
                        v.tensor_reduce(four(mx[l][:]), scores, AX, ALU.max).then_inc(*vec.did("mx", l))
                        v.wait_ge(*vec.at("mx", trip, l))
                        v.tensor_tensor(prob[l][:].rearrange("p (a h) s -> p a h s", a=4), scores,
                                        four(mx[l][:]).unsqueeze(3).to_broadcast([T, 4, 4, S]), ALU.subtract
                                        ).then_inc(*vec.did("sub", l))
                    for l in (0, 1):
                        v.wait_ge(*pe.at("pT", trip, l))
                        v.tensor_copy(probT[l][0:S, 8:16].rearrange("p h t -> p (h t)"),
                                      ps[l][0:S, 2:4].rearrange("p a t -> p (a t)")).then_inc(*vec.did("pT", l))
                    for l in (0, 1):
                        v.wait_ge(*act.at("exp", trip, l))
                        v.tensor_reduce(sm[l][:, 0], prob[l][:], AX, ALU.add).then_inc(*vec.did("sum", l))
                        v.wait_ge(*vec.at("sum", trip, l))
                        v.reciprocal(sm[l][:, 1], sm[l][:, 0]).then_inc(*vec.did("rsum", l))
                    if more:
                        normalise(trip + 1)
                    for l in (0, 1):
                        v.wait_ge(*pe.at("pv", trip, l))
                        v.wait_ge(*vec.at("rsum", trip, l))
                        v.tensor_tensor(att[l][:].rearrange("p (h e) -> p h e", e=HD),
                                        ps[l][:, 0, 0:C].rearrange("p (h e) -> p h e", e=HD),
                                        sm[l][:, 1].unsqueeze(2).to_broadcast([T, H, HD]), ALU.mult
                                        ).then_inc(*vec.did("att", l))
                    for l in (0, 1):
                        v.wait_ge(*pe.at("y", trip, l))
                        v.tensor_tensor(flat(g.x[:, bass.ds(trip * 2 + l, 1), :]), xb[l][:], ps[l][:, 2, 0:C], ALU.add
                                        ).then_inc(*vec.did("x", l))

                normalise(0)
                with v.Fori(0, TRIPS - 1) as trip:
                    attend(trip, True)
                attend(TRIPS - 1, False)


def experts(nc, g):
    E, HID, K = 16, 64, 2
    N = E * HID
    CH = N // 128
    TRIPS = g.NB // 2
    LOW, HIGH = -3.0e38, 3.0e38
    d = g.d
    with ExitStack() as stack:
        m = Memory(nc, stack, "mo")
        w1 = m.sb("w1", [C, E, HID])
        w2 = m.sb("w2", [128, CH, C])
        b2 = m.sb("b2", [128, C])
        wr = m.sb("wr", [C, E])
        b1, br = m.sb("b1", [T, N]), m.sb("br", [T, E])
        eps = m.sb("eps", [128, 1])
        xin, xn = (both(m, n, [T, C]) for n in ("xin", "xn"))
        stats, mv, rstd = both(m, "stats", [T, 6]), both(m, "mv", [T, 2]), both(m, "rstd", [T, 2])
        xnT = both(m, "xnT", [C, T])
        hid = both(m, "hid", [T, E, HID])
        logit = both(m, "logit", [T, E + 8])
        left = both(m, "left", [T, E + 8])
        top, chosen = both(m, "top", [T, 8]), both(m, "chosen", [T, 8])
        carrier = both(m, "carrier", [T, 2])
        gate = both(m, "gate", [T, E])
        hidT = both(m, "hidT", [128, CH, T])
        gateT = both(m, "gateT", [128, T])
        ps = [m.ps(f"ps{l}", [128, 4, 512]) for l in (0, 1)]
        xr = both(m, "xr", [T, C])
        loaded, zeroed = m.sem("loaded"), m.sem("zeroed")
        x_in = [m.sem(f"x_in{l}") for l in (0, 1)]
        vec = Steps([m.sem("vec_done")], ["logit top chosen left mask plus gate hb hid", "x"])
        vec_ahead = Steps([m.sem("vec_ahead_done")], ["stats mv", "xn"])
        act = Steps([m.sem("act_done")], ["hT gT"])
        act_ahead = Steps([m.sem("act_ahead_done")], ["lnv rstd", "xnT"])
        pool = Steps([m.sem("pool_done")], ["xr"])
        pe = Steps([m.sem("pe_done")], ["r h", "hT", "y"])
        pe_ahead = Steps([m.sem("pe_ahead_done")], ["xnT"])
        NZERO, NLOAD = 8, 6 * 16

        with nc.Block() as block:
            @block.sync
            def _(sp):
                sp.dma_start(w1[:], d["L1_ffn_W1"].rearrange("e c h -> c e h")).then_inc(loaded, 16)
                sp.dma_start(w2[:], d["L1_ffn_W2"].rearrange("(j e) h n -> (e h) j n", e=2)).then_inc(loaded, 16)
                sp.dma_start(wr[:], d["L1_ffn_Wr"]).then_inc(loaded, 16)
                sp.dma_start(b1[:], row_bc(d["L1_ffn_b1"].rearrange("e h -> (e h)"))).then_inc(loaded, 16)
                sp.dma_start(br[:], row_bc(d["L1_ffn_br"])).then_inc(loaded, 16)
                sp.wait_ge(zeroed, 1)
                sp.dma_start(b2[0:E], d["L1_ffn_b2"]).then_inc(loaded, 16)
                with sp.Fori(0, TRIPS) as trip:
                    for l in (0, 1):
                        src = flat(g.x[:, bass.ds(sp.snap(trip * 2 + l), 1), :])
                        sp.wait_ge(*vec.at("logit", trip, l, ago=1))
                        sp.dma_start(xin[l][:], src).then_inc(x_in[l], 16)

            @block.gpsimd
            def _(gp):
                gp.memset(b2[:], 0.0).then_inc(zeroed, 1)
                gp.memset(eps[:], LN_EPS).then_inc(zeroed, 1)
                for l in (0, 1):
                    gp.memset(gateT[l][:], 0.0).then_inc(zeroed, 1)
                    gp.memset(logit[l][:], LOW).then_inc(zeroed, 1)
                    gp.memset(chosen[l][:], LOW).then_inc(zeroed, 1)
                pool.start(gp)
                with gp.Fori(0, TRIPS) as trip:
                    for l in (0, 1):
                        gp.wait_ge(*vec_ahead.at("xn", trip, l))
                        gp.wait_ge(*vec.at("x", trip, l, ago=1))
                        gp.tensor_tensor(xr[l][:], xin[l][:], xn[l][:], ALU.add).then_inc(*pool.did("xr", l))

            @block.scalar
            def _(sc):
                sc.preload_act_table_set("natural_log_exp_and_others")
                act.start(sc)
                act_ahead.start(sc)
                sc.wait_ge(zeroed, NZERO)

                def normalise(trip):
                    for l in (0, 1):
                        sc.wait_ge(*vec_ahead.at("mv", trip, l))
                        rsqrt_of_variance(sc, act_ahead, trip, l, rstd[l], mv[l], eps)

                def turn(trip):
                    for l in (0, 1):
                        sc.wait_ge(*pe_ahead.at("xnT", trip, l))
                        sc.activation(xnT[l][:], ps[l][:, 0, 0:T], ACT.Copy).then_inc(*act_ahead.did("xnT", l))

                def route(trip, more):
                    for l in (0, 1):
                        sc.wait_ge(*pe.at("hT", trip, l))
                        sc.activation(hidT[l][:].rearrange("p j t -> p (j t)"),
                                      ps[l][:, 0:2].rearrange("p a t -> p (a t)"), ACT.Copy).then_inc(*act.did("hT", l))
                        sc.activation(gateT[l][0:E], ps[l][0:E, 2, 0:T], ACT.Copy).then_inc(*act.did("gT", l))
                    if more:
                        normalise(trip + 1)
                    if more:
                        turn(trip + 1)

                normalise(0)
                turn(0)
                with sc.Fori(0, TRIPS - 1) as trip:
                    route(trip, True)
                route(TRIPS - 1, False)

            @block.tensor
            def _(te):
                pe.start(te)
                pe_ahead.start(te)
                te.wait_ge(zeroed, NZERO)
                te.wait_ge(loaded, NLOAD)

                def turn(trip):
                    for l in (0, 1):
                        te.wait_ge(*vec_ahead.at("xn", trip, l))
                        te.transpose(ps[l][:, 0, 0:T], xn[l][:], g.ident[:]).then_inc(*pe_ahead.did("xnT", l))

                def route(trip, more):
                    for l in (0, 1):
                        te.wait_ge(*act_ahead.at("xnT", trip, l))
                        te.wait_ge(*vec.at("x", trip, l, ago=1))
                        te.matmul(ps[l][:, 1, 0:E], xnT[l][:], wr[:], start=True, stop=True).then_inc(*pe.did("r", l))
                        for a in (0, 1):
                            mm = te.matmul(ps[l][:, 2 + a], xnT[l][:],
                                           w1[:, 8 * a:8 * a + 8].rearrange("p e h -> p (e h)"), start=True, stop=True)
                        mm.then_inc(*pe.did("h", l))
                    for l in (0, 1):
                        te.wait_ge(*vec.at("hid", trip, l))
                        for j in range(CH):
                            te.transpose(ps[l][:, j // 4, T * (j % 4):T * (j % 4) + T],
                                         hid[l][:, 2 * j:2 * j + 2].rearrange("p e h -> p (e h)"), g.ident[:])
                        te.transpose(ps[l][0:E, 2, 0:T], gate[l][:], g.ident[:]).then_inc(*pe.did("hT", l))
                    for l in (0, 1):
                        te.wait_ge(*act.at("gT", trip, l))
                        for j in range(CH):
                            te.matmul(ps[l][:, 3, 0:C], hidT[l][:, j], w2[:, j], start=(j == 0), stop=False)
                        te.matmul(ps[l][:, 3, 0:C], gateT[l][:], b2[:], start=False, stop=True).then_inc(*pe.did("y", l))
                    if more:
                        turn(trip + 1)

                turn(0)
                with te.Fori(0, TRIPS - 1) as trip:
                    route(trip, True)
                route(TRIPS - 1, False)

            @block.vector
            def _(v):
                vec.start(v)
                vec_ahead.start(v)
                v.wait_ge(loaded, NLOAD)
                v.wait_ge(zeroed, NZERO)

                def normalise(trip):
                    for l in (0, 1):
                        v.wait_ge(x_in[l], trip * 16 + 16)
                        v.wait_ge(*vec_ahead.at("xn", trip, l, ago=1))
                        row_statistics(v, vec_ahead, trip, l, stats[l][:], mv[l], rstd[l][:, 1:2], xin[l][:])
                    for l in (0, 1):
                        v.wait_ge(*act_ahead.at("rstd", trip, l))
                        v.tensor_scalar(xn[l][:], xin[l][:], mv[l][:, 0:1], rstd[l][:, 1:2], ALU.subtract, ALU.mult
                                        ).then_inc(*vec_ahead.did("xn", l))

                def route(trip, more):
                    for l in (0, 1):
                        v.wait_ge(*pool.at("xr", trip, l))
                        v.wait_ge(*pe.at("r", trip, l))
                        v.tensor_tensor(logit[l][:, 0:E], ps[l][:, 1, 0:E], br[:], ALU.add).then_inc(*vec.did("logit", l))
                        v.wait_ge(*vec.at("logit", trip, l))
                        v.memset(carrier[l][:, 0:1], 0.0)
                        v.max(top[l][:], logit[l][:, 0:E]).then_inc(*vec.did("top", l))
                        v.wait_ge(*vec.at("top", trip, l))
                        v.tensor_copy(chosen[l][:, 0:K], top[l][:, 0:K]).then_inc(*vec.did("chosen", l))
                        v.wait_ge(*vec.at("chosen", trip, l))
                        v.memset(carrier[l][:, 1:2], 0.0)
                        v.match_replace(left[l][:], chosen[l][:], logit[l][:], HIGH).then_inc(*vec.did("left", l))
                        v.wait_ge(*vec.at("left", trip, l))
                        v.tensor_tensor(gate[l][:], left[l][:, 0:E], logit[l][:, 0:E], ALU.not_equal
                                        ).then_inc(*vec.did("mask", l))
                        v.wait_ge(*vec.at("mask", trip, l))
                        v.tensor_tensor(gate[l][:], gate[l][:], logit[l][:, 0:E], ALU.add).then_inc(*vec.did("plus", l))
                        v.wait_ge(*vec.at("plus", trip, l))
                        v.tensor_tensor(gate[l][:], gate[l][:], logit[l][:, 0:E], ALU.subtract
                                        ).then_inc(*vec.did("gate", l))
                        v.wait_ge(*pe.at("h", trip, l))
                        v.tensor_tensor(hid[l][:].rearrange("p e h -> p (e h)"),
                                        ps[l][:, 2:4].rearrange("p a t -> p (a t)"), b1[:], ALU.add
                                        ).then_inc(*vec.did("hb", l))
                        v.wait_ge(*vec.at("hb", trip, l))
                        v.scalar_tensor_tensor(out=hid[l][:], in0=hid[l][:], scalar=0.0,
                                               in1=gate[l][:].unsqueeze(2).to_broadcast([T, E, HID]),
                                               op0=ALU.max, op1=ALU.mult).then_inc(*vec.did("hid", l))
                    if more:
                        normalise(trip + 1)
                    for l in (0, 1):
                        v.wait_ge(*pe.at("y", trip, l))
                        v.tensor_tensor(flat(g.x[:, bass.ds(trip * 2 + l, 1), :]), xr[l][:], ps[l][:, 3, 0:C], ALU.add
                                        ).then_inc(*vec.did("x", l))

                normalise(0)
                with v.Fori(0, TRIPS - 1) as trip:
                    route(trip, True)
                route(TRIPS - 1, False)


PHASES = [linear_attention, cross_attention, local_transformer, mamba, context_attention, experts]


def store(nc, g):
    with ExitStack() as stack:
        stored = Memory(nc, stack, "st").sem("stored")
        with nc.Block() as block:
            @block.sync
            def _(sp):
                sp.dma_start(g.out.rearrange("b t c -> t b c"), g.x[:]).then_inc(stored, 16)
                sp.wait_ge(stored, 16)


class Globals:
    pass


def decoder(nc, inputs, out):
    g = Globals()
    g.d, g.out, g.NB = inputs, out, inputs["x"].shape[0]
    with ExitStack() as scope:
        constants(nc, g, scope)
        for phase in PHASES:
            phase(nc, g)
        store(nc, g)


def kernel(**inputs):
    import concourse.bacc as bacc
    from concourse.bass_utils import run_bass_kernel_spmd

    nc = bacc.Bacc("TRN2", target_bir_lowering=False, num_devices=1)
    arrays = {name: np.ascontiguousarray(a) for name, a in inputs.items()}
    arrays.update(shape_tables())
    dram = {name: nc.dram_tensor(f"in_{name}", a.shape, mybir.dt.from_np(a.dtype), kind="ExternalInput").ap()
            for name, a in arrays.items()}
    out = nc.dram_tensor("out_x", arrays["x"].shape, F32, kind="ExternalOutput").ap()
    decoder(nc, dram, out)
    r = run_bass_kernel_spmd(nc, [{f"in_{name}": a for name, a in arrays.items()}], core_ids=[0])
    return r.results[0]["out_x"]
```
